# Optimizing a Trainium2 kernel written in Bass

```python
import numpy as np
import jax
import jax.numpy as jnp

def _softmax(x, axis=-1):
    return jax.nn.softmax(x, axis=axis)

def _gelu(x):
    return jax.nn.gelu(x, approximate=True)

def _silu(x):
    return jax.nn.silu(x)

def _sigmoid(x):
    return jax.nn.sigmoid(x)

def _layernorm(x, axis=-1, eps=1e-05):
    m = jnp.mean(x, axis=axis, keepdims=True)
    v = jnp.var(x, axis=axis, keepdims=True)
    return (x - m) / jnp.sqrt(v + eps)

def _scatter_add(tgt, idx, src, axis=0):
    return tgt.at[idx].add(src)

def _segment_sum(src, seg, n):
    return jax.ops.segment_sum(src, seg, n)
kernel_name = 'mk_seq_preln_d2_jaxref_r4_d699dc'

def setup_inputs(seed: int=0):
    np.random.seed(seed)
    _w = jnp.asarray

    def _L0_attn_setup():
        import jax, jax.numpy as jnp
        import numpy as np
        import math

        def _silu(v):
            return v * jax.nn.sigmoid(v)
        key = jax.random.key(seed)
        ks = jax.random.split(key, 8)
        b, l = (4, 512)
        dim, hidden, d_state, dt_rank = (256, 512, 16, 64)
        s = 0.02
        x = jax.random.normal(ks[0], (b, l, dim), dtype=jnp.float32)
        W_in = jax.random.normal(ks[1], (2 * hidden, dim), dtype=jnp.float32) * s
        conv_w = jax.random.normal(ks[2], (hidden, 1, 3), dtype=jnp.float32) * s
        conv_b = jnp.zeros((hidden,), dtype=jnp.float32)
        W_xproj = jax.random.normal(ks[3], (dt_rank + 2 * d_state, hidden), dtype=jnp.float32) * s
        W_dt = jax.random.uniform(ks[4], (hidden, dt_rank), minval=-1.0 / dt_rank, maxval=1.0 / dt_rank, dtype=jnp.float32)
        dt_init = jnp.exp(jax.random.uniform(ks[5], (hidden,), dtype=jnp.float32) * (math.log(0.1) - math.log(0.001)) + math.log(0.001))
        b_dt = -1.0 / dt_init
        A_log = -jnp.arange(1, d_state + 1, dtype=jnp.float32)
        D = jnp.ones((hidden,), dtype=jnp.float32)
        W_out = jax.random.normal(ks[6], (dim, hidden), dtype=jnp.float32) * s
        return {'x': x, 'W_in': W_in, 'conv_w': conv_w, 'conv_b': conv_b, 'W_xproj': W_xproj, 'W_dt': W_dt, 'b_dt': b_dt, 'A_log': A_log, 'D': D, 'W_out': W_out}
    _L0_attn_in = _L0_attn_setup()

    def _L0_ffn_setup():
        import jax, jax.numpy as jnp
        import numpy as np
        B, S, D, E = (2, 512, 256, 8)
        key = jax.random.key(seed)
        ks = jax.random.split(key, 5)
        x = jax.random.normal(ks[0], (B, S, D), dtype=jnp.float32)
        router_w = jax.random.normal(ks[1], (E, D), dtype=jnp.float32) * 0.02
        router_b = jnp.zeros((E,), dtype=jnp.float32)
        expert_w = jax.random.normal(ks[2], (E, D, D), dtype=jnp.float32) * 0.02
        expert_b = jnp.zeros((E, D), dtype=jnp.float32)
        return {'x': x, 'router_w': router_w, 'router_b': router_b, 'expert_w': expert_w, 'expert_b': expert_b}
    _L0_ffn_in = _L0_ffn_setup()

    def _L1_attn_setup():
        import jax, jax.numpy as jnp
        import numpy as np
        B, S, D, H, DH, FF = (2, 1024, 256, 16, 64, 1024)

        def _ln(x, g, b):
            m = x.mean(-1, keepdims=True)
            v = ((x - m) ** 2).mean(-1, keepdims=True)
            return (x - m) * jax.lax.rsqrt(v + 1e-05) * g + b

        def _phi(x, proj):
            return jax.nn.elu(x @ proj) + 1.0
        key = jax.random.key(seed)
        ks = jax.random.split(key, 10)
        s = 0.02
        return {'x': jax.random.normal(ks[0], (B, S, D), jnp.float32), 'wq': jax.random.normal(ks[1], (D, H * DH), jnp.float32) * s, 'wk': jax.random.normal(ks[2], (D, H * DH), jnp.float32) * s, 'wv': jax.random.normal(ks[3], (D, H * DH), jnp.float32) * s, 'wo': jax.random.normal(ks[4], (H * DH, D), jnp.float32) * s, 'proj': jax.random.normal(ks[5], (DH, DH), jnp.float32) / np.sqrt(DH).astype(np.float32), 'w1': jax.random.normal(ks[6], (D, FF), jnp.float32) * s, 'b1': jnp.zeros((FF,), jnp.float32), 'w2': jax.random.normal(ks[7], (FF, D), jnp.float32) * s, 'b2': jnp.zeros((D,), jnp.float32), 'g1': jnp.ones((D,), jnp.float32), 'beta1': jnp.zeros((D,), jnp.float32), 'g2': jnp.ones((D,), jnp.float32), 'beta2': jnp.zeros((D,), jnp.float32)}
    _L1_attn_in = _L1_attn_setup()

    def _L1_ffn_setup():
        import jax, jax.numpy as jnp
        import numpy as np
        DIM = 256
        DEPTH = 2
        HEADS = 8
        DIM_HEAD = 64
        WINDOW = 128
        INNER = HEADS * DIM_HEAD
        HID = int(DIM * 4 * 2 / 3)
        B, N = (2, 2048)
        QK_SCALE = 8.0

        def shift_token(t):
            t1, t2 = jnp.split(t, 2, axis=-1)
            t2 = jnp.pad(t2, ((0, 0), (1, 0), (0, 0)))[:, :-1]
            return jnp.concatenate([t1, t2], axis=-1)

        def l2norm(t):
            return t / jnp.clip(jnp.linalg.norm(t, axis=-1, keepdims=True), 1e-12)

        def rotate_half(x):
            x1, x2 = jnp.split(x, 2, axis=-1)
            return jnp.concatenate([-x2, x1], axis=-1)

        def rotary_xpos(q, k):
            n = q.shape[-2]
            half_idx = jnp.arange(0, DIM_HEAD, 2, dtype=jnp.float32)
            inv_freq = 1.0 / 10000.0 ** (half_idx / DIM_HEAD)
            t = jnp.arange(n, dtype=jnp.float32)
            freqs = t[:, None] * inv_freq[None, :]
            freqs = jnp.concatenate([freqs, freqs], axis=-1)
            base = (half_idx + 0.4 * DIM_HEAD) / (1.4 * DIM_HEAD)
            power = (t - n // 2) / float(WINDOW // 2)
            scale = base[None, :] ** power[:, None]
            scale = jnp.concatenate([scale, scale], axis=-1)
            cos, sin = (jnp.cos(freqs), jnp.sin(freqs))
            q = q * cos * scale + rotate_half(q) * sin * scale
            k = k * cos / scale + rotate_half(k) * sin / scale
            return (q, k)

        def local_attention(q, k, v):
            b, h, n, d = q.shape
            w = n // WINDOW
            bq = q.reshape(b, h, w, WINDOW, d) * QK_SCALE
            bk = k.reshape(b, h, w, WINDOW, d)
            bv = v.reshape(b, h, w, WINDOW, d)

            def look_around(t):
                p = jnp.pad(t, ((0, 0), (0, 0), (1, 0), (0, 0), (0, 0)))
                return jnp.concatenate([p[:, :, :w], p[:, :, 1:]], axis=3)
            bk, bv = (look_around(bk), look_around(bv))
            bt = jnp.arange(n).reshape(w, WINDOW)
            btp = jnp.pad(bt, ((1, 0), (0, 0)), constant_values=-1)
            btk = jnp.concatenate([btp[:w], btp[1:]], axis=1)
            sim = jnp.einsum('bhwid,bhwjd->bhwij', bq, bk)
            i = bt[:, :, None]
            j = btk[:, None, :]
            mask = (i < j) | (i > j + WINDOW) | (j == -1)
            sim = jnp.where(mask, -jnp.finfo(sim.dtype).max, sim)
            attn = jax.nn.softmax(sim, axis=-1)
            out = jnp.einsum('bhwij,bhwjd->bhwid', attn, bv)
            return out.reshape(b, h, n, d)

        def _layer(x, wqkv, qs, ksc, wo, lg, lb, w1, b1, w2, b2):
            b, n, _ = x.shape
            h = shift_token(x)
            qkv = h @ wqkv
            q, k, v = jnp.split(qkv, 3, axis=-1)
            to_heads = lambda t: t.reshape(b, n, HEADS, DIM_HEAD).transpose(0, 2, 1, 3)
            q, k, v = (to_heads(q), to_heads(k), to_heads(v))
            q = l2norm(q) * qs
            k = l2norm(k) * ksc
            q, k = rotary_xpos(q, k)
            o = local_attention(q, k, v)
            o = o.transpose(0, 2, 1, 3).reshape(b, n, INNER)
            x = x + o @ wo
            h = shift_token(x)
            mu = h.mean(-1, keepdims=True)
            var = h.var(-1, keepdims=True)
            h = (h - mu) / jnp.sqrt(var + 1e-05) * lg + lb
            h = h @ w1 + b1
            a, g = jnp.split(h, 2, axis=-1)
            h = a * jax.nn.gelu(g, approximate=False)
            x = x + h @ w2 + b2
            return x
        key = jax.random.key(seed)
        ks = jax.random.split(key, 6)
        return {'x': jax.random.normal(ks[0], (B, N, DIM), jnp.float32), 'wqkv': jax.random.normal(ks[1], (DEPTH, DIM, 3 * INNER), jnp.float32) * 0.02, 'q_scale': jnp.ones((DEPTH, DIM_HEAD), jnp.float32), 'k_scale': jnp.ones((DEPTH, DIM_HEAD), jnp.float32), 'wo': jax.random.normal(ks[2], (DEPTH, INNER, DIM), jnp.float32) * 0.02, 'ln_g': jnp.ones((DEPTH, DIM), jnp.float32), 'ln_b': jnp.zeros((DEPTH, DIM), jnp.float32), 'w1': jax.random.normal(ks[3], (DEPTH, DIM, 2 * HID), jnp.float32) * 0.02, 'b1': jnp.zeros((DEPTH, 2 * HID), jnp.float32), 'w2': jax.random.normal(ks[4], (DEPTH, HID, DIM), jnp.float32) * 0.02, 'b2': jnp.zeros((DEPTH, DIM), jnp.float32)}
    _L1_ffn_in = _L1_ffn_setup()
    _d = {'L0_attn_x': _L0_attn_in['x'], 'L0_attn_W_in': _L0_attn_in['W_in'], 'L0_attn_conv_w': _L0_attn_in['conv_w'], 'L0_attn_conv_b': _L0_attn_in['conv_b'], 'L0_attn_W_xproj': _L0_attn_in['W_xproj'], 'L0_attn_W_dt': _L0_attn_in['W_dt'], 'L0_attn_b_dt': _L0_attn_in['b_dt'], 'L0_attn_A_log': _L0_attn_in['A_log'], 'L0_attn_D': _L0_attn_in['D'], 'L0_attn_W_out': _L0_attn_in['W_out'], 'L0_ffn_router_w': _L0_ffn_in['router_w'], 'L0_ffn_router_b': _L0_ffn_in['router_b'], 'L0_ffn_expert_w': _L0_ffn_in['expert_w'], 'L0_ffn_expert_b': _L0_ffn_in['expert_b'], 'L1_attn_wq': _L1_attn_in['wq'], 'L1_attn_wk': _L1_attn_in['wk'], 'L1_attn_wv': _L1_attn_in['wv'], 'L1_attn_wo': _L1_attn_in['wo'], 'L1_attn_proj': _L1_attn_in['proj'], 'L1_attn_w1': _L1_attn_in['w1'], 'L1_attn_b1': _L1_attn_in['b1'], 'L1_attn_w2': _L1_attn_in['w2'], 'L1_attn_b2': _L1_attn_in['b2'], 'L1_attn_g1': _L1_attn_in['g1'], 'L1_attn_beta1': _L1_attn_in['beta1'], 'L1_attn_g2': _L1_attn_in['g2'], 'L1_attn_beta2': _L1_attn_in['beta2'], 'L1_ffn_wqkv': _L1_ffn_in['wqkv'], 'L1_ffn_q_scale': _L1_ffn_in['q_scale'], 'L1_ffn_k_scale': _L1_ffn_in['k_scale'], 'L1_ffn_wo': _L1_ffn_in['wo'], 'L1_ffn_ln_g': _L1_ffn_in['ln_g'], 'L1_ffn_ln_b': _L1_ffn_in['ln_b'], 'L1_ffn_w1': _L1_ffn_in['w1'], 'L1_ffn_b1': _L1_ffn_in['b1'], 'L1_ffn_w2': _L1_ffn_in['w2'], 'L1_ffn_b2': _L1_ffn_in['b2']}
    _x0 = _d['L0_attn_x']
    _d['L0_attn_x'] = jax.random.normal(jax.random.fold_in(jax.random.key(seed), 1), (4, 1024, 256), dtype=_x0.dtype)
    del _x0
    return _d

def reference(L0_attn_x, L0_attn_W_in, L0_attn_conv_w, L0_attn_conv_b, L0_attn_W_xproj, L0_attn_W_dt, L0_attn_b_dt, L0_attn_A_log, L0_attn_D, L0_attn_W_out, L0_ffn_router_w, L0_ffn_router_b, L0_ffn_expert_w, L0_ffn_expert_b, L1_attn_wq, L1_attn_wk, L1_attn_wv, L1_attn_wo, L1_attn_proj, L1_attn_w1, L1_attn_b1, L1_attn_w2, L1_attn_b2, L1_attn_g1, L1_attn_beta1, L1_attn_g2, L1_attn_beta2, L1_ffn_wqkv, L1_ffn_q_scale, L1_ffn_k_scale, L1_ffn_wo, L1_ffn_ln_g, L1_ffn_ln_b, L1_ffn_w1, L1_ffn_b1, L1_ffn_w2, L1_ffn_b2):

    def _L0_attn_ref(x, W_in, conv_w, conv_b, W_xproj, W_dt, b_dt, A_log, D, W_out):
        import jax, jax.numpy as jnp
        import numpy as np
        import math

        def _silu(v):
            return v * jax.nn.sigmoid(v)
        b, l, dim = x.shape
        hidden = W_dt.shape[0]
        dt_rank = W_dt.shape[1]
        d_state = A_log.shape[0]
        xz = jnp.einsum('bld,ed->ble', x, W_in)
        u, z = jnp.split(xz, 2, axis=-1)
        uc = jax.lax.conv_general_dilated(jnp.moveaxis(u, 1, 2), conv_w, window_strides=(1,), padding=[(1, 1)], dimension_numbers=('NCH', 'OIH', 'NCH'), feature_group_count=hidden)
        uc = jnp.moveaxis(uc + conv_b[None, :, None], 1, 2)
        uc = _silu(uc)
        x_dbl = jnp.einsum('blh,eh->ble', uc, W_xproj)
        dtp = x_dbl[..., :dt_rank]
        Bm = x_dbl[..., dt_rank:dt_rank + d_state]
        Cm = x_dbl[..., dt_rank + d_state:]
        dt = jax.nn.softplus(jnp.einsum('blr,hr->blh', dtp, W_dt) + b_dt)
        A = -jnp.exp(A_log)

        def step(h, inp):
            u_t, dt_t, B_t, C_t = inp
            dA = jnp.exp(dt_t[:, None, :] * A[None, :, None])
            h = dA * h + B_t[:, :, None] * u_t[:, None, :]
            y_t = jnp.einsum('bn,bnh->bh', C_t, h)
            return (h, y_t)
        xs = (jnp.moveaxis(uc, 0, 1), jnp.moveaxis(dt, 0, 1), jnp.moveaxis(Bm, 0, 1), jnp.moveaxis(Cm, 0, 1))
        h0 = jnp.zeros((b, d_state, hidden), dtype=uc.dtype)
        _, ys = jax.lax.scan(step, h0, xs)
        y = jnp.moveaxis(ys, 0, 1) + D * uc
        y = y * _silu(z)
        out = jnp.einsum('blh,dh->bld', y, W_out)
        return x + out

    def _L0_ffn_ref(x, router_w, router_b, expert_w, expert_b):
        import jax, jax.numpy as jnp
        import numpy as np
        B, S, D, E = (2, 512, 256, 8)
        logits = jnp.einsum('bsd,ed->bse', x, router_w) + router_b
        probs = jax.nn.softmax(logits, axis=-1)
        weights = jnp.max(probs, axis=-1)
        top1 = jnp.argmax(probs, axis=-1)
        y_all = jnp.einsum('bsd,eod->bseo', x, expert_w) + expert_b
        y = jnp.take_along_axis(y_all, top1[:, :, None, None], axis=2)[:, :, 0, :]
        out = y * weights[:, :, None]
        return out

    def _L1_attn_ref(x, wq, wk, wv, wo, proj, w1, b1, w2, b2, g1, beta1, g2, beta2):
        import jax, jax.numpy as jnp
        import numpy as np
        B, S, D, H, DH, FF = (2, 1024, 256, 16, 64, 1024)

        def _ln(x, g, b):
            m = x.mean(-1, keepdims=True)
            v = ((x - m) ** 2).mean(-1, keepdims=True)
            return (x - m) * jax.lax.rsqrt(v + 1e-05) * g + b

        def _phi(x, proj):
            return jax.nn.elu(x @ proj) + 1.0
        b, s, d = x.shape
        h = _ln(x, g1, beta1)
        q = _phi((h @ wq).reshape(b, s, H, DH), proj)
        k = _phi((h @ wk).reshape(b, s, H, DH), proj)
        v = (h @ wv).reshape(b, s, H, DH)
        qs = jnp.moveaxis(q, 1, 0)
        ks_ = jnp.moveaxis(k, 1, 0)
        vs = jnp.moveaxis(v, 1, 0)

        def step(carry, qkv_t):
            kv, ksum = carry
            q_t, k_t, v_t = qkv_t
            kv = kv + k_t[..., :, None] * v_t[..., None, :]
            ksum = ksum + k_t
            num = jnp.einsum('bhd,bhde->bhe', q_t, kv)
            den = jnp.einsum('bhd,bhd->bh', q_t, ksum) + 1e-06
            return ((kv, ksum), num / den[..., None])
        kv0 = jnp.zeros((b, H, DH, DH), x.dtype)
        ks0 = jnp.zeros((b, H, DH), x.dtype)
        _, outs = jax.lax.scan(step, (kv0, ks0), (qs, ks_, vs))
        attn = jnp.moveaxis(outs, 0, 1).reshape(b, s, H * DH) @ wo
        x = x + attn
        h2 = _ln(x, g2, beta2)
        x = x + (jax.nn.gelu(h2 @ w1 + b1, approximate=False) @ w2 + b2)
        return x

    def _L1_ffn_ref(x, wqkv, q_scale, k_scale, wo, ln_g, ln_b, w1, b1, w2, b2):
        import jax, jax.numpy as jnp
        import numpy as np
        DIM = 256
        DEPTH = 2
        HEADS = 8
        DIM_HEAD = 64
        WINDOW = 128
        INNER = HEADS * DIM_HEAD
        HID = int(DIM * 4 * 2 / 3)
        B, N = (2, 2048)
        QK_SCALE = 8.0

        def shift_token(t):
            t1, t2 = jnp.split(t, 2, axis=-1)
            t2 = jnp.pad(t2, ((0, 0), (1, 0), (0, 0)))[:, :-1]
            return jnp.concatenate([t1, t2], axis=-1)

        def l2norm(t):
            return t / jnp.clip(jnp.linalg.norm(t, axis=-1, keepdims=True), 1e-12)

        def rotate_half(x):
            x1, x2 = jnp.split(x, 2, axis=-1)
            return jnp.concatenate([-x2, x1], axis=-1)

        def rotary_xpos(q, k):
            n = q.shape[-2]
            half_idx = jnp.arange(0, DIM_HEAD, 2, dtype=jnp.float32)
            inv_freq = 1.0 / 10000.0 ** (half_idx / DIM_HEAD)
            t = jnp.arange(n, dtype=jnp.float32)
            freqs = t[:, None] * inv_freq[None, :]
            freqs = jnp.concatenate([freqs, freqs], axis=-1)
            base = (half_idx + 0.4 * DIM_HEAD) / (1.4 * DIM_HEAD)
            power = (t - n // 2) / float(WINDOW // 2)
            scale = base[None, :] ** power[:, None]
            scale = jnp.concatenate([scale, scale], axis=-1)
            cos, sin = (jnp.cos(freqs), jnp.sin(freqs))
            q = q * cos * scale + rotate_half(q) * sin * scale
            k = k * cos / scale + rotate_half(k) * sin / scale
            return (q, k)

        def local_attention(q, k, v):
            b, h, n, d = q.shape
            w = n // WINDOW
            bq = q.reshape(b, h, w, WINDOW, d) * QK_SCALE
            bk = k.reshape(b, h, w, WINDOW, d)
            bv = v.reshape(b, h, w, WINDOW, d)

            def look_around(t):
                p = jnp.pad(t, ((0, 0), (0, 0), (1, 0), (0, 0), (0, 0)))
                return jnp.concatenate([p[:, :, :w], p[:, :, 1:]], axis=3)
            bk, bv = (look_around(bk), look_around(bv))
            bt = jnp.arange(n).reshape(w, WINDOW)
            btp = jnp.pad(bt, ((1, 0), (0, 0)), constant_values=-1)
            btk = jnp.concatenate([btp[:w], btp[1:]], axis=1)
            sim = jnp.einsum('bhwid,bhwjd->bhwij', bq, bk)
            i = bt[:, :, None]
            j = btk[:, None, :]
            mask = (i < j) | (i > j + WINDOW) | (j == -1)
            sim = jnp.where(mask, -jnp.finfo(sim.dtype).max, sim)
            attn = jax.nn.softmax(sim, axis=-1)
            out = jnp.einsum('bhwij,bhwjd->bhwid', attn, bv)
            return out.reshape(b, h, n, d)

        def _layer(x, wqkv, qs, ksc, wo, lg, lb, w1, b1, w2, b2):
            b, n, _ = x.shape
            h = shift_token(x)
            qkv = h @ wqkv
            q, k, v = jnp.split(qkv, 3, axis=-1)
            to_heads = lambda t: t.reshape(b, n, HEADS, DIM_HEAD).transpose(0, 2, 1, 3)
            q, k, v = (to_heads(q), to_heads(k), to_heads(v))
            q = l2norm(q) * qs
            k = l2norm(k) * ksc
            q, k = rotary_xpos(q, k)
            o = local_attention(q, k, v)
            o = o.transpose(0, 2, 1, 3).reshape(b, n, INNER)
            x = x + o @ wo
            h = shift_token(x)
            mu = h.mean(-1, keepdims=True)
            var = h.var(-1, keepdims=True)
            h = (h - mu) / jnp.sqrt(var + 1e-05) * lg + lb
            h = h @ w1 + b1
            a, g = jnp.split(h, 2, axis=-1)
            h = a * jax.nn.gelu(g, approximate=False)
            x = x + h @ w2 + b2
            return x
        for l in range(DEPTH):
            x = _layer(x, wqkv[l], q_scale[l], k_scale[l], wo[l], ln_g[l], ln_b[l], w1[l], b1[l], w2[l], b2[l])
        return x
    x = L0_attn_x
    x = x + _L0_attn_ref(_layernorm(x, axis=-1), L0_attn_W_in, L0_attn_conv_w, L0_attn_conv_b, L0_attn_W_xproj, L0_attn_W_dt, L0_attn_b_dt, L0_attn_A_log, L0_attn_D, L0_attn_W_out)
    x = x + _L0_ffn_ref(_layernorm(x, axis=-1), L0_ffn_router_w, L0_ffn_router_b, L0_ffn_expert_w, L0_ffn_expert_b)
    x = x + _L1_attn_ref(_layernorm(x, axis=-1), L1_attn_wq, L1_attn_wk, L1_attn_wv, L1_attn_wo, L1_attn_proj, L1_attn_w1, L1_attn_b1, L1_attn_w2, L1_attn_b2, L1_attn_g1, L1_attn_beta1, L1_attn_g2, L1_attn_beta2)
    x = x + _L1_ffn_ref(_layernorm(x, axis=-1), L1_ffn_wqkv, L1_ffn_q_scale, L1_ffn_k_scale, L1_ffn_wo, L1_ffn_ln_g, L1_ffn_ln_b, L1_ffn_w1, L1_ffn_b1, L1_ffn_w2, L1_ffn_b2)
    return x

_drawn_inputs = setup_inputs


def setup_inputs(seed=0):
    import zlib

    import numpy as np

    out = dict(_drawn_inputs(seed))
    spreads = {'L0_attn_conv_b': (0.0, 0.1),
     'L0_attn_D': (1.0, 0.2),
     'L0_ffn_router_b': (0.0, 0.1),
     'L0_ffn_expert_b': (0.0, 0.1),
     'L1_attn_b1': (0.0, 0.1),
     'L1_attn_b2': (0.0, 0.1),
     'L1_attn_g1': (1.0, 0.2),
     'L1_attn_beta1': (0.0, 0.1),
     'L1_attn_g2': (1.0, 0.2),
     'L1_attn_beta2': (0.0, 0.1),
     'L1_ffn_q_scale': (1.0, 0.2),
     'L1_ffn_k_scale': (1.0, 0.2),
     'L1_ffn_ln_g': (1.0, 0.2),
     'L1_ffn_ln_b': (0.0, 0.1),
     'L1_ffn_b1': (0.0, 0.1),
     'L1_ffn_b2': (0.0, 0.1)}
    factors = {}
    for name, (base, spread) in spreads.items():
        noise = np.random.default_rng([zlib.crc32(name.encode()), seed]).standard_normal(out[name].shape)
        drawn = base * np.exp(spread * noise) if base else spread * noise
        out[name] = jnp.asarray(drawn.astype(out[name].dtype))
    for name, factor in factors.items():
        out[name] = (out[name] * factor).astype(out[name].dtype)
    return out
```

```python
import concourse.bass as bass
from concourse import mybir
from contextlib import ExitStack
import numpy as np

FP32 = mybir.dt.float32
BF16 = mybir.dt.bfloat16
ALU = mybir.AluOpType
ACT = mybir.ActivationFunctionType
AX = mybir.AxisListType

P = 128
B, L, D = 4, 1024, 256
T = B * L
KD = D // P
BLK = 512
TB = BLK // P
NBLK = T // BLK
NT = T // P
LP = L + 1
EPS = 1e-5

HID, NS, RANK = 512, 16, 64
CT = HID // P
E = 8
H1, DH = 16, 64
FF1 = 1024
H2 = 8
INNER = H2 * DH
HID2 = int(D * 4 * 2 / 3)
MASKED = -1e30

class Turn:

    def __init__(self, pair, side):
        self.pair, self.side = pair, side
        self.i = pair * 2 + side

    def next(self):
        return Turn(self.pair, 1) if self.side == 0 else Turn(self.pair + 1, 0)

    def before(self):
        return Turn(self.pair, 0) if self.side else Turn(self.pair - 1, 1)

def turns(eng, n, body):
    with eng.Fori(0, n // 2 - 1) as pair:
        body(Turn(pair, 0), True)
        body(Turn(pair, 1), True)
    body(Turn(n // 2 - 1, 0), True)
    body(Turn(n // 2 - 1, 1), False)

class Counter:

    def __init__(self, sem, per=1, credit=0):
        self.sem, self.per, self.credit = sem, per, credit * per

    def at(self, i, k=None):
        return i * self.per + (self.credit + (self.per if k is None else k))

class Transfers:

    def __init__(self, sems, per=1, credit=0):
        self.sems, self.per, self.credit = sems, 16 * per, 16 * per * credit

    def at(self, turn, back=0):
        return turn.pair * self.per + (self.credit + self.per * (1 - back))

    def total(self, pairs):
        return self.credit + self.per * pairs

def give_credit(eng, *counts):
    for c in counts:
        for sem in (c.sems if isinstance(c, Transfers) else [c.sem]):
            eng.sem_inc(sem, c.credit)

class Scope:

    def __init__(self, nc, ctx, tag):
        self.nc, self.ctx, self.tag, self.sems = nc, ctx, tag, []
        ctx.callback(self.end)

    def end(self):
        self.nc.clear_and_free_semaphores(self.sems)
        self.nc.all_engine_barrier()

    def sb(self, name, shape, dt=FP32):
        return self.ctx.enter_context(self.nc.sbuf_tensor(f"{self.tag}_{name}", shape, dt))

    def ps(self, name, shape, dt=FP32):
        return self.ctx.enter_context(self.nc.psum_tensor(f"{self.tag}_{name}", shape, dt))

    def sem(self, name):
        self.sems.append(self.nc.alloc_semaphore(f"{self.tag}_{name}"))
        return self.sems[-1]

    def counter(self, name, per=1, credit=0):
        return Counter(self.sem(name), per, credit)

    def transfer(self, name, per=1, credit=0):
        return Transfers([self.sem(f"{name}{s}") for s in range(2)], per, credit)

def tiles_of(rows):
    return rows.rearrange("(t p) d -> p t d", p=P)

def block_rows(stream, turn, shift=0):
    return tiles_of(stream[bass.ds(turn.pair * LP + (1 - shift + turn.side * BLK), BLK), :])

def flat_rows(stream, turn):
    return tiles_of(stream[bass.ds(turn.pair * (2 * BLK) + turn.side * BLK, BLK), :])

def stats_of(nc, dve, x, n, sums, mv, sums_ready, mv_ready, i):
    for t in range(n):
        last = nc.vector.bn_stats(sums[:, t, :], x[:, t, :])
    last.then_inc(sums_ready.sem, 1)
    dve.wait_ge(sums_ready.sem, sums_ready.at(i, 1))
    dve.sem_inc(sums_ready.sem, 1)
    for t in range(n):
        last = nc.vector.bn_aggr(mv[:, t, :], sums[:, t, :])
    last.then_inc(mv_ready.sem, 1)

def rstd_of(nc, pool, mv, rstd, eps, minus_half, n, mv_ready, eps_added, rstd_ready, i):
    pool.wait_ge(mv_ready.sem, mv_ready.at(i))
    nc.gpsimd.tensor_tensor(rstd[:, 0:n], mv[:, 0:n, 1], eps[:, 0:n], ALU.add).then_inc(eps_added.sem, 1)
    pool.wait_ge(eps_added.sem, eps_added.at(i))
    nc.gpsimd.tensor_tensor(rstd[:, 0:n], rstd[:, 0:n], minus_half[:, 0:n], ALU.pow).then_inc(rstd_ready.sem, 1)

def normalise(nc, out, x, mv, rstd, n):
    for t in range(n):
        last = nc.vector.tensor_scalar(out[:, t, :], x[:, t, :], mv[:, t, 0:1], rstd[:, t:t + 1],
                                       ALU.subtract, ALU.mult)
    return last

def ahead(eng, body, n=NT):
    with eng.Fori(0, n // 2 - 1) as pair:
        body(Turn(pair, 0), True, True)
        body(Turn(pair, 1), True, True)
    body(Turn(n // 2 - 1, 0), True, False)
    body(Turn(n // 2 - 1, 1), False, False)

def trailing(eng, body):
    body(Turn(0, 0), False, True, True)
    with eng.Fori(0, NT // 2 - 2) as pair:
        body(Turn(pair, 1), True, True, True)
        body(Turn(pair + 1, 0), True, True, True)
    body(Turn(NT // 2 - 2, 1), True, True, True)
    body(Turn(NT // 2 - 1, 0), True, True, False)
    body(Turn(NT // 2 - 1, 1), True, False, False)

def state_space_stage(nc, tag, w, src, dst, ident):
    TS = L // P
    HALVES = L // BLK
    with ExitStack() as ctx:
        s = Scope(nc, ctx, tag)
        w_in = s.sb("w_in", [P, KD, 2 * HID])
        w_x = s.sb("w_x", [P, CT, RANK + 2 * NS])
        w_dt = s.sb("w_dt", [RANK, HID])
        w_out = s.sb("w_out", [P, CT, D])
        conv_w, conv_b = s.sb("conv_w", [P, CT, 3]), s.sb("conv_b", [P, CT])
        b_dt, skip = s.sb("b_dt", [P, CT]), s.sb("skip", [P, CT])
        skip_diag = s.sb("skip_diag", [P, CT, P])
        a_log, decay = s.sb("a_log", [P, NS]), s.sb("decay", [P, NS])
        pick = s.sb("pick", [3 * 2 * NS, 2 * NS, P], BF16)
        minus_half, eps = s.sb("minus_half", [P, TS]), s.sb("eps", [P, TS])
        x, h0, res = s.sb("x", [P, TS, D]), s.sb("h0", [P, TS, D]), s.sb("res", [P, TS, D])
        sums, mv, rstd = s.sb("sums", [P, TS, 6]), s.sb("mv", [P, TS, 2]), s.sb("rstd", [P, TS])
        hT = s.sb("hT", [P, KD, L])
        u = s.sb("u", [P, CT, L + 2])
        uc, z, dt = s.sb("uc", [P, CT, L]), s.sb("z", [P, CT, L]), s.sb("dt", [P, CT, L])
        work = s.sb("work", [P, CT, L])
        middle = s.sb("middle", [2 * NS, L], BF16)
        parts = s.sb("parts", [3 * 2 * NS, L], BF16)
        da, bu = s.sb("da", [P, 2, 2, L]), s.sb("bu", [P, 2, 2, L])
        b_rows = s.sb("b_rows", [P, 2, L])
        state, seen = s.sb("state", [P, 2, L]), s.sb("seen", [P, 2, L])
        rest, dtp = seen[0:2 * NS, 0, :], seen[0:RANK, 1, :]
        out = s.sb("out", [P, 2, D])
        py = [s.ps(f"py{k}", [P, L]) for k in range(2)]
        pb, pc = s.ps("pb", [P, L]), s.ps("pc", [P, L])

        def half(a, j):
            return a[:, j * BLK:(j + 1) * BLK]

        weights = s.sem("weights")
        consts = s.counter("consts")
        x_in, out_sent = s.sem("x_in"), s.transfer("out_sent", credit=1)
        decay_ready, skip_ready = s.counter("decay_ready"), s.counter("skip_ready")
        decay_part = s.counter("decay_part")
        sums_ready, mv_ready = s.counter("sums_ready", per=2), s.counter("mv_ready")
        eps_added, rstd_ready, h0_ready = s.counter("eps_added"), s.counter("rstd_ready"), s.counter("h0_ready")
        res_ready = s.counter("res_ready")
        tp_ready, hT_ready = s.counter("tp_ready", per=2), s.counter("hT_ready", per=2)
        u_made, z_made = s.counter("u_made", per=2 * CT), s.counter("z_made", per=2 * CT)
        u_copied, z_ready = s.counter("u_copied", per=2 * CT), s.counter("z_ready", per=2 * CT)
        conv_steps, uc_ready = s.counter("conv_steps", per=3 * CT), s.counter("uc_ready", per=CT)
        xd_made, dtp_ready = s.counter("xd_made"), s.counter("dtp_ready")
        part_steps = s.counter("part_steps", per=4)
        dt_made, dt_biased = s.counter("dt_made", per=CT), s.counter("dt_biased", per=CT)
        soft_steps, soft_ready = s.counter("soft_steps", per=2 * CT), s.counter("soft_ready", per=CT)
        dt_ready = s.counter("dt_ready", per=CT)
        y_ready = s.counter("y_ready", per=CT, credit=1)
        out_made, out_ready = s.counter("out_made", per=TS), s.counter("out_ready", per=TS, credit=1)
        b_made, b_copied = s.counter("b_made"), s.counter("b_copied", credit=1)
        c_made = s.counter("c_made")
        da_ready, bu_ready = s.counter("da_ready", per=2), s.counter("bu_ready", per=2, credit=2)
        state_ready, seen_ready = s.counter("state_ready", per=2, credit=2), s.counter("seen_ready", per=2, credit=1)
        added = s.counter("added", per=2, credit=1)
        stand = {e: s.sem(f"stand_{e}") for e in ("pool", "pe")}
        block = ctx.enter_context(nc.Block())

        def each_sequence(eng, body):
            with eng.Fori(0, B) as b:
                body(b)

        def each_state(eng, b, cp, body):
            def one(turn, more, more2):
                body(turn.side, turn.i, (b * (CT // 2) + cp) * NS + turn.i, more, more2)
            ahead(eng, one, NS)

        @block.sync
        def _(sp):
            n = [0]

            def put(to, frm, **how):
                sp.dma_start(to, frm, **how).then_inc(weights, 16)
                n[0] += 1

            sp.dma_start(x[:, :, :], tiles_of(src[0:L, :])).then_inc(x_in, 16)
            put(w_in[:, :, :], w["w_in"].rearrange("(k p) n -> p k n", p=P))
            put(w_x[:, :, :], w["w_x"].rearrange("(c p) n -> p c n", p=P))
            put(w_dt[:, :], w["w_dt"])
            put(w_out[:, :, :], w["w_out"].rearrange("(c p) n -> p c n", p=P))
            put(conv_w[:, :, :], w["conv_w"].rearrange("(c p) k -> p c k", p=P))
            for to, name in ((conv_b, "conv_b"), (b_dt, "b_dt"), (skip, "skip")):
                put(to[:, :], w[name].rearrange("(c p) -> p c", p=P), allow_slow_non_contiguous=True)
            put(a_log[:, :], w["a_log"].partition_broadcast(P))
            put(pick[:, :, :], w["pick"].rearrange("r (n p) -> r n p", p=P))
            assert n[0] == 10

            def body(b, more):
                if more:
                    sp.wait_ge(res_ready.sem, res_ready.at(b))
                    sp.dma_start(x[:, :, :], tiles_of(src[bass.ds(b * L + L, L), :])).then_inc(x_in, 16)
                for t in range(TS):
                    sp.wait_ge(out_ready.sem, out_ready.at(b, t + 1))
                    sp.dma_start(dst[bass.ds(b * L + t * P, P), :], out[:, t % 2, :]).then_inc(out_sent.sems[t % 2], 16)

            with sp.Fori(0, B - 1) as b:
                body(b, True)
            body(B - 1, False)
            for side in range(2):
                sp.wait_ge(out_sent.sems[side], 16 * (1 + B * TS // 2))

        @block.gpsimd
        def _(pool):
            give_credit(pool, bu_ready)
            nc.gpsimd.memset(minus_half[:, :], -0.5)
            nc.gpsimd.memset(u[:, :, 0:1], 0.0)
            nc.gpsimd.memset(u[:, :, L + 1:L + 2], 0.0)
            nc.gpsimd.memset(eps[:, :], EPS).then_inc(consts.sem, 1)
            pool.wait_ge(consts.sem, consts.at(0))

            def body(b):
                rstd_of(nc, pool, mv, rstd, eps, minus_half, TS, mv_ready, eps_added, rstd_ready, b)
                pool.wait_ge(h0_ready.sem, h0_ready.at(b))
                nc.gpsimd.tensor_tensor(res[:, :, :], x[:, :, :], h0[:, :, :], ALU.add).then_inc(res_ready.sem, 1)
                pool.wait_ge(uc_ready.sem, uc_ready.at(b))
                pool.sem_inc(stand["pool"], 1)
                for cp in range(CT // 2):
                    def one(side, n, i, more, more2):
                        pool.wait_ge(b_copied.sem, b_copied.at(i))
                        for c in range(2):
                            pool.wait_ge(state_ready.sem, state_ready.at(i - 2, c + 1))
                            nc.gpsimd.tensor_tensor(bu[:, side, c, :], b_rows[:, side, :],
                                                                uc[:, 2 * cp + c, :], ALU.mult).then_inc(bu_ready.sem, 1)
                    each_state(pool, b, cp, one)

            each_sequence(pool, body)

        @block.scalar
        def _(act):
            give_credit(act, b_copied)
            act.wait_ge(weights, 16 * 10)
            nc.scalar.activation(decay[:, :], a_log[:, :], ACT.Exp).then_inc(decay_part.sem, 1)
            act.wait_ge(decay_part.sem, decay_part.at(0))
            nc.scalar.activation(decay[:, :], decay[:, :], ACT.Copy, scale=-1.0).then_inc(decay_ready.sem, 1)
            act.wait_ge(decay_ready.sem, decay_ready.at(0))

            def body(b):
                for j in range(HALVES):
                    act.wait_ge(tp_ready.sem, tp_ready.at(b, j + 1))
                    nc.scalar.activation(hT[:, :, j * BLK:(j + 1) * BLK],
                                                     pb[:, :].rearrange("p (k t) -> p k t", t=BLK), ACT.Copy).then_inc(hT_ready.sem, 1)
                for f in range(2 * CT):
                    c, j = f // 2, f % 2
                    act.wait_ge(z_made.sem, z_made.at(b, f + 1))
                    nc.scalar.activation(z[:, c, j * BLK:(j + 1) * BLK], half(py[1], j), ACT.Silu).then_inc(z_ready.sem, 1)
                    if j:
                        act.wait_ge(conv_steps.sem, conv_steps.at(b, 3 * c + 3))
                        nc.scalar.activation(uc[:, c, :], work[:, c, :], ACT.Silu).then_inc(uc_ready.sem, 1)
                act.wait_ge(xd_made.sem, xd_made.at(b))
                nc.scalar.activation(dtp, pc[0:RANK, :], ACT.Copy).then_inc(dtp_ready.sem, 1)
                for c in range(CT):
                    act.wait_ge(dt_biased.sem, dt_biased.at(b, c + 1))
                    nc.scalar.activation(work[:, c, :], dt[:, c, :], ACT.Abs).then_inc(soft_steps.sem, 1)
                    act.wait_ge(soft_steps.sem, soft_steps.at(b, 2 * c + 1))
                    nc.scalar.activation(work[:, c, :], work[:, c, :], ACT.Exp, scale=-1.0).then_inc(soft_steps.sem, 1)
                for c in range(CT):
                    act.wait_ge(soft_steps.sem, soft_steps.at(b, 2 * c + 2))
                    nc.scalar.activation(work[:, c, :], work[:, c, :], ACT.Ln, bias=1.0).then_inc(soft_ready.sem, 1)
                act.wait_ge(dt_ready.sem, dt_ready.at(b))
                for cp in range(CT // 2):
                    def one(side, n, i, more, more2):
                        act.wait_ge(bu_ready.sem, bu_ready.at(i - 2))
                        act.wait_ge(state_ready.sem, state_ready.at(i - 2))
                        act.wait_ge(b_made.sem, b_made.at(i))
                        nc.scalar.activation(b_rows[:, side, :], pb[:, :], ACT.Copy).then_inc(b_copied.sem, 1)
                        for c in range(2):
                            nc.scalar.activation(da[:, side, c, :], dt[:, 2 * cp + c, :], ACT.Exp,
                                                             scale=decay[:, bass.ds(n, 1)]).then_inc(da_ready.sem, 1)
                    each_state(act, b, cp, one)

            each_sequence(act, body)

        @block.vector
        def _(dve):
            give_credit(dve, y_ready, out_ready, state_ready, seen_ready, out_sent)
            dve.wait_ge(weights, 16 * 10)
            dve.wait_ge(consts.sem, consts.at(0))
            for c in range(CT):
                last = nc.vector.tensor_scalar(skip_diag[:, c, :], ident, skip[:, c:c + 1], None, ALU.mult)
            last.then_inc(skip_ready.sem, 1)

            def body(b):
                dve.wait_ge(x_in, b * 16 + 16)
                stats_of(nc, dve, x, TS, sums, mv, sums_ready, mv_ready, b)
                dve.wait_ge(rstd_ready.sem, rstd_ready.at(b))
                normalise(nc, h0, x, mv, rstd, TS).then_inc(h0_ready.sem, 1)
                for f in range(2 * CT):
                    c, j = f // 2, f % 2
                    dve.wait_ge(u_made.sem, u_made.at(b, f + 1))
                    nc.vector.tensor_copy(u[:, c, 1 + j * BLK:1 + (j + 1) * BLK], half(py[0], j)).then_inc(u_copied.sem, 1)
                    if j:
                        dve.wait_ge(u_copied.sem, u_copied.at(b, f + 1))
                        w0, w1, w2 = (conv_w[:, c, k:k + 1] for k in range(3))
                        nc.vector.tensor_scalar(work[:, c, :], u[:, c, 1:L + 1], w1, conv_b[:, c:c + 1],
                                                              ALU.mult, ALU.add).then_inc(conv_steps.sem, 1)
                        for k, wk in ((0, w0), (2, w2)):
                            dve.wait_ge(conv_steps.sem, conv_steps.at(b, 3 * c + 1 + k // 2))
                            nc.vector.scalar_tensor_tensor(work[:, c, :], u[:, c, k:k + L], wk,
                                                                         work[:, c, :], ALU.mult, ALU.add).then_inc(conv_steps.sem, 1)
                dve.wait_ge(xd_made.sem, xd_made.at(b))
                rows = pc[RANK:RANK + 2 * NS, :]
                R = 2 * NS
                nc.vector.tensor_copy(parts[0:R, :], rows).then_inc(part_steps.sem, 1)
                dve.wait_ge(part_steps.sem, part_steps.at(b, 1))
                nc.vector.tensor_tensor(rest, rows, parts[0:R, :], ALU.subtract).then_inc(part_steps.sem, 1)
                dve.wait_ge(part_steps.sem, part_steps.at(b, 2))
                nc.vector.tensor_copy(middle[:, :], rest).then_inc(part_steps.sem, 1)
                dve.wait_ge(part_steps.sem, part_steps.at(b, 3))
                nc.vector.tensor_copy(parts[R:2 * R, :], middle[:, :])
                nc.vector.tensor_tensor(parts[2 * R:3 * R, :], rest, middle[:, :], ALU.subtract).then_inc(part_steps.sem, 1)
                for c in range(CT):
                    dve.wait_ge(dt_made.sem, dt_made.at(b, c + 1))
                    nc.vector.tensor_scalar(dt[:, c, :], py[c % 2][:, :], b_dt[:, c:c + 1], None, ALU.add).then_inc(dt_biased.sem, 1)
                for c in range(CT):
                    dve.wait_ge(soft_ready.sem, soft_ready.at(b, c + 1))
                    nc.vector.scalar_tensor_tensor(dt[:, c, :], dt[:, c, :], 0.0, work[:, c, :],
                                                               ALU.max, ALU.add).then_inc(dt_ready.sem, 1)
                for cp in range(CT // 2):
                    def one(side, n, i, more, more2):
                        for c in range(2):
                            dve.wait_ge(da_ready.sem, da_ready.at(i, c + 1))
                            dve.wait_ge(bu_ready.sem, bu_ready.at(i, c + 1))
                            dve.wait_ge(seen_ready.sem, seen_ready.at(i - 1, c + 1))
                            nc.vector.tensor_tensor_scan(state[:, c, :], da[:, side, c, :],
                                                         bu[:, side, c, :], 0.0, ALU.mult, ALU.add).then_inc(state_ready.sem, 1)
                        for c in range(2):
                            dve.wait_ge(state_ready.sem, state_ready.at(i, c + 1))
                            dve.wait_ge(c_made.sem, c_made.at(i))
                            dve.wait_ge(added.sem, added.at(i - 1, c + 1))
                            nc.vector.tensor_tensor(seen[:, c, :], state[:, c, :], pc[:, :], ALU.mult).then_inc(seen_ready.sem, 1)
                    each_state(dve, b, cp, one)
                    for c in range(2):
                        dve.wait_ge(added.sem, added.at((b * (CT // 2) + cp) * NS + NS - 1, c + 1))
                        nc.vector.tensor_tensor(u[:, 2 * cp + c, 1:L + 1], py[c][:, :], z[:, 2 * cp + c, :],
                                                           ALU.mult).then_inc(y_ready.sem, 1)
                for t in range(TS):
                    dve.wait_ge(out_made.sem, out_made.at(b, t + 1))
                    dve.wait_ge(out_sent.sems[t % 2], (b * (TS // 2) + t // 2 + 1) * 16)
                    nc.vector.tensor_tensor(out[:, t % 2, :], res[:, t, :],
                                                         [pb, pc][t % 2][:, 0:D], ALU.add).then_inc(out_ready.sem, 1)

            each_sequence(dve, body)

        @block.tensor
        def _(pe):
            give_credit(pe, added)
            pe.wait_ge(weights, 16 * 10)
            pe.wait_ge(skip_ready.sem, skip_ready.at(0))

            def body(b):
                pe.wait_ge(h0_ready.sem, h0_ready.at(b))
                pe.wait_ge(out_ready.sem, out_ready.at(b - 1))
                for j in range(HALVES):
                    if j:
                        pe.wait_ge(hT_ready.sem, hT_ready.at(b, j))
                    for k in range(KD):
                        for t in range(TB):
                            last = nc.tensor.transpose(pb[:, k * BLK + t * P:k * BLK + (t + 1) * P],
                                                       h0[:, j * TB + t, k * P:(k + 1) * P], ident)
                    last.then_inc(tp_ready.sem, 1)
                pe.wait_ge(hT_ready.sem, hT_ready.at(b))
                pe.wait_ge(y_ready.sem, y_ready.at(b - 1))
                for f in range(2 * CT):
                    c, j = f // 2, f % 2
                    for g, (made, read) in enumerate(((u_made, u_copied), (z_made, z_ready))):
                        if f >= 2:
                            pe.wait_ge(read.sem, read.at(b, f - 1))
                        for k in range(KD):
                            last = nc.tensor.matmul(half(py[g], j), w_in[:, k, g * HID + c * P:g * HID + (c + 1) * P],
                                                    hT[:, k, j * BLK:(j + 1) * BLK], start=(k == 0), stop=(k == KD - 1))
                        last.then_inc(made.sem, 1)
                for c in range(CT):
                    pe.wait_ge(uc_ready.sem, uc_ready.at(b, c + 1))
                    for j in range(HALVES):
                        last = nc.tensor.matmul(half(pc, j)[0:RANK + 2 * NS, :], w_x[:, c, :],
                                                uc[:, c, j * BLK:(j + 1) * BLK], start=(c == 0), stop=(c == CT - 1))
                last.then_inc(xd_made.sem, 1)
                pe.wait_ge(dtp_ready.sem, dtp_ready.at(b))
                pe.wait_ge(u_copied.sem, u_copied.at(b))
                pe.wait_ge(z_ready.sem, z_ready.at(b))
                for c in range(CT):
                    if c >= 2:
                        pe.wait_ge(dt_biased.sem, dt_biased.at(b, c - 1))
                    for j in range(HALVES):
                        last = nc.tensor.matmul(half(py[c % 2], j), w_dt[:, c * P:(c + 1) * P],
                                                dtp[:, j * BLK:(j + 1) * BLK], start=True, stop=True)
                    last.then_inc(dt_made.sem, 1)

                def spread(bank, row):
                    for j in range(HALVES):
                        last = nc.tensor.matmul(half(bank, j), pick[:, bass.ds(row, 1), :].squeeze(1)
                                                if not isinstance(row, int) else pick[:, row, :],
                                                parts[:, j * BLK:(j + 1) * BLK], start=True, stop=True)
                    return last

                pe.wait_ge(part_steps.sem, part_steps.at(b))
                pe.wait_ge(dt_biased.sem, dt_biased.at(b))
                for cp in range(CT // 2):
                    if cp:
                        pe.wait_ge(y_ready.sem, y_ready.at(b, 2 * cp))
                    for c in range(2):
                        for j in range(HALVES):
                            nc.tensor.matmul(half(py[c], j), skip_diag[:, 2 * cp + c, :],
                                             uc[:, 2 * cp + c, j * BLK:(j + 1) * BLK], start=True, stop=False)
                    base = (b * (CT // 2) + cp) * NS
                    pe.wait_ge(b_copied.sem, b_copied.at(base - 1))
                    spread(pb, 0).then_inc(b_made.sem, 1)
                    pe.wait_ge(b_copied.sem, b_copied.at(base))
                    spread(pb, 1).then_inc(b_made.sem, 1)
                    pe.wait_ge(seen_ready.sem, seen_ready.at(base - 1))
                    spread(pc, NS).then_inc(c_made.sem, 1)

                    def one(side, n, i, more, more2):
                        if more2:
                            pe.wait_ge(b_copied.sem, b_copied.at(i + 1))
                            pe.sem_inc(stand["pe"], 1)
                            spread(pb, n + 2).then_inc(b_made.sem, 1)
                        for c in range(2):
                            pe.wait_ge(seen_ready.sem, seen_ready.at(i, c + 1))
                            if c and more:
                                pe.sem_inc(stand["pe"], 1)
                                spread(pc, n + NS + 1).then_inc(c_made.sem, 1)
                            for j in range(HALVES):
                                last = nc.tensor.matmul(half(py[c], j), ident, seen[:, c, j * BLK:(j + 1) * BLK],
                                                        start=False, stop=not more)
                            last.then_inc(added.sem, 1)
                    each_state(pe, b, cp, one)
                pe.wait_ge(y_ready.sem, y_ready.at(b))
                pe.wait_ge(seen_ready.sem, seen_ready.at((b * (CT // 2) + CT // 2 - 1) * NS + NS - 1))
                for t in range(TS):
                    bank = [pb, pc][t % 2]
                    if t >= 2:
                        pe.wait_ge(out_ready.sem, out_ready.at(b, t - 1))
                    for c in range(CT):
                        last = nc.tensor.matmul(bank[:, 0:D], u[:, c, 1 + t * P:1 + (t + 1) * P], w_out[:, c, :],
                                                start=(c == 0), stop=(c == CT - 1))
                    last.then_inc(out_made.sem, 1)

            each_sequence(pe, body)

def moe_stage(nc, tag, w, src, dst, ident):
    with ExitStack() as ctx:
        s = Scope(nc, ctx, tag)
        experts = s.sb("experts", [P, KD, E * D])
        router = s.sb("router", [P, KD, E])
        router_b = s.sb("router_b", [P, E])
        expert_b = s.sb("expert_b", [E, D])
        rank = s.sb("rank", [P, E])
        minus_half, eps = s.sb("minus_half", [P, TB]), s.sb("eps", [P, TB])
        x = s.sb("x", [P, 2, TB, D])
        sums, mv, rstd = s.sb("sums", [P, TB, 6]), s.sb("mv", [P, TB, 2]), s.sb("rstd", [P, TB])
        n = s.sb("n", [P, TB, D])
        hT = s.sb("hT", [P, 2, KD, BLK])
        logit, prob = s.sb("logit", [P, TB, E]), s.sb("prob", [P, TB, E])
        best, total, key_max = s.sb("best", [P, TB]), s.sb("total", [P, TB]), s.sb("key_max", [P, TB])
        key = s.sb("key", [P, TB, E])
        gate = s.sb("gate", [P, 2, TB, E])
        gateT = s.sb("gateT", [E, 2, BLK])
        y = s.sb("y", [P, 2, TB, D])
        tp = [s.ps(f"tp{k}", [P, BLK]) for k in range(KD)]
        ex = [s.ps(f"ex{k}", [P, 2 * D]) for k in range(4)]
        small = s.ps("small", [P, BLK])
        bias = s.ps("bias", [P, BLK])
        PAIRS = E // 2
        GATE_STEPS = 9

        weights = s.sem("weights")
        consts = s.counter("consts")
        x_in = s.transfer("x_in")
        sums_ready, mv_ready = s.counter("sums_ready", per=2), s.counter("mv_ready")
        eps_added, rstd_ready, n_ready = s.counter("eps_added"), s.counter("rstd_ready"), s.counter("n_ready")
        tp_ready, hT_ready = s.counter("tp_ready"), s.counter("hT_ready", credit=1)
        logits_ready, gate_steps, prob_ready = s.counter("logits_ready"), s.counter("gate_steps", per=GATE_STEPS, credit=1), s.counter("prob_ready")
        gateT_made, gateT_ready = s.counter("gateT_made"), s.counter("gateT_ready", credit=1)
        bias_ready = s.counter("bias_ready", per=TB)
        base_ready = s.counter("base_ready", per=TB, credit=1)
        ex_ready = s.counter("ex_ready", per=TB * PAIRS)
        sum_ready = s.counter("sum_ready", per=TB * E, credit=1)
        y_out = s.transfer("y_out", credit=1)
        block = ctx.enter_context(nc.Block())

        @block.sync
        def _(sp):
            def load(turn):
                sp.dma_start(x[:, turn.side, :, :], flat_rows(src, turn)).then_inc(x_in.sems[turn.side], 16)

            load(Turn(0, 0))
            load(Turn(0, 1))
            sp.dma_start(router[:, :, :], w["router"].rearrange("(k p) n -> p k n", p=P)).then_inc(weights, 16)
            sp.dma_start(router_b[:, :], w["router_b"].partition_broadcast(P)).then_inc(weights, 16)
            sp.dma_start(rank[:, :], w["rank"].partition_broadcast(P)).then_inc(weights, 16)
            sp.dma_start(expert_b[:, :], w["expert_b"]).then_inc(weights, 16)
            sp.dma_start(experts[:, :, :], w["experts"].rearrange("(k p) n -> p k n", p=P)).then_inc(weights, 16)

            def store(turn):
                sp.wait_ge(sum_ready.sem, sum_ready.at(turn.i))
                sp.dma_start(flat_rows(dst, turn), y[:, turn.side, :, :]).then_inc(y_out.sems[turn.side], 16)

            with sp.Fori(0, NBLK // 2 - 1) as pair:
                for side in range(2):
                    sp.wait_ge(n_ready.sem, n_ready.at(Turn(pair, side).i))
                    sp.wait_ge(base_ready.sem, base_ready.at(Turn(pair, side).i))
                    load(Turn(pair + 1, side))
                    store(Turn(pair, side))
            for side in range(2):
                store(Turn(NBLK // 2 - 1, side))
            for side in range(2):
                sp.wait_ge(y_out.sems[side], y_out.total(NBLK // 2))

        @block.gpsimd
        def _(pool):
            nc.gpsimd.memset(minus_half[:, :], -0.5)
            nc.gpsimd.memset(eps[:, :], EPS).then_inc(consts.sem, 1)
            pool.wait_ge(consts.sem, consts.at(0))

            def front(turn):
                rstd_of(nc, pool, mv, rstd, eps, minus_half, TB, mv_ready, eps_added, rstd_ready, turn.i)

            front(Turn(0, 0))
            turns(pool, NBLK, lambda turn, more: front(turn.next()) if more else None)

        @block.scalar
        def _(act):
            give_credit(act, hT_ready)

            def hidden(turn):
                act.wait_ge(tp_ready.sem, tp_ready.at(turn.i))
                for k in range(KD):
                    last = nc.scalar.activation(hT[:, turn.side, k, :], tp[k][:, :], ACT.Copy)
                last.then_inc(hT_ready.sem, 1)

            def probs(turn):
                act.wait_ge(gate_steps.sem, gate_steps.at(turn.i, 3))
                nc.scalar.activation(prob[:, :, :], logit[:, :, :], ACT.Exp).then_inc(prob_ready.sem, 1)

            def body(turn, more):
                if more:
                    hidden(turn.next())
                    probs(turn.next())

            hidden(Turn(0, 0))
            probs(Turn(0, 0))
            turns(act, NBLK, body)

        @block.vector
        def _(dve):
            give_credit(dve, gate_steps, gateT_ready, base_ready, sum_ready, y_out)

            def front(turn):
                dve.wait_ge(x_in.sems[turn.side], x_in.at(turn))
                stats_of(nc, dve, x[:, turn.side, :, :], TB, sums, mv, sums_ready, mv_ready, turn.i)
                dve.wait_ge(rstd_ready.sem, rstd_ready.at(turn.i))
                normalise(nc, n, x[:, turn.side, :, :], mv, rstd, TB).then_inc(n_ready.sem, 1)

            def gates(turn):
                step = [0]

                def link(ins):
                    ins.then_inc(gate_steps.sem, 1)
                    step[0] += 1
                    dve.wait_ge(gate_steps.sem, gate_steps.at(turn.i, step[0]))

                def wide(a):
                    return a[:, :].unsqueeze(2).to_broadcast([P, TB, E])

                def all_tiles(a):
                    return a[:, :].unsqueeze(1).to_broadcast([P, TB, E])

                g = gate[:, turn.side, :, :]
                dve.wait_ge(logits_ready.sem, logits_ready.at(turn.i))
                logits = small[:, 0:TB * E].rearrange("p (t e) -> p t e", e=E)
                link(nc.vector.tensor_tensor(logit[:, :, :], logits, all_tiles(router_b), ALU.add))
                link(nc.vector.tensor_reduce(best[:, :], logit[:, :, :], AX.X, ALU.max))
                link(nc.vector.tensor_tensor(logit[:, :, :], logit[:, :, :], wide(best), ALU.subtract))
                link(nc.vector.scalar_tensor_tensor(key[:, :, :], logit[:, :, :], 0.0, all_tiles(rank),
                                                    ALU.is_equal, ALU.mult))
                link(nc.vector.tensor_reduce(key_max[:, :], key[:, :, :], AX.X, ALU.max))
                link(nc.vector.tensor_tensor(g, key[:, :, :], wide(key_max), ALU.is_equal))
                dve.wait_ge(prob_ready.sem, prob_ready.at(turn.i))
                link(nc.vector.tensor_reduce(total[:, :], prob[:, :, :], AX.X, ALU.add))
                link(nc.vector.reciprocal(total[:, :], total[:, :]))
                link(nc.vector.tensor_tensor(g, g, wide(total), ALU.mult))
                assert step[0] == GATE_STEPS

            def tile(turn, t):
                acc = y[:, turn.side, t, :]
                dve.wait_ge(bias_ready.sem, bias_ready.at(turn.i, t + 1))
                if t == 0:
                    dve.wait_ge(y_out.sems[turn.side], y_out.at(turn, back=1))
                nc.vector.tensor_tensor(acc, x[:, turn.side, t, :], bias[:, 0:D], ALU.add).then_inc(base_ready.sem, 1)
                dve.wait_ge(base_ready.sem, base_ready.at(turn.i, t + 1))
                for e in range(E):
                    if e % 2 == 0:
                        dve.wait_ge(ex_ready.sem, ex_ready.at(turn.i, t * PAIRS + e // 2 + 1))
                    nc.vector.scalar_tensor_tensor(
                        acc, ex[e // 2][:, e % 2 * D:(e % 2 + 1) * D], gate[:, turn.side, t, e:e + 1], acc,
                        ALU.mult, ALU.add).then_inc(sum_ready.sem, 1)
                    if e < E - 1:
                        dve.wait_ge(sum_ready.sem, sum_ready.at(turn.i, t * E + e + 1))

            def gate_columns(turn):
                dve.wait_ge(gateT_made.sem, gateT_made.at(turn.i))
                nc.vector.tensor_copy(gateT[:, turn.side, :], small[0:E, :]).then_inc(gateT_ready.sem, 1)

            def body(turn, more):
                if more:
                    front(turn.next())
                tile(turn, 0)
                tile(turn, 1)
                if more:
                    gates(turn.next())
                tile(turn, 2)
                if more:
                    gate_columns(turn.next())
                tile(turn, 3)

            dve.wait_ge(weights, 16 * 5)
            front(Turn(0, 0))
            gates(Turn(0, 0))
            gate_columns(Turn(0, 0))
            turns(dve, NBLK, body)

        @block.tensor
        def _(pe):
            def transposes(turn):
                pe.wait_ge(n_ready.sem, n_ready.at(turn.i))
                pe.wait_ge(hT_ready.sem, hT_ready.at(turn.i - 1))
                for k in range(KD):
                    for t in range(TB):
                        last = nc.tensor.transpose(tp[k][:, t * P:(t + 1) * P], n[:, t, k * P:(k + 1) * P], ident)
                last.then_inc(tp_ready.sem, 1)

            def route(turn):
                pe.wait_ge(hT_ready.sem, hT_ready.at(turn.i))
                pe.wait_ge(gateT_ready.sem, gateT_ready.at(turn.i - 1))
                for t in range(TB):
                    for k in range(KD):
                        last = nc.tensor.matmul(small[:, t * E:(t + 1) * E], hT[:, turn.side, k, t * P:(t + 1) * P],
                                                router[:, k, :], start=(k == 0), stop=(k == KD - 1))
                last.then_inc(logits_ready.sem, 1)

            def gate_columns(turn):
                pe.wait_ge(gate_steps.sem, gate_steps.at(turn.i))
                for t in range(TB):
                    last = nc.tensor.transpose(small[0:E, t * P:(t + 1) * P], gate[:, turn.side, t, :], ident)
                last.then_inc(gateT_made.sem, 1)

            def tile(turn, t):
                if t == 0:
                    pe.wait_ge(gateT_ready.sem, gateT_ready.at(turn.i))
                if t:
                    pe.wait_ge(base_ready.sem, base_ready.at(turn.i, t))
                else:
                    pe.wait_ge(base_ready.sem, base_ready.at(turn.i - 1))
                nc.tensor.matmul(bias[:, 0:D], gateT[:, turn.side, t * P:(t + 1) * P], expert_b[:, :],
                                               start=True, stop=True).then_inc(bias_ready.sem, 1)
                for pair in range(PAIRS):
                    if t:
                        pe.wait_ge(sum_ready.sem, sum_ready.at(turn.i, (t - 1) * E + 2 * pair + 2))
                    else:
                        pe.wait_ge(sum_ready.sem, sum_ready.at(turn.i - 1, (TB - 1) * E + 2 * pair + 2))
                    for k in range(KD):
                        last = nc.tensor.matmul(ex[pair][:, :], hT[:, turn.side, k, t * P:(t + 1) * P],
                                                experts[:, k, pair * 2 * D:(pair + 1) * 2 * D],
                                                start=(k == 0), stop=(k == KD - 1))
                    last.then_inc(ex_ready.sem, 1)

            def body(turn, more):
                tile(turn, 0)
                if more:
                    transposes(turn.next())
                tile(turn, 1)
                if more:
                    route(turn.next())
                tile(turn, 2)
                if more:
                    gate_columns(turn.next())
                tile(turn, 3)

            pe.wait_ge(weights, 16 * 5)
            transposes(Turn(0, 0))
            route(Turn(0, 0))
            gate_columns(Turn(0, 0))
            turns(pe, NBLK, body)

def linear_attention_stage(nc, tag, w, src, dst, ident):
    PR = H1 // 2
    GP = 4
    VW = DH + 1
    BANKS = [(0, 3), (3, 6), (6, 8)]
    with ExitStack() as ctx:
        s = Scope(nc, ctx, tag)
        wT = s.sb("wT", [P, 2, PR, D])
        proj2 = s.sb("proj2", [P, P])
        wqk = s.sb("wqk", [P, 2, KD, H1 * DH])
        wv = s.sb("wv", [P, KD, H1 * DH])
        wo = s.sb("wo", [P, PR, D])
        gain, offset = s.sb("gain", [P, KD]), s.sb("offset", [P, KD])
        causal = s.sb("causal", [P, P])
        minus_half, eps = s.sb("minus_half", [P, 1]), s.sb("eps", [P, 1])
        x, keep = s.sb("x", [P, 2, 1, D]), s.sb("keep", [P, 2, 1])
        sums, mv, rstd, rstd2 = s.sb("sums", [P, 1, 6]), s.sb("mv", [P, 1, 2]), s.sb("rstd", [P, 1]), s.sb("rstd2", [P, 1])
        h, h_keep, n = s.sb("h", [P, 2, D]), s.sb("h_keep", [P, D]), s.sb("n", [P, D])
        hT = s.sb("hT", [P, KD, P])
        qkT = s.sb("qkT", [P, 2, 2, PR, P])
        grown = s.sb("grown", [P, 2, GP * P])
        v = s.sb("v", [P, 2, H1, VW])
        k_rows = s.sb("k_rows", [P, PR, P])
        scores = s.sb("scores", [P, H1, P])
        state = s.sb("state", [P, PR, 2 * VW])
        den = s.sb("den", [P, H1])
        attn = s.sb("attn", [P, H1, DH])
        attnT = s.sb("attnT", [P, PR, P])
        y = s.sb("y", [P, 2, D])
        pa = [s.ps(f"pa{k}", [P, 512]) for k in range(2)]
        pb = [s.ps(f"pb{k}", [P, 512]) for k in range(2)]
        pc = [s.ps(f"pc{k}", [P, 512]) for k in range(3)]
        pt = s.ps("pt", [P, 512])
        score_banks = [pb[0], pb[1], pc[0], pc[1]]

        weights, proj_in, zeroed = s.sem("weights"), s.sem("proj_in"), s.counter("zeroed")
        folded, folded_read = s.counter("folded", per=4 * KD), s.counter("folded_read", per=4 * KD)
        consts = s.counter("consts")
        x_in, keep_in = s.transfer("x_in"), s.transfer("keep_in")
        keep_free = s.sem("keep_free")
        sums_ready, mv_ready = s.counter("sums_ready", per=2), s.counter("mv_ready")
        eps_added, rstd_ready, rstd2_ready = s.counter("eps_added", per=4), s.counter("rstd_ready"), s.counter("rstd2_ready")
        h_ready, n_ready, kept = s.counter("h_ready"), s.counter("n_ready"), s.counter("kept")
        tp_ready, hT_ready = s.counter("tp_ready"), s.counter("hT_ready", credit=1)
        proj_ready, exp_ready = s.counter("proj_ready", per=6), s.counter("exp_ready", per=4)
        min_ready, phi_ready = s.counter("min_ready", per=4), s.counter("phi_ready", per=4, credit=1)
        v_ready = s.counter("v_ready", per=2, credit=1)
        kt_ready, k_rows_ready = s.counter("kt_ready", per=2), s.counter("k_rows_ready", per=2)
        st_ready, scores_ready = s.counter("st_ready", per=4), s.counter("scores_ready", per=4)
        num_ready, den_steps = s.counter("num_ready", per=3), s.counter("den_steps", per=6)
        attn_ready = s.counter("attn_ready", per=3)
        delta_ready, state_ready = s.counter("delta_ready", per=3), s.counter("state_ready", per=3, credit=1)
        at_ready, attnT_ready = s.counter("at_ready", per=2), s.counter("attnT_ready", per=2, credit=1)
        out_ready, y_ready = s.counter("out_ready"), s.counter("y_ready", credit=2)
        y_out = s.transfer("y_out", credit=1)
        block = ctx.enter_context(nc.Block())

        @block.sync
        def _(sp):
            def rows(stream, turn):
                at = turn.i * P
                return stream[bass.ds(at if isinstance(at, int) else sp.snap(at), P), :]

            def load(to, rows_of, turn, sems):
                sp.dma_start(to, rows_of).then_inc(sems[turn.side], 16)

            for first in (Turn(0, 0), Turn(0, 1)):
                load(x[:, first.side, 0, :], rows(src, first), first, x_in.sems)
                load(keep[:, first.side, :], rows(w["keep"], first), first, keep_in.sems)
            for j, name in enumerate(("wqT", "wkT")):
                sp.dma_start(wT[:, j, :, :], w[name].rearrange("(r p) d -> p r d", p=P)).then_inc(proj_in, 16)
            sp.wait_ge(zeroed.sem, zeroed.at(0))
            for j in range(2):
                sp.dma_start(proj2[j * DH:(j + 1) * DH, j * DH:(j + 1) * DH], w["proj"]).then_inc(proj_in, 16)
            sp.dma_start(wv[:, :, :], w["wv"].rearrange("(k p) n -> p k n", p=P)).then_inc(weights, 16)
            sp.dma_start(wo[:, :, :], w["wo"].rearrange("(r p) n -> p r n", p=P)).then_inc(weights, 16)
            sp.dma_start(causal[:, :], w["causal"]).then_inc(weights, 16)
            for vec, to in ((w["gain"], gain), (w["offset"], offset)):
                sp.dma_start(to[:, :], vec.rearrange("(k p) -> p k", p=P),
                             allow_slow_non_contiguous=True).then_inc(weights, 16)

            def body(turn, before, more, more2):
                then = Turn(turn.pair + 1, turn.side)
                if more2:
                    x_rows, keep_rows = rows(src, then), rows(w["keep"], then)
                if before:
                    y_rows = rows(dst, turn.before())
                if more2:
                    sp.wait_ge(h_ready.sem, h_ready.at(turn.i))
                    load(x[:, turn.side, 0, :], x_rows, then, x_in.sems)
                if before:
                    sp.wait_ge(y_ready.sem, y_ready.at(turn.i - 1))
                    sp.dma_start(y_rows, y[:, 1 - turn.side, :]).then_inc(y_out.sems[1 - turn.side], 16)
                if more2:
                    sp.wait_ge(k_rows_ready.sem, k_rows_ready.at(turn.i))
                    sp.wait_ge(state_ready.sem, state_ready.at(turn.i))
                    sp.sem_inc(keep_free, 1)
                    load(keep[:, turn.side, :], keep_rows, then, keep_in.sems)

            trailing(sp, body)
            sp.wait_ge(y_ready.sem, y_ready.at(NT - 1))
            sp.dma_start(rows(dst, Turn(NT // 2 - 1, 1)), y[:, 1, :]).then_inc(y_out.sems[1], 16)
            for side in range(2):
                sp.wait_ge(y_out.sems[side], y_out.total(NT // 2))

        @block.gpsimd
        def _(pool):
            nc.gpsimd.memset(proj2[:, :], 0.0).then_inc(zeroed.sem, 1)
            nc.gpsimd.memset(minus_half[:, :], -0.5)
            nc.gpsimd.memset(state[:, :, :], 0.0)
            nc.gpsimd.memset(v[:, :, :, DH:VW], 1.0)
            nc.gpsimd.memset(eps[:, :], EPS).then_inc(consts.sem, 1)
            pool.wait_ge(consts.sem, consts.at(0))

            def front(turn):
                i = turn.i
                pool.wait_ge(mv_ready.sem, mv_ready.at(i))
                nc.gpsimd.tensor_tensor(rstd[:, :], mv[:, :, 1], eps[:, :], ALU.add).then_inc(eps_added.sem, 1)
                pool.wait_ge(eps_added.sem, eps_added.at(i, 1))
                nc.gpsimd.tensor_tensor(rstd[:, :], rstd[:, :], minus_half[:, :], ALU.pow).then_inc(rstd_ready.sem, 1)
                pool.wait_ge(rstd_ready.sem, rstd_ready.at(i))
                nc.gpsimd.tensor_tensor(rstd2[:, :], mv[:, :, 1], rstd[:, :], ALU.mult).then_inc(eps_added.sem, 1)
                pool.wait_ge(eps_added.sem, eps_added.at(i, 2))
                nc.gpsimd.tensor_tensor(rstd2[:, :], rstd2[:, :], rstd[:, :], ALU.mult).then_inc(eps_added.sem, 1)
                pool.wait_ge(eps_added.sem, eps_added.at(i, 3))
                nc.gpsimd.tensor_tensor(rstd2[:, :], rstd2[:, :], eps[:, :], ALU.add).then_inc(eps_added.sem, 1)
                pool.wait_ge(eps_added.sem, eps_added.at(i, 4))
                nc.gpsimd.tensor_tensor(rstd2[:, :], rstd2[:, :], minus_half[:, :], ALU.pow).then_inc(rstd2_ready.sem, 1)

            def body(turn, before, more, more2):
                if more2:
                    front(Turn(turn.pair + 1, turn.side))

            front(Turn(0, 0))
            front(Turn(0, 1))
            trailing(pool, body)

        @block.scalar
        def _(act):
            give_credit(act, v_ready)
            give_credit(act, attnT_ready)
            for f in range(4 * KD):
                j, g, k = f // (2 * KD), f // KD % 2, f % KD
                act.wait_ge(folded.sem, folded.at(0, f + 1))
                nc.scalar.activation(wqk[:, j, k, g * 512:(g + 1) * 512], pa[f % 2][:, :], ACT.Copy).then_inc(folded_read.sem, 1)

            def grow(turn):
                for g in range(4):
                    act.wait_ge(proj_ready.sem, proj_ready.at(turn.i, g + 1))
                    act.wait_ge(phi_ready.sem, phi_ready.at(turn.i if g >= 2 else turn.i - 1, g - 1 if g >= 2 else g + 3))
                    nc.scalar.activation(grown[:, g % 2, :], pa[g % 2][:, :], ACT.Exp).then_inc(exp_ready.sem, 1)

            def values(turn, g):
                act.wait_ge(proj_ready.sem, proj_ready.at(turn.i, 5 + g))
                heads = H1 // 2
                nc.scalar.activation(v[:, turn.side, g * heads:(g + 1) * heads, 0:DH],
                                                pa[g][:, :].rearrange("p (h d) -> p h d", d=DH), ACT.Copy).then_inc(v_ready.sem, 1)

            def body(turn, before, more, more2):
                act.wait_ge(h_ready.sem, h_ready.at(turn.i))
                act.wait_ge(y_ready.sem, y_ready.at(turn.i - 1))
                nc.scalar.activation(h_keep[:, :], h[:, turn.side, :], ACT.Copy).then_inc(kept.sem, 1)
                act.wait_ge(keep_in.sems[turn.side], keep_in.at(turn))
                for g in range(2):
                    act.wait_ge(kt_ready.sem, kt_ready.at(turn.i, g + 1))
                    nc.scalar.activation(
                        k_rows[:, g * GP:(g + 1) * GP, :], pb[g][:, :].rearrange("p (r d) -> p r d", d=P), ACT.Copy,
                        scale=keep[:, turn.side, :]).then_inc(k_rows_ready.sem, 1)
                if more:
                    grow(turn.next())
                    values(turn.next(), 0)
                for g in range(2):
                    act.wait_ge(at_ready.sem, at_ready.at(turn.i, g + 1))
                    nc.scalar.activation(
                        attnT[:, g * GP:(g + 1) * GP, :], pb[g][:, :].rearrange("p (r t) -> p r t", t=P), ACT.Copy).then_inc(attnT_ready.sem, 1)
                if more:
                    values(turn.next(), 1)

            act.wait_ge(consts.sem, consts.at(0))
            grow(Turn(0, 0))
            values(Turn(0, 0), 0)
            values(Turn(0, 0), 1)
            trailing(act, body)

        @block.vector
        def _(dve):
            give_credit(dve, hT_ready, phi_ready, state_ready, y_ready, y_out)

            def statistics(turn):
                dve.wait_ge(x_in.sems[turn.side], x_in.at(turn))
                stats_of(nc, dve, x[:, turn.side, :, :], 1, sums, mv, sums_ready, mv_ready, turn.i)

            def front(turn):
                dve.wait_ge(rstd_ready.sem, rstd_ready.at(turn.i))
                nc.vector.tensor_scalar(h[:, turn.side, :], x[:, turn.side, 0, :], mv[:, 0, 0:1],
                                                   rstd[:, 0:1], ALU.subtract, ALU.mult).then_inc(h_ready.sem, 1)
                dve.wait_ge(h_ready.sem, h_ready.at(turn.i))
                dve.wait_ge(rstd2_ready.sem, rstd2_ready.at(turn.i))
                nc.vector.tensor_scalar(n[:, :], h[:, turn.side, :], rstd2[:, 0:1], None, ALU.mult).then_inc(n_ready.sem, 1)

            def hidden(turn):
                dve.wait_ge(tp_ready.sem, tp_ready.at(turn.i))
                for k in range(KD):
                    last = nc.vector.tensor_scalar(hT[:, k, :], pt[:, k * P:(k + 1) * P], gain[:, k:k + 1],
                                                   offset[:, k:k + 1], ALU.mult, ALU.add)
                last.then_inc(hT_ready.sem, 1)

            def features(turn):
                for g in range(4):
                    dve.wait_ge(exp_ready.sem, exp_ready.at(turn.i, g + 1))
                    nc.vector.tensor_scalar(grown[:, g % 2, :], grown[:, g % 2, :], 1.0, None, ALU.min).then_inc(min_ready.sem, 1)
                    dve.wait_ge(min_ready.sem, min_ready.at(turn.i, g + 1))
                    nc.vector.scalar_tensor_tensor(
                        qkT[:, turn.side, g // 2, g % 2 * GP:(g % 2 + 1) * GP, :],
                        pa[g % 2][:, :].rearrange("p (r t) -> p r t", t=P), 0.0,
                        grown[:, g % 2, :].rearrange("p (r t) -> p r t", t=P), ALU.max, ALU.add).then_inc(phi_ready.sem, 1)

            def residual(turn):
                dve.wait_ge(kept.sem, kept.at(turn.i))
                dve.wait_ge(out_ready.sem, out_ready.at(turn.i))
                dve.wait_ge(y_out.sems[turn.side], y_out.at(turn, back=1))
                nc.vector.tensor_tensor(y[:, turn.side, :], h_keep[:, :], pt[:, 0:D], ALU.add).then_inc(y_ready.sem, 1)

            def body(turn, before, more, more2):
                i = turn.i
                if before:
                    residual(turn.before())
                if more:
                    hidden(turn.next())
                for g in (2, 3, 0, 1):
                    dve.wait_ge(st_ready.sem, st_ready.at(i, (g + 2) % 4 + 1))
                    nc.vector.tensor_tensor(
                        scores[:, g // 2 * 2 * GP + g % 2:(g // 2 + 1) * 2 * GP:2, :],
                        score_banks[g][:, :].rearrange("p (r t) -> p r t", t=P),
                        causal[:, :].unsqueeze(1).to_broadcast([P, GP, P]), ALU.mult).then_inc(scores_ready.sem, 1)
                if more:
                    features(turn.next())
                if more2:
                    statistics(Turn(turn.pair + 1, turn.side))
                for c, (lo, hi) in enumerate(BANKS):
                    heads = 2 * (hi - lo)
                    bank = pc[c][:, 0:heads * VW].rearrange("p (h e) -> p h e", e=VW)
                    dve.wait_ge(num_ready.sem, num_ready.at(i, c + 1))
                    nc.vector.tensor_scalar(den[:, 2 * lo:2 * hi], bank[:, :, DH], 1e-6, None, ALU.add).then_inc(den_steps.sem, 1)
                    dve.wait_ge(den_steps.sem, den_steps.at(i, 2 * c + 1))
                    nc.vector.reciprocal(den[:, 2 * lo:2 * hi], den[:, 2 * lo:2 * hi]).then_inc(den_steps.sem, 1)
                    dve.wait_ge(den_steps.sem, den_steps.at(i, 2 * c + 2))
                    nc.vector.tensor_tensor(
                        attn[:, 2 * lo:2 * hi, :], bank[:, :, 0:DH],
                        den[:, 2 * lo:2 * hi].unsqueeze(2).to_broadcast([P, heads, DH]), ALU.mult).then_inc(attn_ready.sem, 1)
                dve.wait_ge(keep_in.sems[turn.side], keep_in.at(turn))
                for c, (lo, hi) in enumerate(BANKS):
                    dve.wait_ge(delta_ready.sem, delta_ready.at(i, c + 1))
                    for j in range(2):
                        half, cols = slice(j * DH, (j + 1) * DH), slice(j * VW, (j + 1) * VW)
                        bank = pc[c][half, 0:(hi - lo) * 2 * VW].rearrange("p (r e) -> p r e", e=2 * VW)
                        last = nc.vector.scalar_tensor_tensor(
                            state[half, lo:hi, cols], state[half, lo:hi, cols], keep[half, turn.side, :],
                            bank[:, :, cols], ALU.mult, ALU.add)
                    last.then_inc(state_ready.sem, 1)
                if more2:
                    dve.wait_ge(kept.sem, kept.at(i))
                    front(Turn(turn.pair + 1, turn.side))

            dve.wait_ge(weights, 16 * 5)
            dve.wait_ge(consts.sem, consts.at(0))
            statistics(Turn(0, 0))
            front(Turn(0, 0))
            hidden(Turn(0, 0))
            features(Turn(0, 0))
            statistics(Turn(0, 1))
            front(Turn(0, 1))
            trailing(dve, body)
            residual(Turn(NT // 2 - 1, 1))

        @block.tensor
        def _(pe):
            pe.wait_ge(proj_in, 16 * 4)
            for f in range(4 * KD):
                j, g, k = f // (2 * KD), f // KD % 2, f % KD
                if f >= 2:
                    pe.wait_ge(folded_read.sem, folded_read.at(0, f - 1))
                for r in range(GP):
                    last = nc.tensor.matmul(pa[f % 2][:, r * P:(r + 1) * P], wT[:, j, g * GP + r, k * P:(k + 1) * P],
                                            proj2[:, :], start=True, stop=True)
                last.then_inc(folded.sem, 1)
            pe.wait_ge(folded_read.sem, folded_read.at(0))
            pe.wait_ge(weights, 16 * 5)

            def transposes(turn):
                pe.wait_ge(n_ready.sem, n_ready.at(turn.i))
                pe.wait_ge(hT_ready.sem, hT_ready.at(turn.i - 1))
                pe.wait_ge(y_ready.sem, y_ready.at(turn.i - 2))
                for k in range(KD):
                    last = nc.tensor.transpose(pt[:, k * P:(k + 1) * P], n[:, k * P:(k + 1) * P], ident)
                last.then_inc(tp_ready.sem, 1)

            def queries_keys(turn):
                pe.wait_ge(hT_ready.sem, hT_ready.at(turn.i))
                for g in range(4):
                    if g < 2:
                        pe.wait_ge(v_ready.sem, v_ready.at(turn.i - 1, g + 1))
                    else:
                        pe.wait_ge(phi_ready.sem, phi_ready.at(turn.i, g - 1))
                    for r in range(GP):
                        cols = slice((g % 2 * GP + r) * P, (g % 2 * GP + r + 1) * P)
                        for k in range(KD):
                            last = nc.tensor.matmul(pa[g % 2][:, r * P:(r + 1) * P], wqk[:, g // 2, k, cols],
                                                    hT[:, k, :], start=(k == 0), stop=(k == KD - 1))
                    last.then_inc(proj_ready.sem, 1)

            def values(turn, g):
                pe.wait_ge(phi_ready.sem, phi_ready.at(turn.i, 3 + g))
                for k in range(KD):
                    last = nc.tensor.matmul(pa[g][:, :], hT[:, k, :], wv[:, k, g * 512:(g + 1) * 512],
                                            start=(k == 0), stop=(k == KD - 1))
                last.then_inc(proj_ready.sem, 1)

            def scores_of(turn, g):
                i, side = turn.i, turn.side
                for j in range(2):
                    if g == 0:
                        pe.wait_ge(k_rows_ready.sem, k_rows_ready.at(i, j + 1))
                    else:
                        pe.wait_ge(state_ready.sem, state_ready.at(i - 1, j + 1))
                for a in range(GP):
                    for j in range(2):
                        half = slice(j * DH, (j + 1) * DH)
                        ins = nc.tensor.matmul(score_banks[2 * g + j][:, a * P:(a + 1) * P],
                                               qkT[half, side, 1, g * GP + a, :],
                                               qkT[half, side, 0, g * GP + a, :], start=True, stop=True)
                        if a == GP - 1:
                            ins.then_inc(st_ready.sem, 1)

            def body(turn, before, more, more2):
                i, side = turn.i, turn.side
                pe.wait_ge(phi_ready.sem, phi_ready.at(i))
                for g in range(2):
                    pe.wait_ge(attnT_ready.sem, attnT_ready.at(i - 1, g + 1))
                    for r in range(GP):
                        last = nc.tensor.transpose(pb[g][:, r * P:(r + 1) * P], qkT[:, side, 1, g * GP + r, :], ident)
                    last.then_inc(kt_ready.sem, 1)
                scores_of(turn, 1)
                if more:
                    transposes(turn.next())
                scores_of(turn, 0)
                if more:
                    queries_keys(turn.next())
                pe.wait_ge(v_ready.sem, v_ready.at(i))
                pe.wait_ge(scores_ready.sem, scores_ready.at(i))
                for c, (lo, hi) in enumerate(BANKS):
                    pe.wait_ge(state_ready.sem, state_ready.at(i - 1, c + 1))
                    for r in range(lo, hi):
                        at = (r - lo) * 2 * VW
                        nc.tensor.matmul(pc[c][:, at:at + 2 * VW], qkT[:, side, 0, r, :], state[:, r, :],
                                         start=True, stop=False, skip_group_check=True)
                        for j in range(2):
                            last = nc.tensor.matmul(pc[c][:, at + j * VW:at + (j + 1) * VW], scores[:, 2 * r + j, :],
                                                    v[:, side, 2 * r + j, :], start=False, stop=(j == 1),
                                                    skip_group_check=True)
                    last.then_inc(num_ready.sem, 1)
                pe.wait_ge(k_rows_ready.sem, k_rows_ready.at(i))
                for c, (lo, hi) in enumerate(BANKS):
                    pe.wait_ge(attn_ready.sem, attn_ready.at(i, c + 1))
                    for r in range(lo, hi):
                        at = (r - lo) * 2 * VW
                        last = nc.tensor.matmul(pc[c][:, at:at + 2 * VW], k_rows[:, r, :],
                                                v[:, side, 2 * r:2 * r + 2, :], start=True, stop=True)
                    last.then_inc(delta_ready.sem, 1)
                if more:
                    values(turn.next(), 0)
                pe.wait_ge(attn_ready.sem, attn_ready.at(i))
                for g in range(2):
                    pe.wait_ge(scores_ready.sem, scores_ready.at(i, 3 + g))
                    for r in range(GP):
                        at = 2 * (g * GP + r)
                        last = nc.tensor.transpose(pb[g][:, r * P:(r + 1) * P], attn[:, at:at + 2, :], ident)
                    last.then_inc(at_ready.sem, 1)
                if more:
                    values(turn.next(), 1)
                    pe.wait_ge(hT_ready.sem, hT_ready.at(turn.next().i))
                pe.wait_ge(attnT_ready.sem, attnT_ready.at(i))
                for r in range(PR):
                    last = nc.tensor.matmul(pt[:, 0:D], attnT[:, r, :], wo[:, r, :], start=(r == 0), stop=(r == PR - 1))
                last.then_inc(out_ready.sem, 1)

            transposes(Turn(0, 0))
            queries_keys(Turn(0, 0))
            values(Turn(0, 0), 0)
            values(Turn(0, 0), 1)
            trailing(pe, body)

def ffn_stage(nc, tag, glu, w, src, shift_src, add_src, out_flat, out_padded, norm_out, ident):
    ff = HID2 if glu else FF1
    widths = [min(P, ff - m) for m in range(0, ff, P)]
    MT = len(widths)
    wide = w["w1"].shape[1]
    with ExitStack() as ctx:
        s = Scope(nc, ctx, tag)
        w1 = s.sb("w1", [P, KD, wide])
        w2 = s.sb("w2", [P, MT, D])
        b1 = s.sb("b1", [P, 2 if glu else 1, MT])
        b2 = s.sb("b2", [P, D])
        gain = s.sb("gain", [P, KD])
        offset = s.sb("offset", [P, KD])
        minus_half, eps = s.sb("minus_half", [P, TB]), s.sb("eps", [P, TB])
        x = s.sb("x", [P, 2, TB, D])
        xs = s.sb("xs", [P, 2, TB, D]) if shift_src else x
        add = s.sb("add", [P, 2, TB, D]) if add_src is not None else None
        res = s.sb("res", [P, TB, D])
        sums = s.sb("sums", [P, TB, 6])
        mv = s.sb("mv", [P, TB, 2])
        rstd = s.sb("rstd", [P, TB])
        n = s.sb("n", [P, TB, D])
        hT = s.sb("hT", [P, KD, BLK])
        act = s.sb("act", [P, MT, BLK])
        gel = s.sb("gel", [P, 2, BLK]) if glu else None
        y = s.sb("y", [P, 2, TB, D])
        yn = s.sb("yn", [P, 2, TB, D]) if norm_out else None
        tp = [s.ps(f"tp{k}", [P, BLK]) for k in range(KD)]
        up = [s.ps(f"up{k}", [P, BLK]) for k in range(4)]
        dn = [s.ps(f"dn{k}", [P, BLK]) for k in range(2)]

        weights = s.sem("weights")
        consts = s.counter("consts")
        x_in = s.transfer("x_in", per=1 + 2 * shift_src + (add_src is not None))
        sums_ready, mv_ready = s.counter("sums_ready", per=2), s.counter("mv_ready")
        eps_added, rstd_ready = s.counter("eps_added"), s.counter("rstd_ready")
        n_ready = s.counter("n_ready")
        tp_ready = s.counter("tp_ready")
        hT_ready = s.counter("hT_ready", credit=1)
        up_ready = s.counter("up_ready", per=MT)
        gel_ready = s.counter("gel_ready", per=MT) if glu else None
        act_ready = s.counter("act_ready", per=MT, credit=1)
        dn_ready = s.counter("dn_ready", per=TB, credit=1)
        res_part, res_ready = s.counter("res_part"), s.counter("res_ready")
        y_ready = s.counter("y_ready", per=TB, credit=2)
        y_out = s.transfer("y_out", per=(out_flat is not None) + (out_padded is not None and not norm_out), credit=1)
        if norm_out:
            ysums_ready, ymv_ready = s.counter("ysums_ready", per=2), s.counter("ymv_ready")
            yeps_added, yrstd_ready = s.counter("yeps_added"), s.counter("yrstd_ready")
            yn_ready = s.counter("yn_ready")
            yn_out = s.transfer("yn_out", credit=1)
            ysums, ymv, yrstd = s.sb("ysums", [P, TB, 6]), s.sb("ymv", [P, TB, 2]), s.sb("yrstd", [P, TB])
        n_weights = 6 + 2 * (ff % P != 0) + 2 * glu
        block = ctx.enter_context(nc.Block())

        @block.sync
        def _(sp):
            full = ff // P * P

            def load(turn):
                if shift_src:
                    sp.dma_start(xs[:, turn.side, :, 0:D // 2], block_rows(src, turn)[:, :, 0:D // 2]).then_inc(x_in.sems[turn.side], 16)
                    sp.dma_start(xs[:, turn.side, :, D // 2:D],
                                         block_rows(src, turn, 1)[:, :, D // 2:D]).then_inc(x_in.sems[turn.side], 16)
                    sp.dma_start(x[:, turn.side, :, :], block_rows(src, turn)).then_inc(x_in.sems[turn.side], 16)
                else:
                    sp.dma_start(x[:, turn.side, :, :], flat_rows(src, turn)).then_inc(x_in.sems[turn.side], 16)
                if add_src is not None:
                    sp.dma_start(add[:, turn.side, :, :], flat_rows(add_src, turn)).then_inc(x_in.sems[turn.side], 16)

            load(Turn(0, 0))
            load(Turn(0, 1))
            sp.dma_start(w1[:, :, :], w["w1"].rearrange("(k p) n -> p k n", p=P)).then_inc(weights, 16)
            sp.dma_start(w2[:, 0:full // P, :], w["w2"][0:full, :].rearrange("(m p) n -> p m n", p=P))\
              .then_inc(weights, 16)
            if ff > full:
                sp.dma_start(w2[0:ff - full, MT - 1, :], w["w2"][full:ff, :]).then_inc(weights, 16)
            for g in range(1 + glu):
                part = w["b1"][g * ff:(g + 1) * ff]
                sp.dma_start(b1[:, g, 0:full // P], part[0:full].rearrange("(m p) -> p m", p=P),
                             allow_slow_non_contiguous=True).then_inc(weights, 16)
                if ff > full:
                    sp.dma_start(b1[0:ff - full, g, MT - 1:MT], part[full:ff].rearrange("(p a) -> p a", a=1))\
                      .then_inc(weights, 16)
            sp.dma_start(b2[:, :], w["b2"].partition_broadcast(P)).then_inc(weights, 16)
            for v, to in ((w["gain"], gain), (w["offset"], offset)):
                sp.dma_start(to[:, :], v.rearrange("(k p) -> p k", p=P),
                             allow_slow_non_contiguous=True).then_inc(weights, 16)

            def store(turn):
                sp.wait_ge(y_ready.sem, y_ready.at(turn.i))
                if out_flat is not None:
                    sp.dma_start(flat_rows(out_flat, turn), y[:, turn.side, :, :]).then_inc(y_out.sems[turn.side], 16)
                if out_padded is not None and not norm_out:
                    sp.dma_start(block_rows(out_padded, turn), y[:, turn.side, :, :]).then_inc(y_out.sems[turn.side], 16)
                if norm_out:
                    sp.wait_ge(yn_ready.sem, yn_ready.at(turn.i))
                    sp.dma_start(block_rows(out_padded, turn), yn[:, turn.side, :, :]).then_inc(yn_out.sems[turn.side], 16)

            with sp.Fori(0, NBLK // 2 - 1) as pair:
                for side in range(2):
                    sp.wait_ge(res_ready.sem, res_ready.at(Turn(pair, side).i))
                    sp.wait_ge(n_ready.sem, n_ready.at(Turn(pair, side).i))
                    load(Turn(pair + 1, side))
                    store(Turn(pair, side))
            for side in range(2):
                store(Turn(NBLK // 2 - 1, side))
            for side in range(2):
                sp.wait_ge(y_out.sems[side], y_out.total(NBLK // 2))
            if norm_out:
                for side in range(2):
                    sp.wait_ge(yn_out.sems[side], yn_out.total(NBLK // 2))

        @block.gpsimd
        def _(pool):
            nc.gpsimd.memset(minus_half[:, :], -0.5)
            nc.gpsimd.memset(eps[:, :], EPS).then_inc(consts.sem, 1)
            pool.wait_ge(consts.sem, consts.at(0))
            def front(turn):
                rstd_of(nc, pool, mv, rstd, eps, minus_half, TB, mv_ready, eps_added, rstd_ready, turn.i)

            def body(turn, more):
                if more:
                    front(turn.next())
                pool.wait_ge(x_in.sems[turn.side], x_in.at(turn))
                pool.wait_ge(y_ready.sem, y_ready.at(turn.i - 1))
                b2_all = b2[:, :].unsqueeze(1).to_broadcast([P, TB, D])
                first = nc.gpsimd.tensor_tensor(res[:, :, :], x[:, turn.side, :, :], b2_all, ALU.add)
                if add is None:
                    first.then_inc(res_ready.sem, 1)
                else:
                    first.then_inc(res_part.sem, 1)
                    pool.wait_ge(res_part.sem, res_part.at(turn.i))
                    nc.gpsimd.tensor_tensor(res[:, :, :], res[:, :, :], add[:, turn.side, :, :], ALU.add).then_inc(res_ready.sem, 1)
                if norm_out:
                    rstd_of(nc, pool, ymv, yrstd, eps, minus_half, TB, ymv_ready, yeps_added, yrstd_ready, turn.i)

            front(Turn(0, 0))
            pool.wait_ge(weights, 16 * n_weights)
            turns(pool, NBLK, body)

        @block.scalar
        def _(act_eng):
            if not glu:
                give_credit(act_eng, act_ready)
            act_eng.wait_ge(weights, 16 * n_weights)

            def body(turn, more):
                for m, width in enumerate(widths):
                    if glu:
                        act_eng.wait_ge(up_ready.sem, up_ready.at(turn.i, m + 1))
                        if m >= 2:
                            act_eng.wait_ge(act_ready.sem, act_ready.at(turn.i, m - 1))
                        else:
                            act_eng.wait_ge(act_ready.sem, act_ready.at(turn.i - 1, MT - 1 + m))
                        nc.scalar.activation(gel[0:width, m % 2, :], up[2 * (m % 2) + 1][0:width, :],
                                                          ACT.Gelu, bias=b1[0:width, 1, m:m + 1]).then_inc(gel_ready.sem, 1)
                    else:
                        act_eng.wait_ge(up_ready.sem, up_ready.at(turn.i, m + 1))
                        if m == 0:
                            act_eng.wait_ge(dn_ready.sem, dn_ready.at(turn.i - 1))
                        nc.scalar.activation(act[0:width, m, :], up[m % 4][0:width, :],
                                                          ACT.Gelu, bias=b1[0:width, 0, m:m + 1]).then_inc(act_ready.sem, 1)
            turns(act_eng, NBLK, body)

        @block.vector
        def _(dve):
            give_credit(dve, y_ready, hT_ready)
            if glu:
                give_credit(dve, act_ready)
            give_credit(dve, y_out)
            if norm_out:
                give_credit(dve, yn_out)

            def front(turn):
                dve.wait_ge(x_in.sems[turn.side], x_in.at(turn))
                stats_of(nc, dve, xs[:, turn.side, :, :], TB, sums, mv, sums_ready, mv_ready, turn.i)
                dve.wait_ge(rstd_ready.sem, rstd_ready.at(turn.i))
                normalise(nc, n, xs[:, turn.side, :, :], mv, rstd, TB).then_inc(n_ready.sem, 1)

            def hidden(turn):
                dve.wait_ge(tp_ready.sem, tp_ready.at(turn.i))
                for k in range(KD):
                    last = nc.vector.tensor_scalar(hT[:, k, :], tp[k][:, :], gain[:, k:k + 1], offset[:, k:k + 1],
                                                   ALU.mult, ALU.add)
                last.then_inc(hT_ready.sem, 1)

            def body(turn, more):
                if more:
                    front(turn.next())
                if glu:
                    for m, width in enumerate(widths):
                        dve.wait_ge(gel_ready.sem, gel_ready.at(turn.i, m + 1))
                        if m == 0:
                            dve.wait_ge(dn_ready.sem, dn_ready.at(turn.i - 1))
                        nc.vector.scalar_tensor_tensor(
                            act[0:width, m, :], up[2 * (m % 2)][0:width, :], b1[0:width, 0, m:m + 1],
                            gel[0:width, m % 2, :], ALU.add, ALU.mult).then_inc(act_ready.sem, 1)
                if more:
                    hidden(turn.next())
                dve.wait_ge(res_ready.sem, res_ready.at(turn.i))
                dve.wait_ge(y_out.sems[turn.side], y_out.at(turn, back=1))
                for t in range(TB):
                    dve.wait_ge(dn_ready.sem, dn_ready.at(turn.i, t + 1))
                    nc.vector.tensor_tensor(y[:, turn.side, t, :], res[:, t, :], dn[t % 2][:, 0:D], ALU.add).then_inc(y_ready.sem, 1)
                if norm_out:
                    dve.wait_ge(y_ready.sem, y_ready.at(turn.i))
                    stats_of(nc, dve, y[:, turn.side, :, :], TB, ysums, ymv, ysums_ready, ymv_ready, turn.i)
                    dve.wait_ge(yrstd_ready.sem, yrstd_ready.at(turn.i))
                    dve.wait_ge(yn_out.sems[turn.side], yn_out.at(turn, back=1))
                    normalise(nc, yn[:, turn.side, :, :], y[:, turn.side, :, :], ymv, yrstd, TB).then_inc(yn_ready.sem, 1)

            front(Turn(0, 0))
            dve.wait_ge(weights, 16 * n_weights)
            hidden(Turn(0, 0))
            turns(dve, NBLK, body)

        @block.tensor
        def _(pe):
            give_credit(pe, dn_ready)

            def transposes(turn):
                pe.wait_ge(n_ready.sem, n_ready.at(turn.i))
                pe.wait_ge(hT_ready.sem, hT_ready.at(turn.i - 1))
                for k in range(KD):
                    for t in range(TB):
                        last = nc.tensor.transpose(tp[k][:, t * P:(t + 1) * P], n[:, t, k * P:(k + 1) * P], ident)
                last.then_inc(tp_ready.sem, 1)

            def body(turn, more):
                pe.wait_ge(hT_ready.sem, hT_ready.at(turn.i))
                for m, width in enumerate(widths):
                    depth = 2 if glu else 4
                    if m >= depth:
                        pe.wait_ge(act_ready.sem, act_ready.at(turn.i, m - depth + 1))
                    else:
                        pe.wait_ge(act_ready.sem, act_ready.at(turn.i - 1, MT - depth + 1 + m))
                    for g in range(1 + glu):
                        bank = up[2 * (m % 2) + g] if glu else up[m % 4]
                        for k in range(KD):
                            last = nc.tensor.matmul(bank[0:width, :], w1[:, k, g * ff + m * P:g * ff + m * P + width],
                                                    hT[:, k, :], start=(k == 0), stop=(k == KD - 1))
                    last.then_inc(up_ready.sem, 1)
                if more:
                    transposes(turn.next())
                pe.wait_ge(act_ready.sem, act_ready.at(turn.i))
                for t in range(TB):
                    if t >= 2:
                        pe.wait_ge(y_ready.sem, y_ready.at(turn.i, t - 1))
                    else:
                        pe.wait_ge(y_ready.sem, y_ready.at(turn.i - 1, TB - 1 + t))
                    for m, width in enumerate(widths):
                        last = nc.tensor.matmul(dn[t % 2][:, 0:D], act[0:width, m, t * P:(t + 1) * P],
                                                w2[0:width, m, :], start=(m == 0), stop=(m == MT - 1))
                    last.then_inc(dn_ready.sem, 1)

            pe.wait_ge(weights, 16 * n_weights)
            transposes(Turn(0, 0))
            turns(pe, NBLK, body)

def window_attention_stage(nc, tag, w, src, dst, ident):
    PR = H2 // 2
    with ExitStack() as ctx:
        s = Scope(nc, ctx, tag)
        wqkv = s.sb("wqkv", [P, KD, 3 * INNER])
        wo = s.sb("wo", [P, PR, D])
        scales = s.sb("scales", [P, 4 * DH])
        ident16 = s.sb("ident16", [P, P], BF16)
        mask_even = s.sb("mask_even", [P, NT // 2, 2 * P], BF16)
        mask_odd = s.sb("mask_odd", [P, 2 * P], BF16)
        minus_half = s.sb("minus_half", [P, H2])
        x, xs = s.sb("x", [P, 2, D]), s.sb("xs", [P, 2, D])
        raw, table = s.sb("raw", [P, 2, 4 * DH]), s.sb("table", [P, 2, 4 * DH])
        hT = s.sb("hT", [P, KD, P])
        squares = s.sb("squares", [P, 2, INNER])
        ss, rn = s.sb("ss", [P, 2, H2]), s.sb("rn", [P, 2, 2, H2])
        straight, turned = s.sb("straight", [P, 2, INNER]), s.sb("turned", [P, 2, INNER])
        rotated = s.sb("rotated", [P, 2, INNER])
        k_unit = s.sb("k_unit", [P, INNER])
        qT = s.sb("qT", [P, PR, P])
        kT = s.sb("kT", [P, PR, 2, P])
        v = s.sb("v", [P, 2, H2, DH])
        highest, nbias = s.sb("highest", [P, 2, 2, 2]), s.sb("nbias", [P, 2, 2, 2])
        probs = s.sb("probs", [P, H2, 2 * P])
        den, rden = s.sb("den", [P, H2]), s.sb("rden", [P, H2])
        probsT = s.sb("probsT", [P, H2, 2, P])
        o = s.sb("o", [P, H2, DH])
        oT = s.sb("oT", [P, PR, P])
        y = s.sb("y", [P, 2, D])
        pa = [s.ps(f"pa{k}", [P, 512]) for k in range(2)]
        sc = [s.ps(f"sc{k}", [P, 2, 2 * P]) for k in range(2)]
        pp = [s.ps(f"pp{k}", [P, 512]) for k in range(2)]
        po = s.ps("po", [P, 512])
        pt = s.ps("pt", [P, 512])

        weights, consts = s.sem("weights"), s.counter("consts")
        x_in, res_in = s.transfer("x_in", per=3), s.transfer("res_in")
        table_ready = s.counter("table_ready")
        tp_ready, hT_ready = s.counter("tp_ready"), s.counter("hT_ready", credit=1)
        proj_ready, sq_ready = s.counter("proj_ready", per=3), s.counter("sq_ready", per=2, credit=1)
        ss_steps, rn_ready = s.counter("ss_steps", per=4, credit=1), s.counter("rn_ready", per=2, credit=1)
        rot_ready, sum_ready = s.counter("rot_ready", per=2, credit=1), s.counter("sum_ready", per=2, credit=1)
        k_unit_ready = s.counter("k_unit_ready")
        v_ready = s.counter("v_ready", credit=1)
        qkt_ready = s.counter("qkt_ready", per=2, credit=1)
        qT_ready, kT_ready = s.counter("qT_ready"), s.counter("kT_ready")
        st_ready, max_ready, nb_ready = s.counter("st_ready", per=4), s.counter("max_ready", per=4), s.counter("nb_ready", per=2)
        exp_ready = s.counter("exp_ready", per=8, credit=1)
        pt_ready = s.counter("pt_ready", per=4)
        p_even, p_odd = s.counter("p_even", per=2), s.counter("p_odd", per=2)
        o_made, rden_ready, o_ready = s.counter("o_made"), s.counter("rden_ready"), s.counter("o_ready", credit=1)
        ot_made, oT_ready = s.counter("ot_made"), s.counter("oT_ready", credit=1)
        out_ready, y_ready = s.counter("out_ready"), s.counter("y_ready", credit=3)
        y_out = s.transfer("y_out", credit=1)
        block = ctx.enter_context(nc.Block())

        @block.sync
        def _(sp):
            def row(turn):
                at = turn.i * P + turn.pair // (NT // 2 // B)
                return at if isinstance(at, int) else sp.snap(at)

            def load(turn):
                at = row(turn)
                return [(xs[:, turn.side, 0:D // 2], src[bass.ds(at + 1, P), 0:D // 2]),
                        (xs[:, turn.side, D // 2:D], src[bass.ds(at, P), D // 2:D]),
                        (raw[:, turn.side, :], w["tables"][bass.ds(turn.i * P, P), :])]

            def start(turn, copies):
                for to, frm in copies:
                    sp.dma_start(to, frm).then_inc(x_in.sems[turn.side], 16)

            def start_residual(turn):
                sp.dma_start(x[:, turn.side, :], src[bass.ds(row(turn) + 1, P), :]).then_inc(res_in.sems[turn.side], 16)

            def store(turn):
                sp.dma_start(dst[bass.ds(row(turn) + 1, P), :], y[:, turn.side, :]).then_inc(y_out.sems[turn.side], 16)

            for first in (Turn(0, 0), Turn(0, 1)):
                start(first, load(first))
                start_residual(first)
            sp.dma_start(wqkv[:, :, :], w["wqkv"].rearrange("(k p) n -> p k n", p=P)).then_inc(weights, 16)
            sp.dma_start(wo[:, :, :], w["wo"].rearrange("(r p) n -> p r n", p=P)).then_inc(weights, 16)
            for at, vec in ((0, "q_scale"), (1, "k_scale")):
                sp.dma_start(scales[:, at * DH:(at + 1) * DH], w[vec].partition_broadcast(P)).then_inc(weights, 16)
                for j in range(2):
                    to = (2 + at) * DH + j * (DH // 2)
                    sp.dma_start(scales[:, to:to + DH // 2],
                                 w[vec][(1 - j) * (DH // 2):(2 - j) * (DH // 2)].partition_broadcast(P))\
                      .then_inc(weights, 16)
            sp.dma_start(ident16[:, :], w["ident16"]).then_inc(weights, 16)
            sp.dma_start(mask_even[:, :, :], w["mask_even"].rearrange("p (a n) -> p a n", n=2 * P)).then_inc(weights, 16)
            sp.dma_start(mask_odd[:, :], w["mask_odd"]).then_inc(weights, 16)

            def body(turn, before, more, more2):
                if more2:
                    sp.wait_ge(tp_ready.sem, tp_ready.at(turn.i))
                    sp.wait_ge(table_ready.sem, table_ready.at(turn.i))
                    start(Turn(turn.pair + 1, turn.side), load(Turn(turn.pair + 1, turn.side)))
                if before:
                    sp.wait_ge(y_ready.sem, y_ready.at(turn.i - 1))
                    store(turn.before())
                    if more:
                        start_residual(turn.next())

            trailing(sp, body)
            sp.wait_ge(y_ready.sem, y_ready.at(NT - 1))
            store(Turn(NT // 2 - 1, 1))
            for side in range(2):
                sp.wait_ge(y_out.sems[side], y_out.total(NT // 2))

        @block.gpsimd
        def _(pool):
            give_credit(pool, sum_ready, rn_ready)
            nc.gpsimd.memset(kT[:, :, :, :], 0.0)
            nc.gpsimd.memset(v[:, :, :, :], 0.0)
            nc.gpsimd.memset(minus_half[:, :], -0.5).then_inc(consts.sem, 1)
            pool.wait_ge(consts.sem, consts.at(0))

            def front(turn):
                pool.wait_ge(x_in.sems[turn.side], x_in.at(turn))
                nc.gpsimd.tensor_tensor(table[:, turn.side, :], raw[:, turn.side, :], scales[:, :],
                                                       ALU.mult).then_inc(table_ready.sem, 1)

            def rotation(turn):
                for j in range(2):
                    pool.wait_ge(rot_ready.sem, rot_ready.at(turn.i, j + 1))
                    pool.wait_ge(qkt_ready.sem, qkt_ready.at(turn.i - 1, j + 1))
                    nc.gpsimd.tensor_tensor(rotated[:, j, :], straight[:, j, :], turned[:, j, :], ALU.add).then_inc(sum_ready.sem, 1)
                    pool.wait_ge(ss_steps.sem, ss_steps.at(turn.i, 2 * j + 2))
                    nc.gpsimd.tensor_tensor(rn[:, turn.side, j, :], ss[:, j, :], minus_half[:, :], ALU.pow).then_inc(rn_ready.sem, 1)

            def body(turn, before, more, more2):
                if more:
                    rotation(turn.next())
                if more2:
                    front(Turn(turn.pair + 1, turn.side))

            pool.wait_ge(weights, 16 * 11)
            front(Turn(0, 0))
            rotation(Turn(0, 0))
            front(Turn(0, 1))
            trailing(pool, body)

        @block.scalar
        def _(act):
            give_credit(act, hT_ready, sq_ready, v_ready, exp_ready, oT_ready)
            act.wait_ge(consts.sem, consts.at(0))

            def hidden(turn):
                act.wait_ge(tp_ready.sem, tp_ready.at(turn.i))
                nc.scalar.activation(hT[:, :, :], pt[:, 0:KD * P].rearrange("p (k t) -> p k t", t=P), ACT.Copy).then_inc(hT_ready.sem, 1)

            def square(turn, j):
                act.wait_ge(proj_ready.sem, proj_ready.at(turn.i, j + 1))
                act.wait_ge(ss_steps.sem, ss_steps.at(turn.i - 1, 2 * j + 1))
                nc.scalar.activation(squares[:, j, :], pa[j][:, :], ACT.Square).then_inc(sq_ready.sem, 1)

            def queries(turn):
                act.wait_ge(qkt_ready.sem, qkt_ready.at(turn.i, 1))
                nc.scalar.activation(qT[:, :, :], pp[0][:, :].rearrange("p (r t) -> p r t", t=P), ACT.Copy).then_inc(qT_ready.sem, 1)

            def values(turn):
                act.wait_ge(proj_ready.sem, proj_ready.at(turn.i, 3))
                nc.scalar.activation(v[:, turn.side, :, :], pa[0][:, :].rearrange("p (h d) -> p h d", d=DH),
                                                ACT.Copy).then_inc(v_ready.sem, 1)

            def exps(turn, g, j):
                act.wait_ge(nb_ready.sem, nb_ready.at(turn.i, g + 1))
                for r in range(2):
                    head = 4 * g + 2 * r + j
                    nc.scalar.activation(
                        probs[:, head, :], sc[j][:, r, :], ACT.Exp, bias=nbias[:, g, j, r:r + 1],
                        scale=rn[:, turn.side, 0, head:head + 1], accum_out=den[:, head:head + 1]).then_inc(exp_ready.sem, 1)

            def columns(turn, g):
                act.wait_ge(pt_ready.sem, pt_ready.at(turn.i, 2 * g + 1))
                nc.scalar.activation(probsT[:, 4 * g:4 * g + 4:2, :, :],
                                               pp[0][:, :].rearrange("p (r s t) -> p r s t", r=2, t=P), ACT.Copy).then_inc(p_even.sem, 1)

            def output_columns(turn):
                act.wait_ge(ot_made.sem, ot_made.at(turn.i))
                nc.scalar.activation(oT[:, :, :], pp[0][:, :].rearrange("p (r t) -> p r t", t=P), ACT.Copy).then_inc(oT_ready.sem, 1)

            def body(turn, before, more, more2):
                if more:
                    hidden(turn.next())
                if before:
                    act.wait_ge(o_made.sem, o_made.at(turn.i - 1))
                    values(turn)
                    output_columns(turn.before())
                exps(turn, 0, 0)
                if more:
                    square(turn.next(), 0)
                exps(turn, 0, 1)
                if more:
                    square(turn.next(), 1)
                exps(turn, 1, 0)
                exps(turn, 1, 1)
                columns(turn, 0)
                columns(turn, 1)
                if more:
                    queries(turn.next())

            first = Turn(0, 0)
            hidden(first)
            square(first, 0)
            square(first, 1)
            queries(first)
            values(first)
            trailing(act, body)
            output_columns(Turn(NT // 2 - 1, 1))

        @block.vector
        def _(dve):
            give_credit(dve, ss_steps, rot_ready, o_ready, y_ready, y_out)
            dve.wait_ge(consts.sem, consts.at(0))

            def rotate(turn, j):
                dve.wait_ge(sq_ready.sem, sq_ready.at(turn.i, j + 1))
                dve.wait_ge(table_ready.sem, table_ready.at(turn.i))
                dve.wait_ge(sum_ready.sem, sum_ready.at(turn.i - 1, j + 1))
                half = DH // 2

                def of_table(at, width):
                    return table[:, turn.side, at:at + width].unsqueeze(1).to_broadcast([P, H2, width])

                def heads(a):
                    return a.rearrange("p (h d) -> p h d", d=DH)

                nc.vector.tensor_tensor(heads(straight[:, j, :]), heads(pa[j][:, :]), of_table(j * DH, DH), ALU.mult)
                for a in range(2):
                    last = nc.vector.tensor_tensor(heads(turned[:, j, :])[:, :, a * half:(a + 1) * half],
                                                   heads(pa[j][:, :])[:, :, (1 - a) * half:(2 - a) * half],
                                                   of_table((2 + j) * DH + a * half, half), ALU.mult)
                last.then_inc(rot_ready.sem, 1)
                if j == 0:
                    dve.wait_ge(rn_ready.sem, rn_ready.at(turn.i - 1))
                nc.vector.tensor_reduce(ss[:, j, :], heads(squares[:, j, :]), AX.X, ALU.add).then_inc(ss_steps.sem, 1)
                dve.wait_ge(ss_steps.sem, ss_steps.at(turn.i, 2 * j + 1))
                nc.vector.tensor_scalar(ss[:, j, :], ss[:, j, :], 1e-24, None, ALU.max).then_inc(ss_steps.sem, 1)

            def unit_keys(turn):
                dve.wait_ge(rn_ready.sem, rn_ready.at(turn.i))
                dve.wait_ge(sum_ready.sem, sum_ready.at(turn.i))
                nc.vector.tensor_tensor(
                    k_unit[:, :].rearrange("p (h d) -> p h d", d=DH),
                    rotated[:, 1, :].rearrange("p (h d) -> p h d", d=DH),
                    rn[:, turn.side, 1, :].unsqueeze(2).to_broadcast([P, H2, DH]), ALU.mult).then_inc(k_unit_ready.sem, 1)

            def maxima(turn, g):
                for j in range(2):
                    dve.wait_ge(st_ready.sem, st_ready.at(turn.i, 2 * g + j + 1))
                    nc.vector.tensor_reduce(highest[:, g, j, :], sc[j][:, :, :], AX.X, ALU.max).then_inc(max_ready.sem, 1)
                dve.wait_ge(rn_ready.sem, rn_ready.at(turn.i))
                dve.wait_ge(max_ready.sem, max_ready.at(turn.i, 2 * g + 2))
                nc.vector.scalar_tensor_tensor(
                    nbias[:, g, :, :], highest[:, g, :, :], -1.0,
                    rn[:, turn.side, 0, 4 * g:4 * g + 4].rearrange("p (r j) -> p j r", j=2), ALU.mult, ALU.mult).then_inc(nb_ready.sem, 1)

            def columns(turn, g):
                dve.wait_ge(pt_ready.sem, pt_ready.at(turn.i, 2 * g + 2))
                nc.vector.tensor_copy(probsT[:, 4 * g + 1:4 * g + 4:2, :, :],
                                               pp[1][:, :].rearrange("p (r s t) -> p r s t", r=2, t=P)).then_inc(p_odd.sem, 1)

            def keys(turn):
                dve.wait_ge(qkt_ready.sem, qkt_ready.at(turn.i, 2))
                nc.vector.tensor_copy(kT[:, :, turn.side, :], pp[1][:, :].rearrange("p (r t) -> p r t", t=P)).then_inc(kT_ready.sem, 1)

            def output(turn):
                dve.wait_ge(rden_ready.sem, rden_ready.at(turn.i))
                dve.wait_ge(o_made.sem, o_made.at(turn.i))
                nc.vector.tensor_tensor(o[:, :, :], po[:, :].rearrange("p (h d) -> p h d", d=DH),
                                        rden[:, :].unsqueeze(2).to_broadcast([P, H2, DH]), ALU.mult).then_inc(o_ready.sem, 1)

            def residual(turn):
                dve.wait_ge(out_ready.sem, out_ready.at(turn.i))
                dve.wait_ge(res_in.sems[turn.side], res_in.at(turn))
                dve.wait_ge(y_out.sems[turn.side], y_out.at(turn, back=1))
                nc.vector.tensor_tensor(y[:, turn.side, :], x[:, turn.side, :], pt[:, 0:D], ALU.add).then_inc(y_ready.sem, 1)

            def body(turn, before, more, more2):
                i = turn.i
                if before:
                    output(turn.before())
                maxima(turn, 0)
                if more:
                    rotate(turn.next(), 0)
                maxima(turn, 1)
                if more:
                    rotate(turn.next(), 1)
                columns(turn, 0)
                if before:
                    residual(turn.before())
                if more:
                    unit_keys(turn.next())
                columns(turn, 1)
                dve.wait_ge(exp_ready.sem, exp_ready.at(i))
                nc.vector.reciprocal(rden[:, :], den[:, :]).then_inc(rden_ready.sem, 1)
                if more:
                    keys(turn.next())

            first = Turn(0, 0)
            rotate(first, 0)
            rotate(first, 1)
            unit_keys(first)
            keys(first)
            trailing(dve, body)
            output(Turn(NT // 2 - 1, 1))
            residual(Turn(NT // 2 - 1, 1))

        @block.tensor
        def _(pe):
            give_credit(pe, qkt_ready)
            pe.wait_ge(weights, 16 * 11)
            pe.wait_ge(consts.sem, consts.at(0))

            def transposes(turn):
                pe.wait_ge(x_in.sems[turn.side], x_in.at(turn))
                pe.wait_ge(hT_ready.sem, hT_ready.at(turn.i - 1))
                pe.wait_ge(y_ready.sem, y_ready.at(turn.i - 3))
                for k in range(KD):
                    last = nc.tensor.transpose(pt[:, k * P:(k + 1) * P], xs[:, turn.side, k * P:(k + 1) * P], ident)
                last.then_inc(tp_ready.sem, 1)

            def project(turn, g):
                bank = pa[g % 2]
                pe.wait_ge(hT_ready.sem, hT_ready.at(turn.i))
                if g == 0:
                    pe.wait_ge(v_ready.sem, v_ready.at(turn.i - 1))
                elif g == 1:
                    pe.wait_ge(rot_ready.sem, rot_ready.at(turn.i - 1, 2))
                    pe.wait_ge(sq_ready.sem, sq_ready.at(turn.i - 1, 2))
                else:
                    pe.wait_ge(rot_ready.sem, rot_ready.at(turn.i, 1))
                    pe.wait_ge(sq_ready.sem, sq_ready.at(turn.i, 1))
                for k in range(KD):
                    last = nc.tensor.matmul(bank[:, :], hT[:, k, :], wqkv[:, k, g * INNER:(g + 1) * INNER],
                                            start=(k == 0), stop=(k == KD - 1))
                last.then_inc(proj_ready.sem, 1)

            def scores(turn, g):
                i = turn.i
                if g == 0:
                    pe.wait_ge(qT_ready.sem, qT_ready.at(i))
                    pe.wait_ge(kT_ready.sem, kT_ready.at(i))
                for j in range(2):
                    if g == 0:
                        pe.wait_ge(exp_ready.sem, exp_ready.at(i - 1, 6 + 2 * j))
                    else:
                        pe.wait_ge(exp_ready.sem, exp_ready.at(i, 2 + 2 * j))
                mask = mask_odd[:, :] if turn.side else mask_even[:, bass.ds(turn.pair, 1), :].squeeze(1)
                for r in range(2):
                    for j in range(2):
                        nc.tensor.matmul(sc[j][:, r, :], ident16[:, :], mask, start=True, stop=False,
                                         skip_group_check=True)
                    for j in range(2):
                        half = slice(j * DH, (j + 1) * DH)
                        ins = nc.tensor.matmul(sc[j][:, r, :], qT[half, 2 * g + r, :], kT[half, 2 * g + r, :, :],
                                               start=False, stop=True, skip_group_check=True)
                        if r == 1:
                            ins.then_inc(st_ready.sem, 1)

            def columns(turn, g):
                i = turn.i
                for j in range(2):
                    pe.wait_ge(exp_ready.sem, exp_ready.at(i, 4 * g + 2 * j + 2))
                    if g:
                        read = p_odd if j else p_even
                        pe.wait_ge(read.sem, read.at(i, 1))
                    elif j:
                        pe.wait_ge(kT_ready.sem, kT_ready.at(i))
                    else:
                        pe.wait_ge(oT_ready.sem, oT_ready.at(i - 1))
                    for r in range(2):
                        for sd in range(2):
                            at = (2 * r + sd) * P
                            last = nc.tensor.transpose(pp[j][:, at:at + P],
                                                       probs[:, 4 * g + 2 * r + j, sd * P:(sd + 1) * P], ident)
                    last.then_inc(pt_ready.sem, 1)

            def heads_to_rows(turn, previous):
                pe.wait_ge(sum_ready.sem, sum_ready.at(turn.i, 1))
                if previous is not None:
                    pe.wait_ge(p_even.sem, p_even.at(previous.i))
                for r in range(PR):
                    last = nc.tensor.transpose(pp[0][:, r * P:(r + 1) * P], rotated[:, 0, r * P:(r + 1) * P], ident)
                last.then_inc(qkt_ready.sem, 1)
                pe.wait_ge(k_unit_ready.sem, k_unit_ready.at(turn.i))
                if previous is not None:
                    pe.wait_ge(p_odd.sem, p_odd.at(previous.i))
                for r in range(PR):
                    last = nc.tensor.transpose(pp[1][:, r * P:(r + 1) * P], k_unit[:, r * P:(r + 1) * P], ident)
                last.then_inc(qkt_ready.sem, 1)

            def weighted(turn, g):
                i = turn.i
                pe.wait_ge(p_even.sem, p_even.at(i, g + 1))
                pe.wait_ge(p_odd.sem, p_odd.at(i, g + 1))
                if g == 0:
                    pe.wait_ge(v_ready.sem, v_ready.at(i))
                    pe.wait_ge(o_ready.sem, o_ready.at(i - 1))
                for head in range(4 * g, 4 * g + 4):
                    for sd in range(2):
                        last = nc.tensor.matmul(po[:, head * DH:(head + 1) * DH], probsT[:, head, sd, :],
                                                v[:, sd, head, :], start=(sd == 0), stop=(sd == 1))
                if g:
                    last.then_inc(o_made.sem, 1)

            def output_columns(turn, last_reader):
                pe.wait_ge(o_ready.sem, o_ready.at(turn.i))
                pe.wait_ge(last_reader.sem, last_reader.at(turn.i + 1 if last_reader is qT_ready else turn.i))
                for r in range(PR):
                    last = nc.tensor.transpose(pp[0][:, r * P:(r + 1) * P], o[:, 2 * r:2 * r + 2, :], ident)
                last.then_inc(ot_made.sem, 1)

            def output(turn, hidden):
                pe.wait_ge(oT_ready.sem, oT_ready.at(turn.i))
                pe.wait_ge(y_ready.sem, y_ready.at(turn.i - 1))
                if hidden is not None:
                    pe.wait_ge(hT_ready.sem, hT_ready.at(hidden.i))
                for r in range(PR):
                    last = nc.tensor.matmul(pt[:, 0:D], oT[:, r, :], wo[:, r, :], start=(r == 0), stop=(r == PR - 1))
                last.then_inc(out_ready.sem, 1)

            def body(turn, before, more, more2):
                if more:
                    transposes(turn.next())
                scores(turn, 0)
                if before:
                    output_columns(turn.before(), qT_ready)
                if more:
                    project(turn.next(), 0)
                    project(turn.next(), 1)
                scores(turn, 1)
                if before:
                    output(turn.before(), turn.next() if more else None)
                columns(turn, 0)
                if more:
                    project(turn.next(), 2)
                columns(turn, 1)
                weighted(turn, 0)
                if more:
                    heads_to_rows(turn.next(), turn)
                weighted(turn, 1)

            first = Turn(0, 0)
            transposes(first)
            project(first, 0)
            project(first, 1)
            project(first, 2)
            heads_to_rows(first, None)
            trailing(pe, body)
            output_columns(Turn(NT // 2 - 1, 1), p_even)
            output(Turn(NT // 2 - 1, 1), None)

def rotary_tables():
    f = np.float32
    half = np.arange(0, DH, 2, dtype=f)
    inv = (f(1.0) / np.power(f(10000.0), half / f(DH))).astype(f)
    t = np.arange(L, dtype=f)
    freqs = t[:, None] * inv[None, :]
    base = (half + f(0.4 * DH)) / f(1.4 * DH)
    power = (t - f(L // 2)) / f(64.0)
    scale = np.power(base[None, :], power[:, None]).astype(f)
    cos, sin = np.cos(freqs).astype(f), np.sin(freqs).astype(f)
    parts = [cos * scale * f(8), cos / scale, sin * scale * f(8), sin / scale]
    full = [np.concatenate([-a if n >= 2 else a, a], axis=1) for n, a in enumerate(parts)]
    return np.tile(np.concatenate(full, axis=1).astype(f), (B, 1))

def window_masks(bf16):
    t, j = np.arange(P)[:, None], np.arange(P)[None, :]
    own, before = np.where(j <= t, 0.0, MASKED), np.where(j >= t, 0.0, MASKED)
    none = np.full((P, P), MASKED)
    even = [np.concatenate([own, none if a % (L // P // 2) == 0 else before], axis=1) for a in range(NT // 2)]
    odd = np.concatenate([before, own], axis=1)
    return np.concatenate(even, axis=1).astype(bf16), odd.astype(bf16)

def pick_rows(bf16):
    rows = 2 * NS
    return np.concatenate([np.repeat(np.tile(np.eye(rows)[:, r:r + 1], (3, 1)), P, axis=1) for r in range(rows)],
                          axis=1).astype(bf16)

def zero_rows(nc, streams):
    with nc.sbuf_tensor("zero", [B, D], FP32) as zero, nc.semaphore("zero_made") as made, \
            nc.semaphore("zero_sent") as sent, nc.Block() as block:

        @block.gpsimd
        def _(pool):
            nc.gpsimd.memset(zero[:, :], 0.0).then_inc(made, 1)

        @block.sync
        def _(sp):
            sp.wait_ge(made, 1)
            for stream in streams:
                sp.dma_start(stream.rearrange("(b r) d -> b r d", r=LP)[:, 0, :], zero[:, :]).then_inc(sent, 16)
            sp.wait_ge(sent, 16 * len(streams))

def program(nc, a, out):
    def scratch(name, rows):
        return nc.dram_tensor(name, (rows, D), FP32).ap()

    x1, x2, xa, x3 = (scratch(n, T) for n in ("x1", "x2", "xa", "x3"))
    h3, a0, f0, a1 = (scratch(n, B * LP) for n in ("h3", "a0", "f0", "a1"))
    zero_rows(nc, (h3, a0, f0, a1))
    with nc.sbuf_tensor("ident", [P, P], FP32) as ident_sb:
        with nc.semaphore("ident_in") as ident_in, nc.Block() as block:
            @block.sync
            def _(sp):
                sp.dma_start(ident_sb[:, :], a["ident"]).then_inc(ident_in, 16)
                sp.wait_ge(ident_in, 16)
        ident = ident_sb[:, :]
        ssm = {k: a["L0_attn_" + v] for k, v in dict(
            w_in="W_in", w_x="W_xproj", w_dt="W_dt", w_out="W_out", conv_w="conv_w", conv_b="conv_b", b_dt="b_dt",
            skip="D", a_log="A_log").items()}
        state_space_stage(nc, "ssm", dict(ssm, pick=a["pick"]), a["L0_attn_x"], x1, ident)
        moe_stage(nc, "moe", dict(router=a["L0_ffn_router_w"], router_b=a["L0_ffn_router_b"], rank=a["rank"],
                                  experts=a["L0_ffn_expert_w"], expert_b=a["L0_ffn_expert_b"]), x1, x2, ident)
        lin = {k: a["L1_attn_" + v] for k, v in dict(
            wqT="wq", wkT="wk", wv="wv", wo="wo", proj="proj", gain="g1", offset="beta1").items()}
        linear_attention_stage(nc, "lin", dict(lin, causal=a["causal"], keep=a["keep"]), x2, xa, ident)
        mlp = {k: a["L1_attn_" + v] for k, v in dict(w1="w1", b1="b1", w2="w2", b2="b2", gain="g2", offset="beta2").items()}
        ffn_stage(nc, "mlp", False, mlp, xa, False, x2, x3, h3, True, ident)
        for layer, (src, mid, dst) in enumerate(((h3, a0, f0), (f0, a1, None))):
            win = {k: a["L1_ffn_" + k][layer] for k in ("wqkv", "wo", "q_scale", "k_scale")}
            win.update({k: a[k] for k in ("tables", "ident16", "mask_even", "mask_odd")})
            window_attention_stage(nc, f"win{layer}", win, src, mid, ident)
            glu = {k: a["L1_ffn_" + v][layer] for k, v in dict(
                w1="w1", b1="b1", w2="w2", b2="b2", gain="ln_g", offset="ln_b").items()}
            last = dst is None
            ffn_stage(nc, f"glu{layer}", True, glu, mid, True, x3 if last else None, out if last else None, dst,
                      False, ident)

def laid_out(inputs):
    a = {k: np.asarray(v) for k, v in inputs.items()}
    a["L0_attn_x"] = a["L0_attn_x"].reshape(T, D)
    a["L0_attn_conv_w"] = a["L0_attn_conv_w"].reshape(HID, 3)
    for k in ("L0_attn_W_in", "L0_attn_W_xproj", "L0_attn_W_dt", "L0_attn_W_out", "L0_ffn_router_w",
              "L1_attn_wq", "L1_attn_wk"):
        a[k] = a[k].T
    a["L0_ffn_expert_w"] = a["L0_ffn_expert_w"].transpose(2, 0, 1).reshape(D, E * D)
    bf16 = np.dtype("bfloat16")
    keep = np.ones((NT, P, 1), np.float32)
    keep[L // P - 1::L // P] = 0
    even, odd = window_masks(bf16)
    a.update(ident=np.eye(P, dtype=np.float32), ident16=np.eye(P).astype(bf16), pick=pick_rows(bf16),
             rank=np.arange(E, 0, -1).astype(np.float32), causal=np.triu(np.ones((P, P), np.float32)),
             keep=keep.reshape(T, 1), tables=rotary_tables(), mask_even=even, mask_odd=odd)
    return {k: np.ascontiguousarray(v) for k, v in a.items()}

def kernel(**inputs):
    import concourse.bacc as bacc
    from concourse.bass_utils import run_bass_kernel_spmd

    nc = bacc.Bacc("TRN2", target_bir_lowering=False, num_devices=1)
    arrays = {f"in_{k}": v for k, v in laid_out(inputs).items()}
    aps = {k[3:]: nc.dram_tensor(k, v.shape, mybir.dt.from_np(v.dtype), kind="ExternalInput").ap()
           for k, v in arrays.items()}
    out = nc.dram_tensor("out", (T, D), FP32, kind="ExternalOutput").ap()
    program(nc, aps, out)
    r = run_bass_kernel_spmd(nc, [arrays], core_ids=[0])
    return r.results[0]["out"].reshape(B, L, D)
```

```python
import concourse.bass as bass
from concourse import mybir
from contextlib import ExitStack
import numpy as np

FP32 = mybir.dt.float32
BF16 = mybir.dt.bfloat16
ALU = mybir.AluOpType
ACT = mybir.ActivationFunctionType
AX = mybir.AxisListType

P = 128
B, L, D = 4, 1024, 256
T = B * L
KD = D // P
BLK = 512
TB = BLK // P
NBLK = T // BLK
NT = T // P
LP = L + 1
EPS = 1e-5

HID, NS, RANK = 512, 16, 64
CT = HID // P
E = 8
H1, DH = 16, 64
FF1 = 1024
H2 = 8
INNER = H2 * DH
HID2 = int(D * 4 * 2 / 3)
MASKED = -1e30

class Turn:

    def __init__(self, pair, side):
        self.pair, self.side = pair, side
        self.i = pair * 2 + side

    def next(self):
        return Turn(self.pair, 1) if self.side == 0 else Turn(self.pair + 1, 0)

    def before(self):
        return Turn(self.pair, 0) if self.side else Turn(self.pair - 1, 1)

def turns(eng, n, body):
    with eng.Fori(0, n // 2 - 1) as pair:
        body(Turn(pair, 0), True)
        body(Turn(pair, 1), True)
    body(Turn(n // 2 - 1, 0), True)
    body(Turn(n // 2 - 1, 1), False)

class Counter:

    def __init__(self, sem, per=1, credit=0):
        self.sem, self.per, self.credit = sem, per, credit * per

    def at(self, i, k=None):
        return i * self.per + (self.credit + (self.per if k is None else k))

class Transfers:

    def __init__(self, sems, per=1, credit=0):
        self.sems, self.per, self.credit = sems, 16 * per, 16 * per * credit

    def at(self, turn, back=0):
        return turn.pair * self.per + (self.credit + self.per * (1 - back))

    def total(self, pairs):
        return self.credit + self.per * pairs

def give_credit(eng, *counts):
    for c in counts:
        for sem in (c.sems if isinstance(c, Transfers) else [c.sem]):
            eng.sem_inc(sem, c.credit)

class Scope:

    def __init__(self, nc, ctx, tag):
        self.nc, self.ctx, self.tag, self.sems = nc, ctx, tag, []
        ctx.callback(self.end)

    def end(self):
        self.nc.clear_and_free_semaphores(self.sems)
        self.nc.all_engine_barrier()

    def adopt(self, weights):
        self.sems.append(weights.loaded)

    def sb(self, name, shape, dt=FP32):
        return self.ctx.enter_context(self.nc.sbuf_tensor(f"{self.tag}_{name}", shape, dt))

    def ps(self, name, shape, dt=FP32):
        return self.ctx.enter_context(self.nc.psum_tensor(f"{self.tag}_{name}", shape, dt))

    def sem(self, name):
        self.sems.append(self.nc.alloc_semaphore(f"{self.tag}_{name}"))
        return self.sems[-1]

    def counter(self, name, per=1, credit=0):
        return Counter(self.sem(name), per, credit)

    def transfer(self, name, per=1, credit=0):
        return Transfers([self.sem(f"{name}{s}") for s in range(2)], per, credit)

class Weights:

    def __init__(self, nc, memory, tag):
        self.nc, self.memory, self.tag = nc, memory, tag
        self.loaded, self.total = nc.alloc_semaphore(f"{tag}_loaded"), 0

    def sb(self, name, shape, dt=FP32):
        return self.memory.enter_context(self.nc.sbuf_tensor(f"{self.tag}_{name}", shape, dt))

def tiles_of(rows):
    return rows.rearrange("(t p) d -> p t d", p=P)

def block_rows(stream, turn, shift=0):
    return tiles_of(stream[bass.ds(turn.pair * LP + (1 - shift + turn.side * BLK), BLK), :])

def flat_rows(stream, turn):
    return tiles_of(stream[bass.ds(turn.pair * (2 * BLK) + turn.side * BLK, BLK), :])

def stats_of(nc, dve, x, n, sums, mv, sums_ready, mv_ready, i):
    for t in range(n):
        last = nc.vector.bn_stats(sums[:, t, :], x[:, t, :])
    last.then_inc(sums_ready.sem, 1)
    dve.wait_ge(sums_ready.sem, sums_ready.at(i, 1))
    dve.sem_inc(sums_ready.sem, 1)
    for t in range(n):
        last = nc.vector.bn_aggr(mv[:, t, :], sums[:, t, :])
    last.then_inc(mv_ready.sem, 1)

def rstd_of(nc, pool, mv, rstd, eps, minus_half, n, mv_ready, eps_added, rstd_ready, i):
    pool.wait_ge(mv_ready.sem, mv_ready.at(i))
    nc.gpsimd.tensor_tensor(rstd[:, 0:n], mv[:, 0:n, 1], eps[:, 0:n], ALU.add).then_inc(eps_added.sem, 1)
    pool.wait_ge(eps_added.sem, eps_added.at(i))
    nc.gpsimd.tensor_tensor(rstd[:, 0:n], rstd[:, 0:n], minus_half[:, 0:n], ALU.pow).then_inc(rstd_ready.sem, 1)

def normalise(nc, out, x, mv, rstd, n):
    for t in range(n):
        last = nc.vector.tensor_scalar(out[:, t, :], x[:, t, :], mv[:, t, 0:1], rstd[:, t:t + 1],
                                       ALU.subtract, ALU.mult)
    return last

def ahead(eng, body, n=NT):
    with eng.Fori(0, n // 2 - 1) as pair:
        body(Turn(pair, 0), True, True)
        body(Turn(pair, 1), True, True)
    body(Turn(n // 2 - 1, 0), True, False)
    body(Turn(n // 2 - 1, 1), False, False)

def trailing(eng, body):
    body(Turn(0, 0), False, True, True)
    with eng.Fori(0, NT // 2 - 2) as pair:
        body(Turn(pair, 1), True, True, True)
        body(Turn(pair + 1, 0), True, True, True)
    body(Turn(NT // 2 - 2, 1), True, True, True)
    body(Turn(NT // 2 - 1, 0), True, True, False)
    body(Turn(NT // 2 - 1, 1), True, False, False)

def state_space_stage(nc, tag, w, src, dst, ident):
    XR = RANK + 2 * NS
    with ExitStack() as ctx:
        s = Scope(nc, ctx, tag)
        w_in = s.sb("w_in", [P, KD, 2 * HID])
        w_x = s.sb("w_x", [P, CT, XR])
        w_dt = s.sb("w_dt", [RANK, HID])
        w_out = s.sb("w_out", [P, CT, D])
        conv_w, conv_b = s.sb("conv_w", [P, CT, 3]), s.sb("conv_b", [P, CT])
        b_dt, skip = s.sb("b_dt", [P, CT]), s.sb("skip", [P, CT])
        skip_diag = s.sb("skip_diag", [P, CT, P])
        a_log, decay = s.sb("a_log", [P, NS]), s.sb("decay", [P, NS])
        pick = s.sb("pick", [3 * 2 * NS, 2 * NS, P], BF16)
        TX = TB + 1
        minus_half, eps = s.sb("minus_half", [P, TX]), s.sb("eps", [P, TX])
        x, x_after = s.sb("x", [P, 2, TB, D]), s.sb("x_after", [1, D])
        h0, h_after = s.sb("h0", [P, TB, D]), s.sb("h_after", [1, D])
        res = s.sb("res", [P, 2, TB, D])
        sums, mv, rstd = s.sb("sums", [P, TX, 6]), s.sb("mv", [P, TX, 2]), s.sb("rstd", [P, TX])
        hT = s.sb("hT", [P, KD, BLK + 1])
        u = s.sb("u", [P, CT, BLK + 2])
        uc, z, dt = s.sb("uc", [P, 2, CT, BLK]), s.sb("z", [P, 2, CT, BLK]), s.sb("dt", [P, 2, CT, BLK])
        work = s.sb("work", [P, CT, BLK])
        dtp = s.sb("dtp", [RANK, BLK])
        middle, rest = s.sb("middle", [2 * NS, BLK], BF16), s.sb("rest", [2 * NS, BLK])
        parts = s.sb("parts", [3 * 2 * NS, 2, BLK], BF16)
        da = s.sb("da", [P, 2, CT, BLK])
        state = s.sb("state", [P, 3, CT, BLK])
        b_rows, c_rows = s.sb("b_rows", [P, 2, BLK]), s.sb("c_rows", [P, 2, BLK])
        carry = s.sb("carry", [P, NS, CT])
        gated = s.sb("gated", [P, CT, BLK])
        out = s.sb("out", [P, 2, D])
        py = s.ps("py", [P, CT, BLK])
        pb, pc = s.ps("pb", [P, BLK]), s.ps("pc", [P, BLK])
        fa, fb = s.ps("fa", [P, BLK]), s.ps("fb", [P, BLK])

        weights, w_in_loaded = s.sem("weights"), s.sem("w_in_loaded")
        consts = s.counter("consts")
        x_in, after_in, out_sent = s.transfer("x_in"), s.sem("after_in"), s.transfer("out_sent", credit=1)
        decay_ready, skip_ready = s.counter("decay_ready"), s.counter("skip_ready")
        decay_part = s.counter("decay_part")
        sums_ready, mv_ready = s.counter("sums_ready", per=2), s.counter("mv_ready")
        eps_added, rstd_ready, h0_ready = s.counter("eps_added"), s.counter("rstd_ready"), s.counter("h0_ready")
        res_ready = s.counter("res_ready", credit=1)
        tp_ready, hT_ready = s.counter("tp_ready"), s.counter("hT_ready", per=2)
        edge_ready = s.counter("edge_ready")
        u_made, u_copied = s.counter("u_made", per=CT), s.counter("u_copied", per=CT)
        z_made, z_copied, z_ready = s.counter("z_made", per=CT), s.counter("z_copied", per=CT, credit=1), s.counter("z_ready")
        conv_steps, uc_ready = s.counter("conv_steps", per=3 * CT), s.counter("uc_ready")
        xd_made, dtp_ready = s.counter("xd_made"), s.counter("dtp_ready")
        part_steps = s.counter("part_steps", per=4)
        dt_made, abs_ready = s.counter("dt_made", per=CT), s.counter("abs_ready", per=CT)
        relu_ready = s.counter("relu_ready", per=CT)
        soft_steps, dt_ready = s.counter("soft_steps", per=3), s.counter("dt_ready", credit=1)
        gated_ready = s.counter("gated_ready", per=CT)
        out_made, out_ready = s.counter("out_made", per=TB), s.counter("out_ready", per=TB, credit=2)
        after_tp, after_hT = s.counter("after_tp"), s.counter("after_hT")
        after_made, after_copied = s.counter("after_made"), s.counter("after_copied")
        b_made, b_copied = s.counter("b_made"), s.counter("b_copied", credit=1)
        c_made, c_copied = s.counter("c_made"), s.counter("c_copied")
        da_ready, bu_ready = s.counter("da_ready", per=2), s.counter("bu_ready", per=2, credit=2)
        state_ready, seen_ready = s.counter("state_ready", per=CT, credit=2), s.counter("seen_ready", per=2, credit=2)
        added = s.counter("added", per=2, credit=4)
        carried = s.sem("carried")
        stand = s.sem("stand")
        block = ctx.enter_context(nc.Block())
        LAST = Turn(B - 1, 1)
        pairs = [slice(0, 2), slice(2, 4)]
        SLOT = [0, 1, 2] * (NS // 3) + [1]
        SINCE = [4, 2, 4] + [3] * (NS - 4) + [2]

        def halves(eng, body):
            body(Turn(0, 0), False, True)
            with eng.Fori(0, B - 1) as b:
                body(Turn(b, 1), True, True)
                body(Turn(b + 1, 0), True, True)
            body(LAST, True, False)

        def rows(stream, turn):
            return stream[bass.ds(turn.pair * L + turn.side * BLK, BLK), :]

        @block.sync
        def _(sp):
            n = [0]

            def put(to, frm, **how):
                sp.dma_start(to, frm, **how).then_inc(weights, 16)
                n[0] += 1

            def load(turn):
                sp.dma_start(x[:, turn.side, :, :], tiles_of(rows(src, turn))).then_inc(x_in.sems[turn.side], 16)

            def load_after(turn):
                sp.dma_start(x_after[:, :], src[bass.ds(turn.pair * L + BLK, 1), :]).then_inc(after_in, 16)

            load(Turn(0, 0))
            load_after(Turn(0, 0))
            sp.dma_start(w_in[:, :, :], w["w_in"].rearrange("(k p) n -> p k n", p=P)).then_inc(w_in_loaded, 16)
            put(conv_w[:, :, :], w["conv_w"].rearrange("(c p) k -> p c k", p=P))
            put(w_x[:, :, :], w["w_x"].rearrange("(c p) n -> p c n", p=P))
            put(w_dt[:, :], w["w_dt"])
            for to, name in ((conv_b, "conv_b"), (b_dt, "b_dt"), (skip, "skip")):
                put(to[:, :], w[name].rearrange("(c p) -> p c", p=P), allow_slow_non_contiguous=True)
            put(a_log[:, :], w["a_log"].partition_broadcast(P))
            put(pick[:, :, :], w["pick"].rearrange("r (n p) -> r n p", p=P))
            put(w_out[:, :, :], w["w_out"].rearrange("(c p) n -> p c n", p=P))
            assert n[0] == 9
            load(Turn(0, 1))

            def store(turn):
                for t in range(TB):
                    sp.wait_ge(out_ready.sem, out_ready.at(turn.i, t + 1))
                    sp.dma_start(dst[bass.ds(turn.pair * L + (turn.side * BLK + t * P), P), :], out[:, t % 2, :])\
                      .then_inc(out_sent.sems[t % 2], 16)

            def load_next_pair(turn):
                sp.wait_ge(res_ready.sem, res_ready.at(turn.i))
                load(Turn(turn.pair + 1, turn.side))
                if turn.side == 0:
                    sp.wait_ge(h0_ready.sem, h0_ready.at(turn.i))
                    load_after(Turn(turn.pair + 1, 0))

            load_next_pair(Turn(0, 0))
            with sp.Fori(0, B - 2) as b:
                store(Turn(b, 0))
                load_next_pair(Turn(b, 1))
                store(Turn(b, 1))
                load_next_pair(Turn(b + 1, 0))
            store(Turn(B - 2, 0))
            load_next_pair(Turn(B - 2, 1))
            for turn in (Turn(B - 2, 1), Turn(B - 1, 0), Turn(B - 1, 1)):
                store(turn)
            for side in range(2):
                sp.wait_ge(out_sent.sems[side], 16 * (1 + B * TB))

        @block.gpsimd
        def _(pool):
            give_credit(pool, bu_ready, res_ready)
            nc.gpsimd.memset(minus_half[:, :], -0.5)
            nc.gpsimd.memset(mv[:, :, :], 1.0)
            nc.gpsimd.memset(eps[:, :], EPS).then_inc(consts.sem, 1)
            pool.wait_ge(consts.sem, consts.at(0))

            def front(turn, n):
                if n == 1:
                    rstd_of(nc, pool, mv, rstd, eps, minus_half, TX, mv_ready, eps_added, rstd_ready, turn.i)
                elif n == 3:
                    pool.wait_ge(h0_ready.sem, h0_ready.at(turn.i))
                    pool.wait_ge(out_ready.sem, out_ready.at(turn.i - 2))
                    nc.gpsimd.tensor_tensor(res[:, turn.side, :, :], x[:, turn.side, :, :], h0[:, :, :],
                                            ALU.add).then_inc(res_ready.sem, 1)

            def body(turn, before, more):
                for n in range(NS):
                    i = turn.i * NS + n
                    if n == 0:
                        pool.wait_ge(uc_ready.sem, uc_ready.at(turn.i))
                    pool.wait_ge(b_copied.sem, b_copied.at(i))
                    for p in range(2):
                        pool.wait_ge(added.sem, added.at(i - SINCE[n], p + 1))
                        nc.gpsimd.tensor_tensor(state[:, SLOT[n], pairs[p], :], uc[:, turn.side, pairs[p], :],
                                                b_rows[:, n % 2, :].unsqueeze(1).to_broadcast([P, 2, BLK]),
                                                ALU.mult).then_inc(bu_ready.sem, 1)
                    if more:
                        front(turn.next(), n)

            for n in range(NS):
                front(Turn(0, 0), n)
            halves(pool, body)

        @block.scalar
        def _(act):
            give_credit(act, b_copied, z_copied)
            def copy_u(turn, c):
                act.wait_ge(u_made.sem, u_made.at(turn.i, c + 1))
                if c == 0:
                    act.wait_ge(edge_ready.sem, edge_ready.at(turn.i))
                nc.scalar.activation(u[:, c, 1:BLK + 1], fb[:, :], ACT.Copy).then_inc(u_copied.sem, 1)

            def copy_z(turn, c):
                act.wait_ge(z_made.sem, z_made.at(turn.i, c + 1))
                nc.scalar.activation(z[:, turn.side, c, :], [fa, fa, fa, fb][c][:, :], ACT.Copy).then_inc(z_copied.sem, 1)

            def magnitude(turn, c):
                act.wait_ge(dt_made.sem, dt_made.at(turn.i, c + 1))
                nc.scalar.activation(work[:, c, :], [fa, fb][c % 2][:, :], ACT.Abs,
                                     bias=b_dt[:, c:c + 1]).then_inc(abs_ready.sem, 1)
                nc.scalar.activation(dt[:, turn.side, c, :], [fa, fb][c % 2][:, :], ACT.Relu,
                                     bias=b_dt[:, c:c + 1]).then_inc(relu_ready.sem, 1)

            def softplus(turn, p):
                magnitude(turn, 2 * p)
                magnitude(turn, 2 * p + 1)
                act.wait_ge(abs_ready.sem, abs_ready.at(turn.i, 2 * p + 2))
                nc.scalar.activation(work[:, pairs[p], :], work[:, pairs[p], :], ACT.Exp, scale=-1.0).then_inc(soft_steps.sem, 1)

            R = 2 * NS

            def front(turn, n):
                if n == 3:
                    act.wait_ge(tp_ready.sem, tp_ready.at(turn.i))
                    for k in range(KD):
                        nc.scalar.activation(hT[:, k, 0:BLK], [fa, fb][k][:, :], ACT.Copy).then_inc(hT_ready.sem, 1)
                elif n == 4:
                    if turn.side == 0:
                        act.wait_ge(after_tp.sem, after_tp.at(turn.pair))
                        nc.scalar.activation(hT[:, :, BLK:BLK + 1], fa[:, 0:KD].unsqueeze(2), ACT.Copy).then_inc(after_hT.sem, 1)
                    copy_u(turn, 0)
                elif n == 5:
                    if turn.side == 0:
                        act.wait_ge(after_made.sem, after_made.at(turn.pair))
                        nc.scalar.activation(u[:, :, BLK + 1:BLK + 2], fa[:, 0:CT].unsqueeze(2), ACT.Copy)\
                          .then_inc(after_copied.sem, 1)
                    copy_u(turn, 1)
                elif n == 6:
                    copy_u(turn, 2)
                    copy_z(turn, 0)
                elif n == 7:
                    copy_u(turn, 3)
                    copy_z(turn, 1)
                elif n == 8:
                    copy_z(turn, 2)
                    act.wait_ge(conv_steps.sem, conv_steps.at(turn.i))
                    nc.scalar.activation(uc[:, turn.side, :, :], work[:, :, :], ACT.Silu).then_inc(uc_ready.sem, 1)
                elif n == 9:
                    act.wait_ge(xd_made.sem, xd_made.at(turn.i))
                    nc.scalar.activation(dtp[:, :], fb[0:RANK, :], ACT.Copy).then_inc(dtp_ready.sem, 1)
                    nc.scalar.activation(parts[0:R, turn.side, :], fb[RANK:XR, :], ACT.Copy).then_inc(part_steps.sem, 1)
                elif n == 10:
                    softplus(turn, 0)
                elif n == 11:
                    softplus(turn, 1)
                elif n == 12:
                    act.wait_ge(soft_steps.sem, soft_steps.at(turn.i, 2))
                    nc.scalar.activation(work[:, :, :], work[:, :, :], ACT.Ln, bias=1.0).then_inc(soft_steps.sem, 1)
                elif n == 13:
                    act.wait_ge(part_steps.sem, part_steps.at(turn.i, 2))
                    nc.scalar.activation(middle[:, :], rest[:, :], ACT.Copy)
                    nc.scalar.activation(parts[R:2 * R, turn.side, :], rest[:, :], ACT.Copy).then_inc(part_steps.sem, 1)
                    copy_z(turn, 3)

            def gates(turn):
                act.wait_ge(z_copied.sem, z_copied.at(turn.i))
                nc.scalar.activation(z[:, turn.side, :, :], z[:, turn.side, :, :], ACT.Silu).then_inc(z_ready.sem, 1)

            def copy_b(i, side):
                act.wait_ge(bu_ready.sem, bu_ready.at(i - 2))
                act.wait_ge(b_made.sem, b_made.at(i))
                nc.scalar.activation(b_rows[:, side, :], pb[:, :], ACT.Copy).then_inc(b_copied.sem, 1)

            def body(turn, before, more):
                for n in range(NS):
                    i = turn.i * NS + n
                    if n == 0:
                        act.wait_ge(dt_ready.sem, dt_ready.at(turn.i))
                    for p in range(2):
                        act.wait_ge(state_ready.sem, state_ready.at(i - 2, 2 * p + 2))
                        nc.scalar.activation(da[:, n % 2, pairs[p], :], dt[:, turn.side, pairs[p], :], ACT.Exp,
                                             scale=decay[:, n:n + 1]).then_inc(da_ready.sem, 1)
                    if n < NS - 1 or more:
                        copy_b(i + 1, (n + 1) % 2)
                    act.wait_ge(seen_ready.sem, seen_ready.at(i - 2))
                    act.wait_ge(c_made.sem, c_made.at(i))
                    nc.scalar.activation(c_rows[:, n % 2, :], pc[:, :], ACT.Copy).then_inc(c_copied.sem, 1)
                    if n == 1:
                        gates(turn)
                    if more:
                        front(turn.next(), n)

            for n in range(NS):
                if n == 8:
                    act.wait_ge(weights, 16 * 9)
                    nc.scalar.activation(decay[:, :], a_log[:, :], ACT.Exp).then_inc(decay_part.sem, 1)
                    act.wait_ge(decay_part.sem, decay_part.at(0))
                    nc.scalar.activation(decay[:, :], decay[:, :], ACT.Copy, scale=-1.0).then_inc(decay_ready.sem, 1)
                    act.wait_ge(decay_ready.sem, decay_ready.at(0))
                front(Turn(0, 0), n)
            copy_b(0, 0)
            halves(act, body)

        @block.vector
        def _(dve):
            give_credit(dve, out_ready, state_ready, seen_ready, out_sent, dt_ready)
            dve.wait_ge(consts.sem, consts.at(0))

            def statistics(turn):
                dve.wait_ge(x_in.sems[turn.side], x_in.at(turn))
                if turn.side == 0:
                    dve.wait_ge(after_in, turn.pair * 16 + 16)
                dve.wait_ge(res_ready.sem, res_ready.at(turn.i - 1))
                for t in range(TB):
                    last = nc.vector.bn_stats(sums[:, t, :], x[:, turn.side, t, :])
                if turn.side == 0:
                    last = nc.vector.bn_stats(sums[0:1, TB, :], x_after[:, :])
                last.then_inc(sums_ready.sem, 1)
                dve.wait_ge(sums_ready.sem, sums_ready.at(turn.i, 1))
                dve.sem_inc(sums_ready.sem, 1)
                for t in range(TB):
                    last = nc.vector.bn_aggr(mv[:, t, :], sums[:, t, :])
                if turn.side == 0:
                    last = nc.vector.bn_aggr(mv[0:1, TB, :], sums[0:1, TB, :])
                last.then_inc(mv_ready.sem, 1)

            def convolve(turn, c):
                dve.wait_ge(u_copied.sem, u_copied.at(turn.i, c + 1))
                if c == 0:
                    dve.wait_ge(edge_ready.sem, edge_ready.at(turn.i))
                    if turn.side == 0:
                        dve.wait_ge(after_copied.sem, after_copied.at(turn.pair))
                    dve.wait_ge(dt_ready.sem, dt_ready.at(turn.i - 1))
                w0, w1, w2 = (conv_w[:, c, k:k + 1] for k in range(3))
                nc.vector.tensor_scalar(work[:, c, :], u[:, c, 1:BLK + 1], w1, conv_b[:, c:c + 1],
                                        ALU.mult, ALU.add).then_inc(conv_steps.sem, 1)
                for k, wk in ((0, w0), (2, w2)):
                    dve.wait_ge(conv_steps.sem, conv_steps.at(turn.i, 3 * c + 1 + k // 2))
                    nc.vector.scalar_tensor_tensor(work[:, c, :], u[:, c, k:k + BLK], wk,
                                                   work[:, c, :], ALU.mult, ALU.add).then_inc(conv_steps.sem, 1)

            def split(turn, part):
                R, side = 2 * NS, turn.side
                if part == 1:
                    dve.wait_ge(part_steps.sem, part_steps.at(turn.i, 1))
                    nc.vector.tensor_tensor(rest[:, :], fb[RANK:XR, :], parts[0:R, side, :], ALU.subtract).then_inc(part_steps.sem, 1)
                else:
                    dve.wait_ge(part_steps.sem, part_steps.at(turn.i, 3))
                    nc.vector.tensor_tensor(parts[2 * R:3 * R, side, :], rest[:, :], middle[:, :], ALU.subtract)\
                      .then_inc(part_steps.sem, 1)

            def front(turn, n):
                if n == 0:
                    statistics(turn)
                elif n == 1:
                    dve.wait_ge(rstd_ready.sem, rstd_ready.at(turn.i))
                    if turn.side == 0:
                        nc.vector.tensor_scalar(h_after[:, :], x_after[:, :], mv[0:1, TB, 0:1], rstd[0:1, TB:TB + 1],
                                                ALU.subtract, ALU.mult)
                    normalise(nc, h0, x[:, turn.side, :, :], mv, rstd, TB).then_inc(h0_ready.sem, 1)
                elif n == 2:
                    if turn.side:
                        nc.vector.memset(u[:, :, BLK + 1:BLK + 2], 0.0)
                        nc.vector.tensor_copy(u[:, :, 0:1], u[:, :, BLK:BLK + 1]).then_inc(edge_ready.sem, 1)
                    else:
                        nc.vector.memset(u[:, :, 0:1], 0.0).then_inc(edge_ready.sem, 1)
                elif 5 <= n <= 7:
                    convolve(turn, n - 5)
                    if n == 7:
                        convolve(turn, 3)
                elif n == 9:
                    split(turn, 1)
                elif n == 13:
                    split(turn, 2)

            def soften(turn):
                dve.wait_ge(soft_steps.sem, soft_steps.at(turn.i))
                dve.wait_ge(relu_ready.sem, relu_ready.at(turn.i))
                nc.vector.tensor_tensor(dt[:, turn.side, :, :], dt[:, turn.side, :, :], work[:, :, :],
                                        ALU.add).then_inc(dt_ready.sem, 1)

            def gate(turn, p):
                dve.wait_ge(z_ready.sem, z_ready.at(turn.i))
                dve.wait_ge(added.sem, added.at(turn.i * NS + NS - 1, p + 1))
                for c in (2 * p, 2 * p + 1):
                    nc.vector.tensor_tensor(gated[:, c, :], py[:, c, :], z[:, turn.side, c, :],
                                            ALU.mult).then_inc(gated_ready.sem, 1)

            def output(turn, t):
                dve.wait_ge(out_made.sem, out_made.at(turn.i, t + 1))
                dve.wait_ge(res_ready.sem, res_ready.at(turn.i))
                dve.wait_ge(out_sent.sems[t % 2], turn.i * (16 * TB // 2) + 16 * (t // 2 + 1))
                nc.vector.tensor_tensor(out[:, t % 2, :], res[:, turn.side, t, :], [fa, fb][t % 2][:, 0:D],
                                        ALU.add).then_inc(out_ready.sem, 1)

            def body(turn, before, more):
                for n in range(NS):
                    i, slot, side = turn.i * NS + n, SLOT[n], n % 2
                    for p in range(2):
                        dve.wait_ge(da_ready.sem, da_ready.at(i, p + 1))
                        dve.wait_ge(bu_ready.sem, bu_ready.at(i, p + 1))
                        if turn.side and p == 0:
                            dve.wait_ge(carried, turn.pair * NS + n + 1)
                        for c in (2 * p, 2 * p + 1):
                            nc.vector.tensor_tensor_scan(state[:, slot, c, :], da[:, side, c, :], state[:, slot, c, :],
                                                         carry[:, n, c:c + 1] if turn.side else 0.0,
                                                         ALU.mult, ALU.add).then_inc(state_ready.sem, 1)
                    if turn.side == 0:
                        dve.wait_ge(state_ready.sem, state_ready.at(i))
                        nc.vector.tensor_copy(carry[:, n, :].unsqueeze(2), state[:, slot, :, BLK - 1:BLK]).then_inc(carried, 1)
                    if n == 0 and before:
                        gate(turn.before(), 0)
                        gate(turn.before(), 1)
                    if n == NS - 2 and more:
                        soften(turn.next())
                    for p in range(2):
                        dve.wait_ge(state_ready.sem, state_ready.at(i, 2 * p + 2))
                        if turn.side == 0 and p == 0:
                            dve.wait_ge(carried, turn.pair * NS + n + 1)
                        dve.wait_ge(c_copied.sem, c_copied.at(i))
                        nc.vector.tensor_tensor(state[:, slot, pairs[p], :], state[:, slot, pairs[p], :],
                                                c_rows[:, side, :].unsqueeze(1).to_broadcast([P, 2, BLK]),
                                                ALU.mult).then_inc(seen_ready.sem, 1)
                    if before and n < 2:
                        output(turn.before(), 2 * n)
                        output(turn.before(), 2 * n + 1)
                    if more:
                        front(turn.next(), n)

            for n in range(NS):
                if n == 4:
                    dve.wait_ge(weights, 16 * 9)
                    for c in range(CT):
                        last = nc.vector.tensor_scalar(skip_diag[:, c, :], ident, skip[:, c:c + 1], None, ALU.mult)
                    last.then_inc(skip_ready.sem, 1)
                front(Turn(0, 0), n)
            soften(Turn(0, 0))
            halves(dve, body)
            gate(LAST, 0)
            gate(LAST, 1)
            for t in range(TB):
                output(LAST, t)

        @block.tensor
        def _(pe):
            give_credit(pe, added)

            def product_in(turn, bank, c, g):
                for k in range(KD):
                    last = nc.tensor.matmul(bank[:, :], w_in[:, k, g * HID + c * P:g * HID + (c + 1) * P],
                                            hT[:, k, 0:BLK], start=(k == 0), stop=(k == KD - 1))
                return last

            def product_u(turn, c):
                if c:
                    pe.wait_ge(u_copied.sem, u_copied.at(turn.i, c))
                else:
                    pe.wait_ge(hT_ready.sem, hT_ready.at(turn.i))
                product_in(turn, fb, c, 0).then_inc(u_made.sem, 1)

            def product_z(turn, c):
                if c == 0:
                    if turn.side == 0:
                        pe.wait_ge(after_copied.sem, after_copied.at(turn.pair))
                elif c < 3:
                    pe.wait_ge(z_copied.sem, z_copied.at(turn.i, c))
                else:
                    pe.wait_ge(relu_ready.sem, relu_ready.at(turn.i, 4))
                product_in(turn, [fa, fa, fa, fb][c], c, 1).then_inc(z_made.sem, 1)

            def product_x(turn, c):
                if c == 0:
                    pe.wait_ge(uc_ready.sem, uc_ready.at(turn.i))
                    pe.wait_ge(u_copied.sem, u_copied.at(turn.i))
                last = nc.tensor.matmul(fb[0:XR, :], w_x[:, c, :], uc[:, turn.side, c, :],
                                        start=(c == 0), stop=(c == CT - 1))
                if c == CT - 1:
                    last.then_inc(xd_made.sem, 1)

            def product_dt(turn, c):
                if c == 0:
                    pe.wait_ge(dtp_ready.sem, dtp_ready.at(turn.i))
                    pe.wait_ge(z_copied.sem, z_copied.at(turn.i, 3))
                elif c == 1:
                    pe.wait_ge(part_steps.sem, part_steps.at(turn.i, 2))
                else:
                    pe.wait_ge(relu_ready.sem, relu_ready.at(turn.i, c - 1))
                nc.tensor.matmul([fa, fb][c % 2][:, :], w_dt[:, c * P:(c + 1) * P], dtp[:, :],
                                 start=True, stop=True).then_inc(dt_made.sem, 1)

            def front(turn, n):
                if n == 2:
                    pe.wait_ge(h0_ready.sem, h0_ready.at(turn.i))
                    pe.wait_ge(out_ready.sem, out_ready.at(turn.i - 2))
                    pe.wait_ge(z_copied.sem, z_copied.at(turn.i - 1))
                    for k in range(KD):
                        for t in range(TB):
                            last = nc.tensor.transpose([fa, fb][k][:, t * P:(t + 1) * P],
                                                       h0[:, t, k * P:(k + 1) * P], ident)
                    last.then_inc(tp_ready.sem, 1)
                elif n == 3:
                    if turn.side == 0:
                        pe.wait_ge(hT_ready.sem, hT_ready.at(turn.i, 1))
                        pe.sem_inc(stand, 1)
                        for k in range(KD):
                            last = nc.tensor.transpose(fa[:, k:k + 1], h_after[:, k * P:(k + 1) * P], ident[0:1, 0:1])
                        last.then_inc(after_tp.sem, 1)
                    product_u(turn, 0)
                elif n == 4:
                    if turn.side == 0:
                        pe.wait_ge(after_hT.sem, after_hT.at(turn.pair))
                        for c in range(CT):
                            for k in range(KD):
                                last = nc.tensor.matmul(fa[:, c:c + 1], w_in[:, k, c * P:(c + 1) * P],
                                                        hT[:, k, BLK:BLK + 1], start=(k == 0), stop=(k == KD - 1))
                        last.then_inc(after_made.sem, 1)
                    product_u(turn, 1)
                elif n == 5:
                    product_u(turn, 2)
                    product_z(turn, 0)
                elif n == 6:
                    product_u(turn, 3)
                    product_z(turn, 1)
                elif n == 7:
                    product_z(turn, 2)
                elif n == 8:
                    for c in range(CT):
                        product_x(turn, c)
                elif n == 9:
                    product_dt(turn, 0)
                    product_dt(turn, 1)
                elif n == 10:
                    product_dt(turn, 2)
                    product_dt(turn, 3)
                elif n == 12:
                    product_z(turn, 3)

            def spread(bank, row, turn):
                return nc.tensor.matmul(bank[:, :], pick[:, row, :], parts[:, turn.side, :], start=True, stop=True)

            def product_out(turn, t):
                if t < 2:
                    pe.wait_ge(gated_ready.sem, gated_ready.at(turn.i))
                    pe.wait_ge(z_copied.sem, z_copied.at(turn.i if turn is LAST else turn.i + 1))
                else:
                    pe.wait_ge(out_ready.sem, out_ready.at(turn.i, t - 1))
                for c in range(CT):
                    last = nc.tensor.matmul([fa, fb][t % 2][:, 0:D], gated[:, c, t * P:(t + 1) * P], w_out[:, c, :],
                                            start=(c == 0), stop=(c == CT - 1))
                last.then_inc(out_made.sem, 1)

            def body(turn, before, more):
                for n in range(NS):
                    i = turn.i * NS + n
                    if n == 0:
                        for c in range(CT):
                            if before:
                                pe.wait_ge(gated_ready.sem, gated_ready.at(turn.i - 1, c + 1))
                            nc.tensor.matmul(py[:, c, :], skip_diag[:, c, :], uc[:, turn.side, c, :],
                                             start=True, stop=False)
                    if n == NS - 2 and more:
                        pe.wait_ge(part_steps.sem, part_steps.at(turn.i + 1))
                    if n < NS - 2 or more:
                        pe.wait_ge(b_copied.sem, b_copied.at(i + 1))
                        spread(pb, (n + 2) % NS, turn if n < NS - 2 else turn.next()).then_inc(b_made.sem, 1)
                    if n < NS - 1 or more:
                        pe.wait_ge(c_copied.sem, c_copied.at(i))
                        spread(pc, NS + (n + 1) % NS, turn if n < NS - 1 else turn.next()).then_inc(c_made.sem, 1)
                    if before and n < 2:
                        product_out(turn.before(), 2 * n)
                        product_out(turn.before(), 2 * n + 1)
                    if more:
                        front(turn.next(), n)
                    for p in range(2):
                        pe.wait_ge(seen_ready.sem, seen_ready.at(i, p + 1))
                        for c in (2 * p, 2 * p + 1):
                            last = nc.tensor.matmul(py[:, c, :], ident, state[:, SLOT[n], c, :], start=False, stop=(n == NS - 1))
                        last.then_inc(added.sem, 1)

            for n in range(NS):
                if n == 3:
                    pe.wait_ge(w_in_loaded, 16)
                elif n == 8:
                    pe.wait_ge(weights, 16 * 9)
                front(Turn(0, 0), n)
            pe.wait_ge(skip_ready.sem, skip_ready.at(0))
            pe.wait_ge(part_steps.sem, part_steps.at(0))
            spread(pb, 0, Turn(0, 0)).then_inc(b_made.sem, 1)
            spread(pc, NS, Turn(0, 0)).then_inc(c_made.sem, 1)
            pe.wait_ge(b_copied.sem, b_copied.at(0))
            spread(pb, 1, Turn(0, 0)).then_inc(b_made.sem, 1)
            halves(pe, body)
            for t in range(TB):
                product_out(LAST, t)

class MoeWeights(Weights):
    def __init__(self, nc, memory, tag, w):
        super().__init__(nc, memory, tag)
        self.w, self.total = w, 16 * 4
        self.experts_in = nc.alloc_semaphore(f"{tag}_experts_in")
        self.experts = self.sb("experts", [P, KD, E * D])
        self.router = self.sb("router", [P, KD, E])
        self.router_b = self.sb("router_b", [P, E])
        self.expert_b = self.sb("expert_b", [E, D])
        self.rank = self.sb("rank", [P, E])

    def load(self, sp):
        w = self.w
        sp.dma_start(self.router[:, :, :], w["router"].rearrange("(k p) n -> p k n", p=P)).then_inc(self.loaded, 16)
        sp.dma_start(self.router_b[:, :], w["router_b"].partition_broadcast(P)).then_inc(self.loaded, 16)
        sp.dma_start(self.rank[:, :], w["rank"].partition_broadcast(P)).then_inc(self.loaded, 16)
        sp.dma_start(self.expert_b[:, :], w["expert_b"]).then_inc(self.loaded, 16)
        sp.dma_start(self.experts[:, :, :], w["experts"].rearrange("(k p) n -> p k n", p=P)).then_inc(self.experts_in, 16)

def moe_stage(nc, tag, own, src, dst, ident, upcoming):
    with ExitStack() as ctx:
        s = Scope(nc, ctx, tag)
        s.adopt(own)
        s.sems.append(own.experts_in)
        experts, router, router_b, expert_b, rank = own.experts, own.router, own.router_b, own.expert_b, own.rank
        minus_half, eps = s.sb("minus_half", [P, TB]), s.sb("eps", [P, TB])
        x = s.sb("x", [P, 2, TB, D])
        sums, mv, rstd = s.sb("sums", [P, TB, 6]), s.sb("mv", [P, TB, 2]), s.sb("rstd", [P, TB])
        n = s.sb("n", [P, TB, D])
        hT = s.sb("hT", [P, 2, KD, BLK])
        logit, prob = s.sb("logit", [P, TB, E]), s.sb("prob", [P, TB, E])
        best, total, key_max = s.sb("best", [P, TB]), s.sb("total", [P, TB]), s.sb("key_max", [P, TB])
        key = s.sb("key", [P, TB, E])
        gate = s.sb("gate", [P, 2, TB, E])
        gateT = s.sb("gateT", [E, 2, BLK])
        y = s.sb("y", [P, 2, TB, D])
        tp = [s.ps(f"tp{k}", [P, BLK]) for k in range(KD)]
        ex = [s.ps(f"ex{k}", [P, 2 * D]) for k in range(4)]
        small = s.ps("small", [P, BLK])
        bias = s.ps("bias", [P, BLK])
        PAIRS = E // 2
        GATE_STEPS = 9

        consts = s.counter("consts")
        x_in = s.transfer("x_in")
        sums_ready, mv_ready = s.counter("sums_ready", per=2), s.counter("mv_ready")
        eps_added, rstd_ready, n_ready = s.counter("eps_added"), s.counter("rstd_ready"), s.counter("n_ready")
        tp_ready, hT_ready = s.counter("tp_ready"), s.counter("hT_ready", credit=1)
        logits_ready, gate_steps, prob_ready = s.counter("logits_ready"), s.counter("gate_steps", per=GATE_STEPS, credit=1), s.counter("prob_ready")
        gateT_made, gateT_ready = s.counter("gateT_made"), s.counter("gateT_ready", credit=1)
        bias_ready = s.counter("bias_ready", per=TB)
        base_ready = s.counter("base_ready", per=TB, credit=1)
        ex_ready = s.counter("ex_ready", per=TB * PAIRS)
        sum_ready = s.counter("sum_ready", per=TB * E, credit=1)
        y_out = s.transfer("y_out", credit=1)
        block = ctx.enter_context(nc.Block())

        @block.sync
        def _(sp):
            def load(turn):
                sp.dma_start(x[:, turn.side, :, :], flat_rows(src, turn)).then_inc(x_in.sems[turn.side], 16)

            load(Turn(0, 0))
            own.load(sp)
            load(Turn(0, 1))
            upcoming.load(sp)

            def store(turn):
                sp.wait_ge(sum_ready.sem, sum_ready.at(turn.i))
                sp.dma_start(flat_rows(dst, turn), y[:, turn.side, :, :]).then_inc(y_out.sems[turn.side], 16)

            with sp.Fori(0, NBLK // 2 - 1) as pair:
                for side in range(2):
                    sp.wait_ge(n_ready.sem, n_ready.at(Turn(pair, side).i))
                    sp.wait_ge(base_ready.sem, base_ready.at(Turn(pair, side).i))
                    load(Turn(pair + 1, side))
                    store(Turn(pair, side))
            for side in range(2):
                store(Turn(NBLK // 2 - 1, side))
            for side in range(2):
                sp.wait_ge(y_out.sems[side], y_out.total(NBLK // 2))

        @block.gpsimd
        def _(pool):
            nc.gpsimd.memset(minus_half[:, :], -0.5)
            nc.gpsimd.memset(eps[:, :], EPS).then_inc(consts.sem, 1)
            pool.wait_ge(consts.sem, consts.at(0))

            def front(turn):
                rstd_of(nc, pool, mv, rstd, eps, minus_half, TB, mv_ready, eps_added, rstd_ready, turn.i)

            front(Turn(0, 0))
            turns(pool, NBLK, lambda turn, more: front(turn.next()) if more else None)

        @block.scalar
        def _(act):
            give_credit(act, hT_ready)

            def hidden(turn):
                act.wait_ge(tp_ready.sem, tp_ready.at(turn.i))
                for k in range(KD):
                    last = nc.scalar.activation(hT[:, turn.side, k, :], tp[k][:, :], ACT.Copy)
                last.then_inc(hT_ready.sem, 1)

            def probs(turn):
                act.wait_ge(gate_steps.sem, gate_steps.at(turn.i, 3))
                nc.scalar.activation(prob[:, :, :], logit[:, :, :], ACT.Exp).then_inc(prob_ready.sem, 1)

            def body(turn, more):
                if more:
                    hidden(turn.next())
                    probs(turn.next())

            hidden(Turn(0, 0))
            probs(Turn(0, 0))
            turns(act, NBLK, body)

        @block.vector
        def _(dve):
            give_credit(dve, gate_steps, gateT_ready, base_ready, sum_ready, y_out)

            def front(turn):
                dve.wait_ge(x_in.sems[turn.side], x_in.at(turn))
                stats_of(nc, dve, x[:, turn.side, :, :], TB, sums, mv, sums_ready, mv_ready, turn.i)
                dve.wait_ge(rstd_ready.sem, rstd_ready.at(turn.i))
                normalise(nc, n, x[:, turn.side, :, :], mv, rstd, TB).then_inc(n_ready.sem, 1)

            def gates(turn):
                step = [0]

                def link(ins):
                    ins.then_inc(gate_steps.sem, 1)
                    step[0] += 1
                    dve.wait_ge(gate_steps.sem, gate_steps.at(turn.i, step[0]))

                def wide(a):
                    return a[:, :].unsqueeze(2).to_broadcast([P, TB, E])

                def all_tiles(a):
                    return a[:, :].unsqueeze(1).to_broadcast([P, TB, E])

                g = gate[:, turn.side, :, :]
                dve.wait_ge(logits_ready.sem, logits_ready.at(turn.i))
                logits = small[:, 0:TB * E].rearrange("p (t e) -> p t e", e=E)
                link(nc.vector.tensor_tensor(logit[:, :, :], logits, all_tiles(router_b), ALU.add))
                link(nc.vector.tensor_reduce(best[:, :], logit[:, :, :], AX.X, ALU.max))
                link(nc.vector.tensor_tensor(logit[:, :, :], logit[:, :, :], wide(best), ALU.subtract))
                link(nc.vector.scalar_tensor_tensor(key[:, :, :], logit[:, :, :], 0.0, all_tiles(rank),
                                                    ALU.is_equal, ALU.mult))
                link(nc.vector.tensor_reduce(key_max[:, :], key[:, :, :], AX.X, ALU.max))
                link(nc.vector.tensor_tensor(g, key[:, :, :], wide(key_max), ALU.is_equal))
                dve.wait_ge(prob_ready.sem, prob_ready.at(turn.i))
                link(nc.vector.tensor_reduce(total[:, :], prob[:, :, :], AX.X, ALU.add))
                link(nc.vector.reciprocal(total[:, :], total[:, :]))
                link(nc.vector.tensor_tensor(g, g, wide(total), ALU.mult))
                assert step[0] == GATE_STEPS

            def tile(turn, t):
                acc = y[:, turn.side, t, :]
                dve.wait_ge(bias_ready.sem, bias_ready.at(turn.i, t + 1))
                if t == 0:
                    dve.wait_ge(y_out.sems[turn.side], y_out.at(turn, back=1))
                nc.vector.tensor_tensor(acc, x[:, turn.side, t, :], bias[:, 0:D], ALU.add).then_inc(base_ready.sem, 1)
                dve.wait_ge(base_ready.sem, base_ready.at(turn.i, t + 1))
                for e in range(E):
                    if e % 2 == 0:
                        dve.wait_ge(ex_ready.sem, ex_ready.at(turn.i, t * PAIRS + e // 2 + 1))
                    nc.vector.scalar_tensor_tensor(
                        acc, ex[e // 2][:, e % 2 * D:(e % 2 + 1) * D], gate[:, turn.side, t, e:e + 1], acc,
                        ALU.mult, ALU.add).then_inc(sum_ready.sem, 1)
                    if e < E - 1:
                        dve.wait_ge(sum_ready.sem, sum_ready.at(turn.i, t * E + e + 1))

            def gate_columns(turn):
                dve.wait_ge(gateT_made.sem, gateT_made.at(turn.i))
                nc.vector.tensor_copy(gateT[:, turn.side, :], small[0:E, :]).then_inc(gateT_ready.sem, 1)

            def body(turn, more):
                if more:
                    front(turn.next())
                tile(turn, 0)
                tile(turn, 1)
                if more:
                    gates(turn.next())
                tile(turn, 2)
                if more:
                    gate_columns(turn.next())
                tile(turn, 3)

            dve.wait_ge(own.loaded, own.total)
            front(Turn(0, 0))
            gates(Turn(0, 0))
            gate_columns(Turn(0, 0))
            turns(dve, NBLK, body)

        @block.tensor
        def _(pe):
            def transposes(turn):
                pe.wait_ge(n_ready.sem, n_ready.at(turn.i))
                pe.wait_ge(hT_ready.sem, hT_ready.at(turn.i - 1))
                for k in range(KD):
                    for t in range(TB):
                        last = nc.tensor.transpose(tp[k][:, t * P:(t + 1) * P], n[:, t, k * P:(k + 1) * P], ident)
                last.then_inc(tp_ready.sem, 1)

            def route(turn):
                pe.wait_ge(hT_ready.sem, hT_ready.at(turn.i))
                pe.wait_ge(gateT_ready.sem, gateT_ready.at(turn.i - 1))
                for t in range(TB):
                    for k in range(KD):
                        last = nc.tensor.matmul(small[:, t * E:(t + 1) * E], hT[:, turn.side, k, t * P:(t + 1) * P],
                                                router[:, k, :], start=(k == 0), stop=(k == KD - 1))
                last.then_inc(logits_ready.sem, 1)

            def gate_columns(turn):
                pe.wait_ge(gate_steps.sem, gate_steps.at(turn.i))
                for t in range(TB):
                    last = nc.tensor.transpose(small[0:E, t * P:(t + 1) * P], gate[:, turn.side, t, :], ident)
                last.then_inc(gateT_made.sem, 1)

            def tile(turn, t):
                if t == 0:
                    pe.wait_ge(gateT_ready.sem, gateT_ready.at(turn.i))
                if t:
                    pe.wait_ge(base_ready.sem, base_ready.at(turn.i, t))
                else:
                    pe.wait_ge(base_ready.sem, base_ready.at(turn.i - 1))
                nc.tensor.matmul(bias[:, 0:D], gateT[:, turn.side, t * P:(t + 1) * P], expert_b[:, :],
                                               start=True, stop=True).then_inc(bias_ready.sem, 1)
                for pair in range(PAIRS):
                    if t:
                        pe.wait_ge(sum_ready.sem, sum_ready.at(turn.i, (t - 1) * E + 2 * pair + 2))
                    else:
                        pe.wait_ge(sum_ready.sem, sum_ready.at(turn.i - 1, (TB - 1) * E + 2 * pair + 2))
                    for k in range(KD):
                        last = nc.tensor.matmul(ex[pair][:, :], hT[:, turn.side, k, t * P:(t + 1) * P],
                                                experts[:, k, pair * 2 * D:(pair + 1) * 2 * D],
                                                start=(k == 0), stop=(k == KD - 1))
                    last.then_inc(ex_ready.sem, 1)

            def body(turn, more):
                tile(turn, 0)
                if more:
                    transposes(turn.next())
                tile(turn, 1)
                if more:
                    route(turn.next())
                tile(turn, 2)
                if more:
                    gate_columns(turn.next())
                tile(turn, 3)

            pe.wait_ge(own.loaded, own.total)
            transposes(Turn(0, 0))
            route(Turn(0, 0))
            gate_columns(Turn(0, 0))
            pe.wait_ge(own.experts_in, 16)
            turns(pe, NBLK, body)

class LinWeights(Weights):
    def __init__(self, nc, memory, tag, w):
        super().__init__(nc, memory, tag)
        self.w, self.total = w, 16 * 9
        self.wT = self.sb("wT", [P, 2, H1 // 2, D])
        self.proj = self.sb("proj", [P, DH])
        self.wv = self.sb("wv", [P, KD, H1 * DH])
        self.wo = self.sb("wo", [P, H1 // 2, D])
        self.gain, self.offset = self.sb("gain", [P, KD]), self.sb("offset", [P, KD])
        self.causal = self.sb("causal", [P, P])

    def load(self, sp):
        w = self.w
        for j, name in enumerate(("wqT", "wkT")):
            sp.dma_start(self.wT[:, j, :, :], w[name].rearrange("(r p) d -> p r d", p=P)).then_inc(self.loaded, 16)
        for j in range(2):
            sp.dma_start(self.proj[j * DH:(j + 1) * DH, :], w["proj"]).then_inc(self.loaded, 16)
        sp.dma_start(self.wv[:, :, :], w["wv"].rearrange("(k p) n -> p k n", p=P)).then_inc(self.loaded, 16)
        sp.dma_start(self.wo[:, :, :], w["wo"].rearrange("(r p) n -> p r n", p=P)).then_inc(self.loaded, 16)
        sp.dma_start(self.causal[:, :], w["causal"]).then_inc(self.loaded, 16)
        for vec, to in ((w["gain"], self.gain), (w["offset"], self.offset)):
            sp.dma_start(to[:, :], vec.rearrange("(k p) -> p k", p=P),
                         allow_slow_non_contiguous=True).then_inc(self.loaded, 16)

def linear_attention_stage(nc, tag, own, src, dst, ident, upcoming):
    PR = H1 // 2
    GP = 4
    VW = DH + 1
    BANKS = [(0, 3), (3, 6), (6, 8)]
    with ExitStack() as ctx:
        s = Scope(nc, ctx, tag)
        s.adopt(own)
        wT, wv, wo, gain, offset, causal = own.wT, own.wv, own.wo, own.gain, own.offset, own.causal
        proj2 = s.sb("proj2", [P, P])
        wqk = s.sb("wqk", [P, 2, KD, H1 * DH])
        minus_half, eps = s.sb("minus_half", [P, 1]), s.sb("eps", [P, 1])
        x, keep = s.sb("x", [P, 2, 1, D]), s.sb("keep", [P, 2, 1])
        sums, mv, rstd, rstd2 = s.sb("sums", [P, 1, 6]), s.sb("mv", [P, 1, 2]), s.sb("rstd", [P, 1]), s.sb("rstd2", [P, 1])
        h, h_keep, n = s.sb("h", [P, 2, D]), s.sb("h_keep", [P, D]), s.sb("n", [P, D])
        hT = s.sb("hT", [P, KD, P])
        qkT = s.sb("qkT", [P, 2, 2, PR, P])
        grown = s.sb("grown", [P, 2, GP * P])
        v = s.sb("v", [P, 2, H1, VW])
        k_rows = s.sb("k_rows", [P, PR, P])
        scores = s.sb("scores", [P, H1, P])
        state = s.sb("state", [P, PR, 2 * VW])
        den = s.sb("den", [P, H1])
        attn = s.sb("attn", [P, H1, DH])
        attnT = s.sb("attnT", [P, PR, P])
        y = s.sb("y", [P, 2, D])
        pa = [s.ps(f"pa{k}", [P, 512]) for k in range(2)]
        pb = [s.ps(f"pb{k}", [P, 512]) for k in range(2)]
        pc = [s.ps(f"pc{k}", [P, 512]) for k in range(3)]
        pt = s.ps("pt", [P, 512])
        score_banks = [pb[0], pb[1], pc[0], pc[1]]

        zeroed, proj_laid = s.counter("zeroed"), s.counter("proj_laid")
        folded, folded_read = s.counter("folded", per=4 * KD), s.counter("folded_read", per=4 * KD)
        consts = s.counter("consts")
        x_in, keep_in = s.transfer("x_in"), s.transfer("keep_in")
        keep_free = s.sem("keep_free")
        sums_ready, mv_ready = s.counter("sums_ready", per=2), s.counter("mv_ready")
        eps_added, rstd_ready, rstd2_ready = s.counter("eps_added", per=4), s.counter("rstd_ready"), s.counter("rstd2_ready")
        h_ready, n_ready, kept = s.counter("h_ready"), s.counter("n_ready"), s.counter("kept")
        tp_ready, hT_ready = s.counter("tp_ready"), s.counter("hT_ready", credit=1)
        proj_ready, exp_ready = s.counter("proj_ready", per=6), s.counter("exp_ready", per=4)
        min_ready, phi_ready = s.counter("min_ready", per=4), s.counter("phi_ready", per=4, credit=1)
        v_ready = s.counter("v_ready", per=2, credit=1)
        kt_ready, k_rows_ready = s.counter("kt_ready", per=2), s.counter("k_rows_ready", per=2)
        st_ready, scores_ready = s.counter("st_ready", per=4), s.counter("scores_ready", per=4)
        num_ready, den_steps = s.counter("num_ready", per=3), s.counter("den_steps", per=6)
        attn_ready = s.counter("attn_ready", per=3)
        delta_ready, state_ready = s.counter("delta_ready", per=3), s.counter("state_ready", per=3, credit=1)
        at_ready, attnT_ready = s.counter("at_ready", per=2), s.counter("attnT_ready", per=2, credit=1)
        out_ready, y_ready = s.counter("out_ready"), s.counter("y_ready", credit=2)
        y_out = s.transfer("y_out", credit=1)
        block = ctx.enter_context(nc.Block())

        @block.sync
        def _(sp):
            def rows(stream, turn):
                at = turn.i * P
                return stream[bass.ds(at if isinstance(at, int) else sp.snap(at), P), :]

            def load(to, rows_of, turn, sems):
                sp.dma_start(to, rows_of).then_inc(sems[turn.side], 16)

            for first in (Turn(0, 0), Turn(0, 1)):
                load(x[:, first.side, 0, :], rows(src, first), first, x_in.sems)
                load(keep[:, first.side, :], rows(own.w["keep"], first), first, keep_in.sems)
            upcoming.load(sp)

            def body(turn, before, more, more2):
                then = Turn(turn.pair + 1, turn.side)
                if more2:
                    x_rows, keep_rows = rows(src, then), rows(own.w["keep"], then)
                if before:
                    y_rows = rows(dst, turn.before())
                if more2:
                    sp.wait_ge(h_ready.sem, h_ready.at(turn.i))
                    load(x[:, turn.side, 0, :], x_rows, then, x_in.sems)
                if before:
                    sp.wait_ge(y_ready.sem, y_ready.at(turn.i - 1))
                    sp.dma_start(y_rows, y[:, 1 - turn.side, :]).then_inc(y_out.sems[1 - turn.side], 16)
                if more2:
                    sp.wait_ge(k_rows_ready.sem, k_rows_ready.at(turn.i))
                    sp.wait_ge(state_ready.sem, state_ready.at(turn.i))
                    sp.sem_inc(keep_free, 1)
                    load(keep[:, turn.side, :], keep_rows, then, keep_in.sems)

            trailing(sp, body)
            sp.wait_ge(y_ready.sem, y_ready.at(NT - 1))
            sp.dma_start(rows(dst, Turn(NT // 2 - 1, 1)), y[:, 1, :]).then_inc(y_out.sems[1], 16)
            for side in range(2):
                sp.wait_ge(y_out.sems[side], y_out.total(NT // 2))

        @block.gpsimd
        def _(pool):
            nc.gpsimd.memset(proj2[:, :], 0.0).then_inc(zeroed.sem, 1)
            nc.gpsimd.memset(minus_half[:, :], -0.5)
            nc.gpsimd.memset(state[:, :, :], 0.0)
            nc.gpsimd.memset(v[:, :, :, DH:VW], 1.0)
            nc.gpsimd.memset(eps[:, :], EPS).then_inc(consts.sem, 1)
            pool.wait_ge(consts.sem, consts.at(0))

            def front(turn):
                i = turn.i
                pool.wait_ge(mv_ready.sem, mv_ready.at(i))
                nc.gpsimd.tensor_tensor(rstd[:, :], mv[:, :, 1], eps[:, :], ALU.add).then_inc(eps_added.sem, 1)
                pool.wait_ge(eps_added.sem, eps_added.at(i, 1))
                nc.gpsimd.tensor_tensor(rstd[:, :], rstd[:, :], minus_half[:, :], ALU.pow).then_inc(rstd_ready.sem, 1)
                pool.wait_ge(rstd_ready.sem, rstd_ready.at(i))
                nc.gpsimd.tensor_tensor(rstd2[:, :], mv[:, :, 1], rstd[:, :], ALU.mult).then_inc(eps_added.sem, 1)
                pool.wait_ge(eps_added.sem, eps_added.at(i, 2))
                nc.gpsimd.tensor_tensor(rstd2[:, :], rstd2[:, :], rstd[:, :], ALU.mult).then_inc(eps_added.sem, 1)
                pool.wait_ge(eps_added.sem, eps_added.at(i, 3))
                nc.gpsimd.tensor_tensor(rstd2[:, :], rstd2[:, :], eps[:, :], ALU.add).then_inc(eps_added.sem, 1)
                pool.wait_ge(eps_added.sem, eps_added.at(i, 4))
                nc.gpsimd.tensor_tensor(rstd2[:, :], rstd2[:, :], minus_half[:, :], ALU.pow).then_inc(rstd2_ready.sem, 1)

            def body(turn, before, more, more2):
                if more2:
                    front(Turn(turn.pair + 1, turn.side))

            front(Turn(0, 0))
            front(Turn(0, 1))
            trailing(pool, body)

        @block.scalar
        def _(act):
            give_credit(act, v_ready)
            give_credit(act, attnT_ready)
            for f in range(4 * KD):
                j, g, k = f // (2 * KD), f // KD % 2, f % KD
                act.wait_ge(folded.sem, folded.at(0, f + 1))
                nc.scalar.activation(wqk[:, j, k, g * 512:(g + 1) * 512], pa[f % 2][:, :], ACT.Copy).then_inc(folded_read.sem, 1)

            def grow(turn):
                for g in range(4):
                    act.wait_ge(proj_ready.sem, proj_ready.at(turn.i, g + 1))
                    act.wait_ge(phi_ready.sem, phi_ready.at(turn.i if g >= 2 else turn.i - 1, g - 1 if g >= 2 else g + 3))
                    nc.scalar.activation(grown[:, g % 2, :], pa[g % 2][:, :], ACT.Exp).then_inc(exp_ready.sem, 1)

            def values(turn, g):
                act.wait_ge(proj_ready.sem, proj_ready.at(turn.i, 5 + g))
                heads = H1 // 2
                nc.scalar.activation(v[:, turn.side, g * heads:(g + 1) * heads, 0:DH],
                                                pa[g][:, :].rearrange("p (h d) -> p h d", d=DH), ACT.Copy).then_inc(v_ready.sem, 1)

            def body(turn, before, more, more2):
                act.wait_ge(h_ready.sem, h_ready.at(turn.i))
                act.wait_ge(y_ready.sem, y_ready.at(turn.i - 1))
                nc.scalar.activation(h_keep[:, :], h[:, turn.side, :], ACT.Copy).then_inc(kept.sem, 1)
                act.wait_ge(keep_in.sems[turn.side], keep_in.at(turn))
                for g in range(2):
                    act.wait_ge(kt_ready.sem, kt_ready.at(turn.i, g + 1))
                    nc.scalar.activation(
                        k_rows[:, g * GP:(g + 1) * GP, :], pb[g][:, :].rearrange("p (r d) -> p r d", d=P), ACT.Copy,
                        scale=keep[:, turn.side, :]).then_inc(k_rows_ready.sem, 1)
                if more:
                    grow(turn.next())
                    values(turn.next(), 0)
                for g in range(2):
                    act.wait_ge(at_ready.sem, at_ready.at(turn.i, g + 1))
                    nc.scalar.activation(
                        attnT[:, g * GP:(g + 1) * GP, :], pb[g][:, :].rearrange("p (r t) -> p r t", t=P), ACT.Copy).then_inc(attnT_ready.sem, 1)
                if more:
                    values(turn.next(), 1)

            act.wait_ge(consts.sem, consts.at(0))
            grow(Turn(0, 0))
            values(Turn(0, 0), 0)
            values(Turn(0, 0), 1)
            trailing(act, body)

        @block.vector
        def _(dve):
            give_credit(dve, hT_ready, phi_ready, state_ready, y_ready, y_out)

            def statistics(turn):
                dve.wait_ge(x_in.sems[turn.side], x_in.at(turn))
                stats_of(nc, dve, x[:, turn.side, :, :], 1, sums, mv, sums_ready, mv_ready, turn.i)

            def front(turn):
                dve.wait_ge(rstd_ready.sem, rstd_ready.at(turn.i))
                nc.vector.tensor_scalar(h[:, turn.side, :], x[:, turn.side, 0, :], mv[:, 0, 0:1],
                                                   rstd[:, 0:1], ALU.subtract, ALU.mult).then_inc(h_ready.sem, 1)
                dve.wait_ge(h_ready.sem, h_ready.at(turn.i))
                dve.wait_ge(rstd2_ready.sem, rstd2_ready.at(turn.i))
                nc.vector.tensor_scalar(n[:, :], h[:, turn.side, :], rstd2[:, 0:1], None, ALU.mult).then_inc(n_ready.sem, 1)

            def hidden(turn):
                dve.wait_ge(tp_ready.sem, tp_ready.at(turn.i))
                for k in range(KD):
                    last = nc.vector.tensor_scalar(hT[:, k, :], pt[:, k * P:(k + 1) * P], gain[:, k:k + 1],
                                                   offset[:, k:k + 1], ALU.mult, ALU.add)
                last.then_inc(hT_ready.sem, 1)

            def features(turn):
                for g in range(4):
                    dve.wait_ge(exp_ready.sem, exp_ready.at(turn.i, g + 1))
                    nc.vector.tensor_scalar(grown[:, g % 2, :], grown[:, g % 2, :], 1.0, None, ALU.min).then_inc(min_ready.sem, 1)
                    dve.wait_ge(min_ready.sem, min_ready.at(turn.i, g + 1))
                    nc.vector.scalar_tensor_tensor(
                        qkT[:, turn.side, g // 2, g % 2 * GP:(g % 2 + 1) * GP, :],
                        pa[g % 2][:, :].rearrange("p (r t) -> p r t", t=P), 0.0,
                        grown[:, g % 2, :].rearrange("p (r t) -> p r t", t=P), ALU.max, ALU.add).then_inc(phi_ready.sem, 1)

            def residual(turn):
                dve.wait_ge(kept.sem, kept.at(turn.i))
                dve.wait_ge(out_ready.sem, out_ready.at(turn.i))
                dve.wait_ge(y_out.sems[turn.side], y_out.at(turn, back=1))
                nc.vector.tensor_tensor(y[:, turn.side, :], h_keep[:, :], pt[:, 0:D], ALU.add).then_inc(y_ready.sem, 1)

            def body(turn, before, more, more2):
                i = turn.i
                if before:
                    residual(turn.before())
                if more:
                    hidden(turn.next())
                for g in (2, 3, 0, 1):
                    dve.wait_ge(st_ready.sem, st_ready.at(i, (g + 2) % 4 + 1))
                    nc.vector.tensor_tensor(
                        scores[:, g // 2 * 2 * GP + g % 2:(g // 2 + 1) * 2 * GP:2, :],
                        score_banks[g][:, :].rearrange("p (r t) -> p r t", t=P),
                        causal[:, :].unsqueeze(1).to_broadcast([P, GP, P]), ALU.mult).then_inc(scores_ready.sem, 1)
                if more:
                    features(turn.next())
                if more2:
                    statistics(Turn(turn.pair + 1, turn.side))
                for c, (lo, hi) in enumerate(BANKS):
                    heads = 2 * (hi - lo)
                    bank = pc[c][:, 0:heads * VW].rearrange("p (h e) -> p h e", e=VW)
                    dve.wait_ge(num_ready.sem, num_ready.at(i, c + 1))
                    nc.vector.tensor_scalar(den[:, 2 * lo:2 * hi], bank[:, :, DH], 1e-6, None, ALU.add).then_inc(den_steps.sem, 1)
                    dve.wait_ge(den_steps.sem, den_steps.at(i, 2 * c + 1))
                    nc.vector.reciprocal(den[:, 2 * lo:2 * hi], den[:, 2 * lo:2 * hi]).then_inc(den_steps.sem, 1)
                    dve.wait_ge(den_steps.sem, den_steps.at(i, 2 * c + 2))
                    nc.vector.tensor_tensor(
                        attn[:, 2 * lo:2 * hi, :], bank[:, :, 0:DH],
                        den[:, 2 * lo:2 * hi].unsqueeze(2).to_broadcast([P, heads, DH]), ALU.mult).then_inc(attn_ready.sem, 1)
                dve.wait_ge(keep_in.sems[turn.side], keep_in.at(turn))
                for c, (lo, hi) in enumerate(BANKS):
                    dve.wait_ge(delta_ready.sem, delta_ready.at(i, c + 1))
                    for j in range(2):
                        half, cols = slice(j * DH, (j + 1) * DH), slice(j * VW, (j + 1) * VW)
                        bank = pc[c][half, 0:(hi - lo) * 2 * VW].rearrange("p (r e) -> p r e", e=2 * VW)
                        last = nc.vector.scalar_tensor_tensor(
                            state[half, lo:hi, cols], state[half, lo:hi, cols], keep[half, turn.side, :],
                            bank[:, :, cols], ALU.mult, ALU.add)
                    last.then_inc(state_ready.sem, 1)
                if more2:
                    dve.wait_ge(kept.sem, kept.at(i))
                    front(Turn(turn.pair + 1, turn.side))

            dve.wait_ge(own.loaded, own.total)
            dve.wait_ge(zeroed.sem, zeroed.at(0))
            for j in range(2):
                half = slice(j * DH, (j + 1) * DH)
                last = nc.vector.tensor_copy(proj2[half, half], own.proj[half, :])
            last.then_inc(proj_laid.sem, 1)
            dve.wait_ge(consts.sem, consts.at(0))
            statistics(Turn(0, 0))
            front(Turn(0, 0))
            hidden(Turn(0, 0))
            features(Turn(0, 0))
            statistics(Turn(0, 1))
            front(Turn(0, 1))
            trailing(dve, body)
            residual(Turn(NT // 2 - 1, 1))

        @block.tensor
        def _(pe):
            pe.wait_ge(own.loaded, own.total)
            pe.wait_ge(proj_laid.sem, proj_laid.at(0))
            for f in range(4 * KD):
                j, g, k = f // (2 * KD), f // KD % 2, f % KD
                if f >= 2:
                    pe.wait_ge(folded_read.sem, folded_read.at(0, f - 1))
                for r in range(GP):
                    last = nc.tensor.matmul(pa[f % 2][:, r * P:(r + 1) * P], wT[:, j, g * GP + r, k * P:(k + 1) * P],
                                            proj2[:, :], start=True, stop=True)
                last.then_inc(folded.sem, 1)
            pe.wait_ge(folded_read.sem, folded_read.at(0))

            def transposes(turn):
                pe.wait_ge(n_ready.sem, n_ready.at(turn.i))
                pe.wait_ge(hT_ready.sem, hT_ready.at(turn.i - 1))
                pe.wait_ge(y_ready.sem, y_ready.at(turn.i - 2))
                for k in range(KD):
                    last = nc.tensor.transpose(pt[:, k * P:(k + 1) * P], n[:, k * P:(k + 1) * P], ident)
                last.then_inc(tp_ready.sem, 1)

            def queries_keys(turn):
                pe.wait_ge(hT_ready.sem, hT_ready.at(turn.i))
                for g in range(4):
                    if g < 2:
                        pe.wait_ge(v_ready.sem, v_ready.at(turn.i - 1, g + 1))
                    else:
                        pe.wait_ge(phi_ready.sem, phi_ready.at(turn.i, g - 1))
                    for r in range(GP):
                        cols = slice((g % 2 * GP + r) * P, (g % 2 * GP + r + 1) * P)
                        for k in range(KD):
                            last = nc.tensor.matmul(pa[g % 2][:, r * P:(r + 1) * P], wqk[:, g // 2, k, cols],
                                                    hT[:, k, :], start=(k == 0), stop=(k == KD - 1))
                    last.then_inc(proj_ready.sem, 1)

            def values(turn, g):
                pe.wait_ge(phi_ready.sem, phi_ready.at(turn.i, 3 + g))
                for k in range(KD):
                    last = nc.tensor.matmul(pa[g][:, :], hT[:, k, :], wv[:, k, g * 512:(g + 1) * 512],
                                            start=(k == 0), stop=(k == KD - 1))
                last.then_inc(proj_ready.sem, 1)

            def scores_of(turn, g):
                i, side = turn.i, turn.side
                for j in range(2):
                    if g == 0:
                        pe.wait_ge(k_rows_ready.sem, k_rows_ready.at(i, j + 1))
                    else:
                        pe.wait_ge(state_ready.sem, state_ready.at(i - 1, j + 1))
                for a in range(GP):
                    for j in range(2):
                        half = slice(j * DH, (j + 1) * DH)
                        ins = nc.tensor.matmul(score_banks[2 * g + j][:, a * P:(a + 1) * P],
                                               qkT[half, side, 1, g * GP + a, :],
                                               qkT[half, side, 0, g * GP + a, :], start=True, stop=True)
                        if a == GP - 1:
                            ins.then_inc(st_ready.sem, 1)

            def body(turn, before, more, more2):
                i, side = turn.i, turn.side
                pe.wait_ge(phi_ready.sem, phi_ready.at(i))
                for g in range(2):
                    pe.wait_ge(attnT_ready.sem, attnT_ready.at(i - 1, g + 1))
                    for r in range(GP):
                        last = nc.tensor.transpose(pb[g][:, r * P:(r + 1) * P], qkT[:, side, 1, g * GP + r, :], ident)
                    last.then_inc(kt_ready.sem, 1)
                scores_of(turn, 1)
                if more:
                    transposes(turn.next())
                scores_of(turn, 0)
                if more:
                    queries_keys(turn.next())
                pe.wait_ge(v_ready.sem, v_ready.at(i))
                pe.wait_ge(scores_ready.sem, scores_ready.at(i))
                for c, (lo, hi) in enumerate(BANKS):
                    pe.wait_ge(state_ready.sem, state_ready.at(i - 1, c + 1))
                    for r in range(lo, hi):
                        at = (r - lo) * 2 * VW
                        nc.tensor.matmul(pc[c][:, at:at + 2 * VW], qkT[:, side, 0, r, :], state[:, r, :],
                                         start=True, stop=False, skip_group_check=True)
                        for j in range(2):
                            last = nc.tensor.matmul(pc[c][:, at + j * VW:at + (j + 1) * VW], scores[:, 2 * r + j, :],
                                                    v[:, side, 2 * r + j, :], start=False, stop=(j == 1),
                                                    skip_group_check=True)
                    last.then_inc(num_ready.sem, 1)
                pe.wait_ge(k_rows_ready.sem, k_rows_ready.at(i))
                for c, (lo, hi) in enumerate(BANKS):
                    pe.wait_ge(attn_ready.sem, attn_ready.at(i, c + 1))
                    for r in range(lo, hi):
                        at = (r - lo) * 2 * VW
                        for j in range(2):
                            last = nc.tensor.matmul(pc[c][j * DH:(j + 1) * DH, at + j * VW:at + (j + 1) * VW],
                                                    k_rows[:, r, j * DH:(j + 1) * DH],
                                                    v[:, side, 2 * r + j, :], start=True, stop=True)
                    last.then_inc(delta_ready.sem, 1)
                if more:
                    values(turn.next(), 0)
                pe.wait_ge(attn_ready.sem, attn_ready.at(i))
                for g in range(2):
                    pe.wait_ge(scores_ready.sem, scores_ready.at(i, 3 + g))
                    for r in range(GP):
                        at = 2 * (g * GP + r)
                        last = nc.tensor.transpose(pb[g][:, r * P:(r + 1) * P], attn[:, at:at + 2, :], ident)
                    last.then_inc(at_ready.sem, 1)
                if more:
                    values(turn.next(), 1)
                    pe.wait_ge(hT_ready.sem, hT_ready.at(turn.next().i))
                pe.wait_ge(attnT_ready.sem, attnT_ready.at(i))
                for r in range(PR):
                    last = nc.tensor.matmul(pt[:, 0:D], attnT[:, r, :], wo[:, r, :], start=(r == 0), stop=(r == PR - 1))
                last.then_inc(out_ready.sem, 1)

            transposes(Turn(0, 0))
            queries_keys(Turn(0, 0))
            values(Turn(0, 0), 0)
            values(Turn(0, 0), 1)
            trailing(pe, body)

class FfnWeights(Weights):

    def __init__(self, nc, memory, tag, glu, w):
        super().__init__(nc, memory, tag)
        self.w, self.glu, self.ff = w, glu, HID2 if glu else FF1
        self.total = 16 * (6 + 2 * (self.ff % P != 0) + 2 * glu)
        tiles = -(-self.ff // P)
        self.w1 = self.sb("w1", [P, KD, w["w1"].shape[1]])
        self.w2 = self.sb("w2", [P, tiles, D])
        self.b1 = self.sb("b1", [P, 2 if glu else 1, tiles])
        self.b2 = self.sb("b2", [P, D])
        self.gain, self.offset = self.sb("gain", [P, KD]), self.sb("offset", [P, KD])

    def load(self, sp):
        w, ff, n = self.w, self.ff, self.ff // P
        full = n * P
        sp.dma_start(self.w1[:, :, :], w["w1"].rearrange("(k p) n -> p k n", p=P)).then_inc(self.loaded, 16)
        sp.dma_start(self.w2[:, 0:n, :], w["w2"][0:full, :].rearrange("(m p) n -> p m n", p=P)).then_inc(self.loaded, 16)
        if ff > full:
            sp.dma_start(self.w2[0:ff - full, n, :], w["w2"][full:ff, :]).then_inc(self.loaded, 16)
        for g in range(1 + self.glu):
            part = w["b1"][g * ff:(g + 1) * ff]
            sp.dma_start(self.b1[:, g, 0:n], part[0:full].rearrange("(m p) -> p m", p=P),
                         allow_slow_non_contiguous=True).then_inc(self.loaded, 16)
            if ff > full:
                low = g * (P // 2)
                sp.dma_start(self.b1[low:low + ff - full, g, n:n + 1], part[full:ff].rearrange("(p a) -> p a", a=1))\
                  .then_inc(self.loaded, 16)
        sp.dma_start(self.b2[:, :], w["b2"].partition_broadcast(P)).then_inc(self.loaded, 16)
        for v, to in ((w["gain"], self.gain), (w["offset"], self.offset)):
            sp.dma_start(to[:, :], v.rearrange("(k p) -> p k", p=P),
                         allow_slow_non_contiguous=True).then_inc(self.loaded, 16)

def ffn_stage(nc, tag, glu, own, src, shift_src, add_src, out_flat, out_padded, norm_out, ident, upcoming):
    ff = HID2 if glu else FF1
    widths = [min(P, ff - m) for m in range(0, ff, P)]
    MT = len(widths)
    with ExitStack() as ctx:
        s = Scope(nc, ctx, tag)
        s.adopt(own)
        w1, w2, b1, b2, gain, offset = own.w1, own.w2, own.b1, own.b2, own.gain, own.offset
        minus_half, eps = s.sb("minus_half", [P, TB]), s.sb("eps", [P, TB])
        x = s.sb("x", [P, 2, TB, D])
        xs = s.sb("xs", [P, 2, TB, D]) if shift_src else x
        add = s.sb("add", [P, 2, TB, D]) if add_src is not None else None
        res = s.sb("res", [P, TB, D])
        sums = s.sb("sums", [P, TB, 6])
        mv = s.sb("mv", [P, TB, 2])
        rstd = s.sb("rstd", [P, TB])
        n = s.sb("n", [P, TB, D])
        hT = s.sb("hT", [P, KD, BLK])
        act = s.sb("act", [P, MT, BLK])
        gel = s.sb("gel", [P, 2, BLK]) if glu else None
        y = s.sb("y", [P, 2, TB, D])
        yn = s.sb("yn", [P, 2, TB, D]) if norm_out else None
        tp = [s.ps(f"tp{k}", [P, BLK]) for k in range(KD)]
        up = [s.ps(f"up{k}", [P, BLK]) for k in range(4)]
        dn = [s.ps(f"dn{k}", [P, BLK]) for k in range(2)]

        consts = s.counter("consts")
        x_in = s.transfer("x_in", per=1 + 2 * shift_src + (add_src is not None))
        sums_ready, mv_ready = s.counter("sums_ready", per=2), s.counter("mv_ready")
        eps_added, rstd_ready = s.counter("eps_added"), s.counter("rstd_ready")
        n_ready = s.counter("n_ready")
        tp_ready = s.counter("tp_ready")
        hT_ready = s.counter("hT_ready", credit=1)
        up_ready = s.counter("up_ready", per=MT)
        gel_ready = s.counter("gel_ready", per=MT) if glu else None
        act_ready = s.counter("act_ready", per=MT, credit=1)
        dn_ready = s.counter("dn_ready", per=TB, credit=1)
        res_part, res_ready = s.counter("res_part"), s.counter("res_ready")
        y_ready = s.counter("y_ready", per=TB, credit=2)
        y_out = s.transfer("y_out", per=(out_flat is not None) + (out_padded is not None and not norm_out), credit=1)
        if norm_out:
            ysums_ready, ymv_ready = s.counter("ysums_ready", per=2), s.counter("ymv_ready")
            yeps_added, yrstd_ready = s.counter("yeps_added"), s.counter("yrstd_ready")
            yn_ready = s.counter("yn_ready")
            yn_out = s.transfer("yn_out", credit=1)
            ysums, ymv, yrstd = s.sb("ysums", [P, TB, 6]), s.sb("ymv", [P, TB, 2]), s.sb("yrstd", [P, TB])
        block = ctx.enter_context(nc.Block())

        @block.sync
        def _(sp):
            def load(turn):
                if shift_src:
                    sp.dma_start(xs[:, turn.side, :, 0:D // 2], block_rows(src, turn)[:, :, 0:D // 2]).then_inc(x_in.sems[turn.side], 16)
                    sp.dma_start(xs[:, turn.side, :, D // 2:D],
                                         block_rows(src, turn, 1)[:, :, D // 2:D]).then_inc(x_in.sems[turn.side], 16)
                    sp.dma_start(x[:, turn.side, :, :], block_rows(src, turn)).then_inc(x_in.sems[turn.side], 16)
                else:
                    sp.dma_start(x[:, turn.side, :, :], flat_rows(src, turn)).then_inc(x_in.sems[turn.side], 16)
                if add_src is not None:
                    sp.dma_start(add[:, turn.side, :, :], flat_rows(add_src, turn)).then_inc(x_in.sems[turn.side], 16)

            load(Turn(0, 0))
            load(Turn(0, 1))
            if upcoming is not None:
                upcoming.load(sp)

            def store(turn):
                sp.wait_ge(y_ready.sem, y_ready.at(turn.i))
                if out_flat is not None:
                    sp.dma_start(flat_rows(out_flat, turn), y[:, turn.side, :, :]).then_inc(y_out.sems[turn.side], 16)
                if out_padded is not None and not norm_out:
                    sp.dma_start(block_rows(out_padded, turn), y[:, turn.side, :, :]).then_inc(y_out.sems[turn.side], 16)
                if norm_out:
                    sp.wait_ge(yn_ready.sem, yn_ready.at(turn.i))
                    sp.dma_start(block_rows(out_padded, turn), yn[:, turn.side, :, :]).then_inc(yn_out.sems[turn.side], 16)

            with sp.Fori(0, NBLK // 2 - 1) as pair:
                for side in range(2):
                    sp.wait_ge(res_ready.sem, res_ready.at(Turn(pair, side).i))
                    sp.wait_ge(n_ready.sem, n_ready.at(Turn(pair, side).i))
                    load(Turn(pair + 1, side))
                    store(Turn(pair, side))
            for side in range(2):
                store(Turn(NBLK // 2 - 1, side))
            for side in range(2):
                sp.wait_ge(y_out.sems[side], y_out.total(NBLK // 2))
            if norm_out:
                for side in range(2):
                    sp.wait_ge(yn_out.sems[side], yn_out.total(NBLK // 2))

        @block.gpsimd
        def _(pool):
            nc.gpsimd.memset(minus_half[:, :], -0.5)
            nc.gpsimd.memset(eps[:, :], EPS).then_inc(consts.sem, 1)
            pool.wait_ge(consts.sem, consts.at(0))
            def front(turn):
                rstd_of(nc, pool, mv, rstd, eps, minus_half, TB, mv_ready, eps_added, rstd_ready, turn.i)

            def body(turn, more):
                if more:
                    front(turn.next())
                pool.wait_ge(x_in.sems[turn.side], x_in.at(turn))
                pool.wait_ge(y_ready.sem, y_ready.at(turn.i - 1))
                b2_all = b2[:, :].unsqueeze(1).to_broadcast([P, TB, D])
                first = nc.gpsimd.tensor_tensor(res[:, :, :], x[:, turn.side, :, :], b2_all, ALU.add)
                if add is None:
                    first.then_inc(res_ready.sem, 1)
                else:
                    first.then_inc(res_part.sem, 1)
                    pool.wait_ge(res_part.sem, res_part.at(turn.i))
                    nc.gpsimd.tensor_tensor(res[:, :, :], res[:, :, :], add[:, turn.side, :, :], ALU.add).then_inc(res_ready.sem, 1)
                if norm_out:
                    rstd_of(nc, pool, ymv, yrstd, eps, minus_half, TB, ymv_ready, yeps_added, yrstd_ready, turn.i)

            front(Turn(0, 0))
            pool.wait_ge(own.loaded, own.total)
            turns(pool, NBLK, body)

        @block.scalar
        def _(act_eng):
            if not glu:
                give_credit(act_eng, act_ready)
            act_eng.wait_ge(own.loaded, own.total)

            def body(turn, more):
                for m, width in enumerate(widths):
                    if glu:
                        act_eng.wait_ge(up_ready.sem, up_ready.at(turn.i, m + 1))
                        if m >= 2:
                            act_eng.wait_ge(act_ready.sem, act_ready.at(turn.i, m - 1))
                        else:
                            act_eng.wait_ge(act_ready.sem, act_ready.at(turn.i - 1, MT - 1 + m))
                        low = P // 2 if width < P else 0
                        bank = up[2 * (m % 2) + (width == P)]
                        nc.scalar.activation(gel[0:width, m % 2, :], bank[low:low + width, :],
                                             ACT.Gelu, bias=b1[low:low + width, 1, m:m + 1]).then_inc(gel_ready.sem, 1)
                    else:
                        act_eng.wait_ge(up_ready.sem, up_ready.at(turn.i, m + 1))
                        if m == 0:
                            act_eng.wait_ge(dn_ready.sem, dn_ready.at(turn.i - 1))
                        nc.scalar.activation(act[0:width, m, :], up[m % 4][0:width, :],
                                                          ACT.Gelu, bias=b1[0:width, 0, m:m + 1]).then_inc(act_ready.sem, 1)
            turns(act_eng, NBLK, body)

        @block.vector
        def _(dve):
            give_credit(dve, y_ready, hT_ready)
            if glu:
                give_credit(dve, act_ready)
            give_credit(dve, y_out)
            if norm_out:
                give_credit(dve, yn_out)

            def front(turn):
                dve.wait_ge(x_in.sems[turn.side], x_in.at(turn))
                stats_of(nc, dve, xs[:, turn.side, :, :], TB, sums, mv, sums_ready, mv_ready, turn.i)
                dve.wait_ge(rstd_ready.sem, rstd_ready.at(turn.i))
                normalise(nc, n, xs[:, turn.side, :, :], mv, rstd, TB).then_inc(n_ready.sem, 1)

            def hidden(turn):
                dve.wait_ge(tp_ready.sem, tp_ready.at(turn.i))
                for k in range(KD):
                    last = nc.vector.tensor_scalar(hT[:, k, :], tp[k][:, :], gain[:, k:k + 1], offset[:, k:k + 1],
                                                   ALU.mult, ALU.add)
                last.then_inc(hT_ready.sem, 1)

            def body(turn, more):
                if more:
                    front(turn.next())
                if glu:
                    for m, width in enumerate(widths):
                        dve.wait_ge(gel_ready.sem, gel_ready.at(turn.i, m + 1))
                        if m == 0:
                            dve.wait_ge(dn_ready.sem, dn_ready.at(turn.i - 1))
                        nc.vector.scalar_tensor_tensor(
                            act[0:width, m, :], up[2 * (m % 2)][0:width, :], b1[0:width, 0, m:m + 1],
                            gel[0:width, m % 2, :], ALU.add, ALU.mult).then_inc(act_ready.sem, 1)
                if more:
                    hidden(turn.next())
                dve.wait_ge(res_ready.sem, res_ready.at(turn.i))
                dve.wait_ge(y_out.sems[turn.side], y_out.at(turn, back=1))
                for t in range(TB):
                    dve.wait_ge(dn_ready.sem, dn_ready.at(turn.i, t + 1))
                    nc.vector.tensor_tensor(y[:, turn.side, t, :], res[:, t, :], dn[t % 2][:, 0:D], ALU.add).then_inc(y_ready.sem, 1)
                if norm_out:
                    dve.wait_ge(y_ready.sem, y_ready.at(turn.i))
                    stats_of(nc, dve, y[:, turn.side, :, :], TB, ysums, ymv, ysums_ready, ymv_ready, turn.i)
                    dve.wait_ge(yrstd_ready.sem, yrstd_ready.at(turn.i))
                    dve.wait_ge(yn_out.sems[turn.side], yn_out.at(turn, back=1))
                    normalise(nc, yn[:, turn.side, :, :], y[:, turn.side, :, :], ymv, yrstd, TB).then_inc(yn_ready.sem, 1)

            front(Turn(0, 0))
            dve.wait_ge(own.loaded, own.total)
            hidden(Turn(0, 0))
            turns(dve, NBLK, body)

        @block.tensor
        def _(pe):
            give_credit(pe, dn_ready)

            def transposes(turn):
                pe.wait_ge(n_ready.sem, n_ready.at(turn.i))
                pe.wait_ge(hT_ready.sem, hT_ready.at(turn.i - 1))
                for k in range(KD):
                    for t in range(TB):
                        last = nc.tensor.transpose(tp[k][:, t * P:(t + 1) * P], n[:, t, k * P:(k + 1) * P], ident)
                last.then_inc(tp_ready.sem, 1)

            def body(turn, more):
                pe.wait_ge(hT_ready.sem, hT_ready.at(turn.i))
                for m, width in enumerate(widths):
                    depth = 2 if glu else 4
                    if m >= depth:
                        pe.wait_ge(act_ready.sem, act_ready.at(turn.i, m - depth + 1))
                    else:
                        pe.wait_ge(act_ready.sem, act_ready.at(turn.i - 1, MT - depth + 1 + m))
                    if glu and width < P:
                        assert width <= P // 2
                        for k in range(KD):
                            for g in range(2):
                                last = nc.tensor.matmul(up[2 * (m % 2)][g * P // 2:g * P // 2 + width, :],
                                                        w1[:, k, g * ff + m * P:g * ff + m * P + width],
                                                        hT[:, k, :], start=(k == 0), stop=(k == KD - 1))
                    for g in range(1 + glu if width == P else 0):
                        bank = up[2 * (m % 2) + g] if glu else up[m % 4]
                        for k in range(KD):
                            last = nc.tensor.matmul(bank[:, :], w1[:, k, g * ff + m * P:g * ff + (m + 1) * P],
                                                    hT[:, k, :], start=(k == 0), stop=(k == KD - 1))
                    last.then_inc(up_ready.sem, 1)
                if more:
                    transposes(turn.next())
                pe.wait_ge(act_ready.sem, act_ready.at(turn.i, MT - 1))
                for t in range(TB):
                    if t >= 2:
                        pe.wait_ge(y_ready.sem, y_ready.at(turn.i, t - 1))
                    else:
                        pe.wait_ge(y_ready.sem, y_ready.at(turn.i - 1, TB - 1 + t))
                    for m, width in enumerate(widths):
                        if t == 0 and m == MT - 1:
                            pe.wait_ge(act_ready.sem, act_ready.at(turn.i))
                        last = nc.tensor.matmul(dn[t % 2][:, 0:D], act[0:width, m, t * P:(t + 1) * P],
                                                w2[0:width, m, :], start=(m == 0), stop=(m == MT - 1))
                    last.then_inc(dn_ready.sem, 1)

            pe.wait_ge(own.loaded, own.total)
            transposes(Turn(0, 0))
            turns(pe, NBLK, body)

class WindowConstants(Weights):

    def __init__(self, nc, memory, tag, w):
        super().__init__(nc, memory, tag)
        self.w, self.total = w, 16 * 3
        self.ident16 = self.sb("ident16", [P, P], BF16)
        self.even = self.sb("even", [P, NT // 2, 2 * P], BF16)
        self.odd = self.sb("odd", [P, 2 * P], BF16)

    def load(self, sp):
        w = self.w
        sp.dma_start(self.ident16[:, :], w["ident16"]).then_inc(self.loaded, 16)
        sp.dma_start(self.even[:, :, :], w["mask_even"].rearrange("p (a n) -> p a n", n=2 * P)).then_inc(self.loaded, 16)
        sp.dma_start(self.odd[:, :], w["mask_odd"]).then_inc(self.loaded, 16)

class WindowWeights(Weights):
    def __init__(self, nc, memory, tag, w, shared, first):
        super().__init__(nc, memory, tag)
        self.w, self.total, self.shared, self.first = w, 16 * 8, shared, first
        self.wqkv = self.sb("wqkv", [P, KD, 3 * INNER])
        self.wo = self.sb("wo", [P, H2 // 2, D])
        self.scales = self.sb("scales", [P, 4 * DH])

    def load(self, sp):
        w = self.w
        if self.first:
            self.shared.load(sp)
        sp.dma_start(self.wqkv[:, :, :], w["wqkv"].rearrange("(k p) n -> p k n", p=P)).then_inc(self.loaded, 16)
        sp.dma_start(self.wo[:, :, :], w["wo"].rearrange("(r p) n -> p r n", p=P)).then_inc(self.loaded, 16)
        for at, vec in ((0, "q_scale"), (1, "k_scale")):
            sp.dma_start(self.scales[:, at * DH:(at + 1) * DH], w[vec].partition_broadcast(P)).then_inc(self.loaded, 16)
            for j in range(2):
                to = (2 + at) * DH + j * (DH // 2)
                sp.dma_start(self.scales[:, to:to + DH // 2],
                             w[vec][(1 - j) * (DH // 2):(2 - j) * (DH // 2)].partition_broadcast(P))\
                  .then_inc(self.loaded, 16)

def window_attention_stage(nc, tag, own, src, dst, ident, upcoming):
    PR = H2 // 2
    with ExitStack() as ctx:
        s = Scope(nc, ctx, tag)
        s.adopt(own)
        wqkv, wo, scales = own.wqkv, own.wo, own.scales
        ident16, mask_even, mask_odd = own.shared.ident16, own.shared.even, own.shared.odd
        minus_half = s.sb("minus_half", [P, H2])
        x, xs = s.sb("x", [P, 2, D]), s.sb("xs", [P, 2, D])
        raw, table = s.sb("raw", [P, 2, 4 * DH]), s.sb("table", [P, 2, 4 * DH])
        hT = s.sb("hT", [P, KD, P])
        squares = s.sb("squares", [P, 2, INNER])
        ss, rn = s.sb("ss", [P, 2, H2]), s.sb("rn", [P, 2, 2, H2])
        straight, turned = s.sb("straight", [P, 2, INNER]), s.sb("turned", [P, 2, INNER])
        rotated = s.sb("rotated", [P, 2, INNER])
        k_unit = s.sb("k_unit", [P, INNER])
        qT = s.sb("qT", [P, PR, P])
        kT = s.sb("kT", [P, PR, 2, P])
        v = s.sb("v", [P, 2, H2, DH])
        highest, nbias = s.sb("highest", [P, 2, 2, 2]), s.sb("nbias", [P, 2, 2, 2])
        probs = s.sb("probs", [P, H2, 2 * P])
        den, rden = s.sb("den", [P, H2]), s.sb("rden", [P, H2])
        probsT = s.sb("probsT", [P, H2, 2, P])
        rden_rows = s.sb("rden_rows", [P, PR, P])
        oT = s.sb("oT", [P, PR, P])
        y = s.sb("y", [P, 2, D])
        pa = [s.ps(f"pa{k}", [P, 512]) for k in range(2)]
        sc = [s.ps(f"sc{k}", [P, 2, 2 * P]) for k in range(2)]
        pp = [s.ps(f"pp{k}", [P, 512]) for k in range(2)]
        po = s.ps("po", [P, 512])
        pt = s.ps("pt", [P, 512])

        consts = s.counter("consts")
        x_in, res_in = s.transfer("x_in", per=3), s.transfer("res_in")
        table_ready = s.counter("table_ready")
        tp_ready, hT_ready = s.counter("tp_ready"), s.counter("hT_ready", credit=1)
        proj_ready, sq_ready = s.counter("proj_ready", per=3), s.counter("sq_ready", per=2, credit=1)
        ss_steps, rn_ready = s.counter("ss_steps", per=4, credit=1), s.counter("rn_ready", per=2, credit=1)
        rot_ready, sum_ready = s.counter("rot_ready", per=2, credit=1), s.counter("sum_ready", per=2, credit=1)
        k_unit_ready = s.counter("k_unit_ready")
        v_ready = s.counter("v_ready", credit=1)
        qkt_ready = s.counter("qkt_ready", per=2, credit=1)
        qT_ready, kT_ready = s.counter("qT_ready"), s.counter("kT_ready")
        st_ready, max_ready, nb_ready = s.counter("st_ready", per=4), s.counter("max_ready", per=4), s.counter("nb_ready", per=2)
        exp_ready = s.counter("exp_ready", per=8, credit=1)
        pt_ready = s.counter("pt_ready", per=4)
        p_even, p_odd = s.counter("p_even", per=2), s.counter("p_odd", per=2)
        ot_made, rden_ready, oT_ready = s.counter("ot_made"), s.counter("rden_ready"), s.counter("oT_ready", credit=1)
        spread_made, rows_ready = s.counter("spread_made"), s.counter("rows_ready", credit=1)
        out_ready, y_ready = s.counter("out_ready"), s.counter("y_ready", credit=3)
        y_out = s.transfer("y_out", credit=1)
        block = ctx.enter_context(nc.Block())

        @block.sync
        def _(sp):
            def row(turn):
                at = turn.i * P + turn.pair // (NT // 2 // B)
                return at if isinstance(at, int) else sp.snap(at)

            def load(turn):
                at = row(turn)
                return [(xs[:, turn.side, 0:D // 2], src[bass.ds(at + 1, P), 0:D // 2]),
                        (xs[:, turn.side, D // 2:D], src[bass.ds(at, P), D // 2:D]),
                        (raw[:, turn.side, :], own.w["tables"][bass.ds(turn.i * P, P), :])]

            def start(turn, copies):
                for to, frm in copies:
                    sp.dma_start(to, frm).then_inc(x_in.sems[turn.side], 16)

            def start_residual(turn):
                sp.dma_start(x[:, turn.side, :], src[bass.ds(row(turn) + 1, P), :]).then_inc(res_in.sems[turn.side], 16)

            def store(turn):
                sp.dma_start(dst[bass.ds(row(turn) + 1, P), :], y[:, turn.side, :]).then_inc(y_out.sems[turn.side], 16)

            for first in (Turn(0, 0), Turn(0, 1)):
                start(first, load(first))
                start_residual(first)
            upcoming.load(sp)

            def body(turn, before, more, more2):
                if more2:
                    sp.wait_ge(tp_ready.sem, tp_ready.at(turn.i))
                    sp.wait_ge(table_ready.sem, table_ready.at(turn.i))
                    start(Turn(turn.pair + 1, turn.side), load(Turn(turn.pair + 1, turn.side)))
                if before:
                    sp.wait_ge(y_ready.sem, y_ready.at(turn.i - 1))
                    store(turn.before())
                    if more:
                        start_residual(turn.next())

            trailing(sp, body)
            sp.wait_ge(y_ready.sem, y_ready.at(NT - 1))
            store(Turn(NT // 2 - 1, 1))
            for side in range(2):
                sp.wait_ge(y_out.sems[side], y_out.total(NT // 2))

        @block.gpsimd
        def _(pool):
            give_credit(pool, sum_ready, rn_ready)
            nc.gpsimd.memset(kT[:, :, :, :], 0.0)
            nc.gpsimd.memset(v[:, :, :, :], 0.0)
            nc.gpsimd.memset(minus_half[:, :], -0.5).then_inc(consts.sem, 1)
            pool.wait_ge(consts.sem, consts.at(0))

            def front(turn):
                pool.wait_ge(x_in.sems[turn.side], x_in.at(turn))
                nc.gpsimd.tensor_tensor(table[:, turn.side, :], raw[:, turn.side, :], scales[:, :],
                                                       ALU.mult).then_inc(table_ready.sem, 1)

            def rotation(turn):
                for j in range(2):
                    pool.wait_ge(rot_ready.sem, rot_ready.at(turn.i, j + 1))
                    pool.wait_ge(qkt_ready.sem, qkt_ready.at(turn.i - 1, j + 1))
                    nc.gpsimd.tensor_tensor(rotated[:, j, :], straight[:, j, :], turned[:, j, :], ALU.add).then_inc(sum_ready.sem, 1)
                    pool.wait_ge(ss_steps.sem, ss_steps.at(turn.i, 2 * j + 2))
                    nc.gpsimd.tensor_tensor(rn[:, turn.side, j, :], ss[:, j, :], minus_half[:, :], ALU.pow).then_inc(rn_ready.sem, 1)

            def body(turn, before, more, more2):
                if more:
                    rotation(turn.next())
                if more2:
                    front(Turn(turn.pair + 1, turn.side))

            pool.wait_ge(own.loaded, own.total)
            front(Turn(0, 0))
            rotation(Turn(0, 0))
            front(Turn(0, 1))
            trailing(pool, body)

        @block.scalar
        def _(act):
            give_credit(act, hT_ready, sq_ready, v_ready, exp_ready, rows_ready)
            act.wait_ge(consts.sem, consts.at(0))

            def hidden(turn):
                act.wait_ge(tp_ready.sem, tp_ready.at(turn.i))
                nc.scalar.activation(hT[:, :, :], pt[:, 0:KD * P].rearrange("p (k t) -> p k t", t=P), ACT.Copy).then_inc(hT_ready.sem, 1)

            def square(turn, j):
                act.wait_ge(proj_ready.sem, proj_ready.at(turn.i, j + 1))
                act.wait_ge(ss_steps.sem, ss_steps.at(turn.i - 1, 2 * j + 1))
                nc.scalar.activation(squares[:, j, :], pa[j][:, :], ACT.Square).then_inc(sq_ready.sem, 1)

            def queries(turn):
                act.wait_ge(qkt_ready.sem, qkt_ready.at(turn.i, 1))
                nc.scalar.activation(qT[:, :, :], pp[0][:, :].rearrange("p (r t) -> p r t", t=P), ACT.Copy).then_inc(qT_ready.sem, 1)

            def values(turn):
                act.wait_ge(proj_ready.sem, proj_ready.at(turn.i, 3))
                nc.scalar.activation(v[:, turn.side, :, :], pa[0][:, :].rearrange("p (h d) -> p h d", d=DH),
                                                ACT.Copy).then_inc(v_ready.sem, 1)

            def exps(turn, g, j):
                act.wait_ge(nb_ready.sem, nb_ready.at(turn.i, g + 1))
                for r in range(2):
                    head = 4 * g + 2 * r + j
                    nc.scalar.activation(
                        probs[:, head, :], sc[j][:, r, :], ACT.Exp, bias=nbias[:, g, j, r:r + 1],
                        scale=rn[:, turn.side, 0, head:head + 1], accum_out=den[:, head:head + 1]).then_inc(exp_ready.sem, 1)

            def columns(turn, g):
                act.wait_ge(pt_ready.sem, pt_ready.at(turn.i, 2 * g + 1))
                nc.scalar.activation(probsT[:, 4 * g:4 * g + 4:2, :, :],
                                               pp[0][:, :].rearrange("p (r s t) -> p r s t", r=2, t=P), ACT.Copy).then_inc(p_even.sem, 1)

            def reciprocal_rows(turn):
                act.wait_ge(spread_made.sem, spread_made.at(turn.i))
                nc.scalar.activation(rden_rows[:, :, :], pp[0][:, :].rearrange("p (r t) -> p r t", t=P),
                                     ACT.Copy).then_inc(rows_ready.sem, 1)

            def body(turn, before, more, more2):
                if more:
                    hidden(turn.next())
                if before:
                    act.wait_ge(ot_made.sem, ot_made.at(turn.i - 1))
                    values(turn)
                exps(turn, 0, 0)
                if before:
                    reciprocal_rows(turn.before())
                if more:
                    square(turn.next(), 0)
                exps(turn, 0, 1)
                if more:
                    square(turn.next(), 1)
                columns(turn, 0)
                exps(turn, 1, 0)
                exps(turn, 1, 1)
                columns(turn, 1)
                if more:
                    queries(turn.next())

            first = Turn(0, 0)
            hidden(first)
            square(first, 0)
            square(first, 1)
            queries(first)
            values(first)
            trailing(act, body)
            reciprocal_rows(Turn(NT // 2 - 1, 1))

        @block.vector
        def _(dve):
            give_credit(dve, ss_steps, rot_ready, oT_ready, y_ready, y_out)
            dve.wait_ge(consts.sem, consts.at(0))

            def rotate(turn, j):
                dve.wait_ge(sq_ready.sem, sq_ready.at(turn.i, j + 1))
                dve.wait_ge(table_ready.sem, table_ready.at(turn.i))
                dve.wait_ge(sum_ready.sem, sum_ready.at(turn.i - 1, j + 1))
                half = DH // 2

                def of_table(at, width):
                    return table[:, turn.side, at:at + width].unsqueeze(1).to_broadcast([P, H2, width])

                def heads(a):
                    return a.rearrange("p (h d) -> p h d", d=DH)

                nc.vector.tensor_tensor(heads(straight[:, j, :]), heads(pa[j][:, :]), of_table(j * DH, DH), ALU.mult)
                for a in range(2):
                    last = nc.vector.tensor_tensor(heads(turned[:, j, :])[:, :, a * half:(a + 1) * half],
                                                   heads(pa[j][:, :])[:, :, (1 - a) * half:(2 - a) * half],
                                                   of_table((2 + j) * DH + a * half, half), ALU.mult)
                last.then_inc(rot_ready.sem, 1)
                if j == 0:
                    dve.wait_ge(rn_ready.sem, rn_ready.at(turn.i - 1))
                nc.vector.tensor_reduce(ss[:, j, :], heads(squares[:, j, :]), AX.X, ALU.add).then_inc(ss_steps.sem, 1)
                dve.wait_ge(ss_steps.sem, ss_steps.at(turn.i, 2 * j + 1))
                nc.vector.tensor_scalar(ss[:, j, :], ss[:, j, :], 1e-24, None, ALU.max).then_inc(ss_steps.sem, 1)

            def unit_keys(turn):
                dve.wait_ge(rn_ready.sem, rn_ready.at(turn.i))
                dve.wait_ge(sum_ready.sem, sum_ready.at(turn.i))
                nc.vector.tensor_tensor(
                    k_unit[:, :].rearrange("p (h d) -> p h d", d=DH),
                    rotated[:, 1, :].rearrange("p (h d) -> p h d", d=DH),
                    rn[:, turn.side, 1, :].unsqueeze(2).to_broadcast([P, H2, DH]), ALU.mult).then_inc(k_unit_ready.sem, 1)

            def maxima(turn, g):
                for j in range(2):
                    dve.wait_ge(st_ready.sem, st_ready.at(turn.i, 2 * g + j + 1))
                    nc.vector.tensor_reduce(highest[:, g, j, :], sc[j][:, :, :], AX.X, ALU.max).then_inc(max_ready.sem, 1)
                dve.wait_ge(rn_ready.sem, rn_ready.at(turn.i))
                dve.wait_ge(max_ready.sem, max_ready.at(turn.i, 2 * g + 2))
                nc.vector.scalar_tensor_tensor(
                    nbias[:, g, :, :], highest[:, g, :, :], -1.0,
                    rn[:, turn.side, 0, 4 * g:4 * g + 4].rearrange("p (r j) -> p j r", j=2), ALU.mult, ALU.mult).then_inc(nb_ready.sem, 1)

            def columns(turn, g):
                dve.wait_ge(pt_ready.sem, pt_ready.at(turn.i, 2 * g + 2))
                nc.vector.tensor_copy(probsT[:, 4 * g + 1:4 * g + 4:2, :, :],
                                               pp[1][:, :].rearrange("p (r s t) -> p r s t", r=2, t=P)).then_inc(p_odd.sem, 1)

            def keys(turn):
                dve.wait_ge(qkt_ready.sem, qkt_ready.at(turn.i, 2))
                nc.vector.tensor_copy(kT[:, :, turn.side, :], pp[1][:, :].rearrange("p (r t) -> p r t", t=P)).then_inc(kT_ready.sem, 1)

            def output(turn):
                dve.wait_ge(ot_made.sem, ot_made.at(turn.i))
                dve.wait_ge(rows_ready.sem, rows_ready.at(turn.i))
                nc.vector.tensor_tensor(oT[:, :, :], po[:, :].rearrange("p (r t) -> p r t", t=P),
                                        rden_rows[:, :, :], ALU.mult).then_inc(oT_ready.sem, 1)

            def residual(turn):
                dve.wait_ge(out_ready.sem, out_ready.at(turn.i))
                dve.wait_ge(res_in.sems[turn.side], res_in.at(turn))
                dve.wait_ge(y_out.sems[turn.side], y_out.at(turn, back=1))
                nc.vector.tensor_tensor(y[:, turn.side, :], x[:, turn.side, :], pt[:, 0:D], ALU.add).then_inc(y_ready.sem, 1)

            def body(turn, before, more, more2):
                i = turn.i
                maxima(turn, 0)
                if more:
                    rotate(turn.next(), 0)
                if before:
                    output(turn.before())
                maxima(turn, 1)
                if more:
                    rotate(turn.next(), 1)
                columns(turn, 0)
                if before:
                    residual(turn.before())
                columns(turn, 1)
                if more:
                    unit_keys(turn.next())
                dve.wait_ge(exp_ready.sem, exp_ready.at(i))
                nc.vector.reciprocal(rden[:, :], den[:, :]).then_inc(rden_ready.sem, 1)
                if more:
                    keys(turn.next())

            first = Turn(0, 0)
            rotate(first, 0)
            rotate(first, 1)
            unit_keys(first)
            keys(first)
            trailing(dve, body)
            output(Turn(NT // 2 - 1, 1))
            residual(Turn(NT // 2 - 1, 1))

        @block.tensor
        def _(pe):
            give_credit(pe, qkt_ready)
            pe.wait_ge(own.loaded, own.total)
            pe.wait_ge(own.shared.loaded, own.shared.total)
            pe.wait_ge(consts.sem, consts.at(0))

            def transposes(turn):
                pe.wait_ge(x_in.sems[turn.side], x_in.at(turn))
                pe.wait_ge(hT_ready.sem, hT_ready.at(turn.i - 1))
                pe.wait_ge(y_ready.sem, y_ready.at(turn.i - 3))
                for k in range(KD):
                    last = nc.tensor.transpose(pt[:, k * P:(k + 1) * P], xs[:, turn.side, k * P:(k + 1) * P], ident)
                last.then_inc(tp_ready.sem, 1)

            def project(turn, g):
                bank = pa[g % 2]
                pe.wait_ge(hT_ready.sem, hT_ready.at(turn.i))
                if g == 0:
                    pe.wait_ge(v_ready.sem, v_ready.at(turn.i - 1))
                elif g == 1:
                    pe.wait_ge(rot_ready.sem, rot_ready.at(turn.i - 1, 2))
                    pe.wait_ge(sq_ready.sem, sq_ready.at(turn.i - 1, 2))
                else:
                    pe.wait_ge(rot_ready.sem, rot_ready.at(turn.i, 1))
                    pe.wait_ge(sq_ready.sem, sq_ready.at(turn.i, 1))
                for k in range(KD):
                    last = nc.tensor.matmul(bank[:, :], hT[:, k, :], wqkv[:, k, g * INNER:(g + 1) * INNER],
                                            start=(k == 0), stop=(k == KD - 1))
                last.then_inc(proj_ready.sem, 1)

            def scores(turn, g):
                i = turn.i
                if g == 0:
                    pe.wait_ge(qT_ready.sem, qT_ready.at(i))
                    pe.wait_ge(kT_ready.sem, kT_ready.at(i))
                for j in range(2):
                    if g == 0:
                        pe.wait_ge(exp_ready.sem, exp_ready.at(i - 1, 6 + 2 * j))
                    else:
                        pe.wait_ge(exp_ready.sem, exp_ready.at(i, 2 + 2 * j))
                mask = mask_odd[:, :] if turn.side else mask_even[:, bass.ds(turn.pair, 1), :].squeeze(1)
                for r in range(2):
                    for j in range(2):
                        nc.tensor.matmul(sc[j][:, r, :], ident16[:, :], mask, start=True, stop=False,
                                         skip_group_check=True)
                    for j in range(2):
                        half = slice(j * DH, (j + 1) * DH)
                        ins = nc.tensor.matmul(sc[j][:, r, :], qT[half, 2 * g + r, :], kT[half, 2 * g + r, :, :],
                                               start=False, stop=True, skip_group_check=True)
                        if r == 1:
                            ins.then_inc(st_ready.sem, 1)

            def columns(turn, g):
                i = turn.i
                for j in range(2):
                    pe.wait_ge(exp_ready.sem, exp_ready.at(i, 4 * g + 2 * j + 2))
                    if g:
                        read = p_odd if j else p_even
                        pe.wait_ge(read.sem, read.at(i, 1))
                    elif j:
                        pe.wait_ge(kT_ready.sem, kT_ready.at(i))
                    else:
                        pe.wait_ge(rows_ready.sem, rows_ready.at(i - 1))
                    for r in range(2):
                        for sd in range(2):
                            at = (2 * r + sd) * P
                            last = nc.tensor.transpose(pp[j][:, at:at + P],
                                                       probs[:, 4 * g + 2 * r + j, sd * P:(sd + 1) * P], ident)
                    last.then_inc(pt_ready.sem, 1)

            def heads_to_rows(turn, previous):
                pe.wait_ge(sum_ready.sem, sum_ready.at(turn.i, 1))
                if previous is not None:
                    pe.wait_ge(p_even.sem, p_even.at(previous.i))
                for r in range(PR):
                    last = nc.tensor.transpose(pp[0][:, r * P:(r + 1) * P], rotated[:, 0, r * P:(r + 1) * P], ident)
                last.then_inc(qkt_ready.sem, 1)
                pe.wait_ge(k_unit_ready.sem, k_unit_ready.at(turn.i))
                if previous is not None:
                    pe.wait_ge(p_odd.sem, p_odd.at(previous.i))
                for r in range(PR):
                    last = nc.tensor.transpose(pp[1][:, r * P:(r + 1) * P], k_unit[:, r * P:(r + 1) * P], ident)
                last.then_inc(qkt_ready.sem, 1)

            def weighted(turn, g):
                i = turn.i
                pe.wait_ge(p_even.sem, p_even.at(i, g + 1))
                pe.wait_ge(p_odd.sem, p_odd.at(i, g + 1))
                if g == 0:
                    pe.wait_ge(v_ready.sem, v_ready.at(i))
                    pe.wait_ge(oT_ready.sem, oT_ready.at(i - 1))
                for r in (2 * g, 2 * g + 1):
                    for sd in range(2):
                        for j in range(2):
                            last = nc.tensor.matmul(po[j * DH:(j + 1) * DH, r * P:(r + 1) * P], v[:, sd, 2 * r + j, :],
                                                    probsT[:, 2 * r + j, sd, :], start=(sd == 0), stop=(sd == 1))
                if g:
                    last.then_inc(ot_made.sem, 1)

            def spread_reciprocals(turn, more):
                pe.wait_ge(rden_ready.sem, rden_ready.at(turn.i))
                if more:
                    pe.wait_ge(qT_ready.sem, qT_ready.at(turn.i + 1))
                for r in range(PR):
                    for j in range(2):
                        last = nc.tensor.matmul(pp[0][j * DH:(j + 1) * DH, r * P:(r + 1) * P],
                                                rden[:, 2 * r + j:2 * r + j + 1].to_broadcast([P, DH]), ident,
                                                start=True, stop=True)
                last.then_inc(spread_made.sem, 1)

            def output(turn, hidden):
                pe.wait_ge(oT_ready.sem, oT_ready.at(turn.i))
                pe.wait_ge(y_ready.sem, y_ready.at(turn.i - 1))
                if hidden is not None:
                    pe.wait_ge(hT_ready.sem, hT_ready.at(hidden.i))
                for r in range(PR):
                    last = nc.tensor.matmul(pt[:, 0:D], oT[:, r, :], wo[:, r, :], start=(r == 0), stop=(r == PR - 1))
                last.then_inc(out_ready.sem, 1)

            def body(turn, before, more, more2):
                if more:
                    transposes(turn.next())
                scores(turn, 0)
                if before:
                    spread_reciprocals(turn.before(), True)
                if more:
                    project(turn.next(), 0)
                    project(turn.next(), 1)
                scores(turn, 1)
                columns(turn, 0)
                if more:
                    project(turn.next(), 2)
                if before:
                    output(turn.before(), turn.next() if more else None)
                columns(turn, 1)
                weighted(turn, 0)
                if more:
                    heads_to_rows(turn.next(), turn)
                weighted(turn, 1)

            first = Turn(0, 0)
            transposes(first)
            project(first, 0)
            project(first, 1)
            project(first, 2)
            heads_to_rows(first, None)
            trailing(pe, body)
            spread_reciprocals(Turn(NT // 2 - 1, 1), False)
            output(Turn(NT // 2 - 1, 1), None)

def rotary_tables():
    f = np.float32
    half = np.arange(0, DH, 2, dtype=f)
    inv = (f(1.0) / np.power(f(10000.0), half / f(DH))).astype(f)
    t = np.arange(L, dtype=f)
    freqs = t[:, None] * inv[None, :]
    base = (half + f(0.4 * DH)) / f(1.4 * DH)
    power = (t - f(L // 2)) / f(64.0)
    scale = np.power(base[None, :], power[:, None]).astype(f)
    cos, sin = np.cos(freqs).astype(f), np.sin(freqs).astype(f)
    parts = [cos * scale * f(8), cos / scale, sin * scale * f(8), sin / scale]
    full = [np.concatenate([-a if n >= 2 else a, a], axis=1) for n, a in enumerate(parts)]
    return np.tile(np.concatenate(full, axis=1).astype(f), (B, 1))

def window_masks(bf16):
    t, j = np.arange(P)[:, None], np.arange(P)[None, :]
    own, before = np.where(j <= t, 0.0, MASKED), np.where(j >= t, 0.0, MASKED)
    none = np.full((P, P), MASKED)
    even = [np.concatenate([own, none if a % (L // P // 2) == 0 else before], axis=1) for a in range(NT // 2)]
    odd = np.concatenate([before, own], axis=1)
    return np.concatenate(even, axis=1).astype(bf16), odd.astype(bf16)

def pick_rows(bf16):
    rows = 2 * NS
    return np.concatenate([np.repeat(np.tile(np.eye(rows)[:, r:r + 1], (3, 1)), P, axis=1) for r in range(rows)],
                          axis=1).astype(bf16)

def zero_rows(nc, streams):
    with nc.sbuf_tensor("zero", [B, D], FP32) as zero, nc.semaphore("zero_made") as made, \
            nc.semaphore("zero_sent") as sent, nc.Block() as block:

        @block.gpsimd
        def _(pool):
            nc.gpsimd.memset(zero[:, :], 0.0).then_inc(made, 1)

        @block.sync
        def _(sp):
            sp.wait_ge(made, 1)
            for stream in streams:
                sp.dma_start(stream.rearrange("(b r) d -> b r d", r=LP)[:, 0, :], zero[:, :]).then_inc(sent, 16)
            sp.wait_ge(sent, 16 * len(streams))

def program(nc, a, out):
    def scratch(name, rows):
        return nc.dram_tensor(name, (rows, D), FP32).ap()

    x1, x2, xa, x3 = (scratch(n, T) for n in ("x1", "x2", "xa", "x3"))
    h3, a0, f0, a1 = (scratch(n, B * LP) for n in ("h3", "a0", "f0", "a1"))
    zero_rows(nc, (h3, a0, f0, a1))
    with nc.sbuf_tensor("ident", [P, P], FP32) as ident_sb, ExitStack() as memory:
        with nc.semaphore("ident_in") as ident_in, nc.Block() as block:
            @block.sync
            def _(sp):
                sp.dma_start(ident_sb[:, :], a["ident"]).then_inc(ident_in, 16)
                sp.wait_ge(ident_in, 16)
        ident = ident_sb[:, :]
        ssm = {k: a["L0_attn_" + v] for k, v in dict(
            w_in="W_in", w_x="W_xproj", w_dt="W_dt", w_out="W_out", conv_w="conv_w", conv_b="conv_b", b_dt="b_dt",
            skip="D", a_log="A_log").items()}
        state_space_stage(nc, "ssm", dict(ssm, pick=a["pick"]), a["L0_attn_x"], x1, ident)
        mlp = {k: a["L1_attn_" + v] for k, v in dict(w1="w1", b1="b1", w2="w2", b2="b2", gain="g2", offset="beta2").items()}
        mlp = FfnWeights(nc, memory, "mlp_w", False, mlp)
        shared = WindowConstants(nc, memory, "win_c", {k: a[k] for k in ("ident16", "mask_even", "mask_odd")})
        win = [WindowWeights(nc, memory, f"win{layer}_w",
                             dict({k: a["L1_ffn_" + k][layer] for k in ("wqkv", "wo", "q_scale", "k_scale")},
                                  tables=a["tables"]), shared, layer == 0) for layer in range(2)]
        glu = [FfnWeights(nc, memory, f"glu{layer}_w", True, {k: a["L1_ffn_" + v][layer] for k, v in dict(
            w1="w1", b1="b1", w2="w2", b2="b2", gain="ln_g", offset="ln_b").items()}) for layer in range(2)]
        with ExitStack() as lin_memory:
            lin = {k: a["L1_attn_" + v] for k, v in dict(
                wqT="wq", wkT="wk", wv="wv", wo="wo", proj="proj", gain="g1", offset="beta1").items()}
            lin = LinWeights(nc, lin_memory, "lin_w", dict(lin, causal=a["causal"], keep=a["keep"]))
            with ExitStack() as moe_memory:
                moe = MoeWeights(nc, moe_memory, "moe_w", dict(
                    router=a["L0_ffn_router_w"], router_b=a["L0_ffn_router_b"], rank=a["rank"],
                    experts=a["L0_ffn_expert_w"], expert_b=a["L0_ffn_expert_b"]))
                moe_stage(nc, "moe", moe, x1, x2, ident, lin)
            linear_attention_stage(nc, "lin", lin, x2, xa, ident, mlp)
        ffn_stage(nc, "mlp", False, mlp, xa, False, x2, x3, h3, True, ident, win[0])
        window_attention_stage(nc, "win0", win[0], h3, a0, ident, glu[0])
        ffn_stage(nc, "glu0", True, glu[0], a0, True, None, None, f0, False, ident, win[1])
        window_attention_stage(nc, "win1", win[1], f0, a1, ident, glu[1])
        ffn_stage(nc, "glu1", True, glu[1], a1, True, x3, out, None, False, ident, None)
        nc.clear_and_free_semaphores([shared.loaded])

def laid_out(inputs):
    a = {k: np.asarray(v) for k, v in inputs.items()}
    a["L0_attn_x"] = a["L0_attn_x"].reshape(T, D)
    a["L0_attn_conv_w"] = a["L0_attn_conv_w"].reshape(HID, 3)
    for k in ("L0_attn_W_in", "L0_attn_W_xproj", "L0_attn_W_dt", "L0_attn_W_out", "L0_ffn_router_w",
              "L1_attn_wq", "L1_attn_wk"):
        a[k] = a[k].T
    a["L0_ffn_expert_w"] = a["L0_ffn_expert_w"].transpose(2, 0, 1).reshape(D, E * D)
    bf16 = np.dtype("bfloat16")
    keep = np.ones((NT, P, 1), np.float32)
    keep[L // P - 1::L // P] = 0
    even, odd = window_masks(bf16)
    a.update(ident=np.eye(P, dtype=np.float32), ident16=np.eye(P).astype(bf16), pick=pick_rows(bf16),
             rank=np.arange(E, 0, -1).astype(np.float32), causal=np.triu(np.ones((P, P), np.float32)),
             keep=keep.reshape(T, 1), tables=rotary_tables(), mask_even=even, mask_odd=odd)
    return {k: np.ascontiguousarray(v) for k, v in a.items()}

def kernel(**inputs):
    import concourse.bacc as bacc
    from concourse.bass_utils import run_bass_kernel_spmd

    nc = bacc.Bacc("TRN2", target_bir_lowering=False, num_devices=1)
    arrays = {f"in_{k}": v for k, v in laid_out(inputs).items()}
    aps = {k[3:]: nc.dram_tensor(k, v.shape, mybir.dt.from_np(v.dtype), kind="ExternalInput").ap()
           for k, v in arrays.items()}
    out = nc.dram_tensor("out", (T, D), FP32, kind="ExternalOutput").ap()
    program(nc, aps, out)
    r = run_bass_kernel_spmd(nc, [arrays], core_ids=[0])
    return r.results[0]["out"].reshape(B, L, D)
```
